# Optimizing a Trainium2 kernel written in Bass

```python
import numpy as np
import jax
import jax.numpy as jnp

def _softmax(x, axis=-1):
    return jax.nn.softmax(x, axis=axis)

def _gelu(x):
    return jax.nn.gelu(x, approximate=True)

def _silu(x):
    return jax.nn.silu(x)

def _sigmoid(x):
    return jax.nn.sigmoid(x)

def _layernorm(x, axis=-1, eps=1e-05):
    m = jnp.mean(x, axis=axis, keepdims=True)
    v = jnp.var(x, axis=axis, keepdims=True)
    return (x - m) / jnp.sqrt(v + eps)

def _scatter_add(tgt, idx, src, axis=0):
    return tgt.at[idx].add(src)

def _segment_sum(src, seg, n):
    return jax.ops.segment_sum(src, seg, n)
kernel_name = 'mk_decoder_postln_d1_seqx_r4_13d3c4'

def setup_inputs(seed: int=0):
    np.random.seed(seed)
    _w = jnp.asarray

    def _rec_inputs():
        import jax
        import jax.numpy as jnp
        _rk = jax.random.key(seed)
        x = -0.0002928 + 1 * jax.random.normal(jax.random.fold_in(_rk, 1), (4, 1024, 256), jnp.float32)
        _lenS = 1024 - jax.random.randint(jax.random.fold_in(_rk, 7), (4,), 0, max(1, 1024 // 4) + 1, jnp.int32)
        _lenS2 = 154 - jax.random.randint(jax.random.fold_in(_rk, 8), (4,), 0, max(1, 154 // 4) + 1, jnp.int32)
        _ctx_1024P = jax.random.normal(jax.random.fold_in(_rk, 11), (4, 16, 256), jnp.float32)
        _ctx_1024c = jax.random.dirichlet(jax.random.fold_in(_rk, 511), 0.3 * jnp.ones((16,), jnp.float32), (4, 154))
        _ctx_1024t = jnp.einsum('bsk,bkd->bsd', _ctx_1024c, _ctx_1024P)
        _ctx_1024t = _ctx_1024t * jax.lax.rsqrt(jnp.mean(jnp.square(_ctx_1024t)) + 1e-12) * 0.953939
        ctx_1024 = 0.000227908 + 0.99994 * (_ctx_1024t + 0.3 * jax.random.normal(jax.random.fold_in(_rk, 611), (4, 154, 256), jnp.float32))
        return (x, ctx_1024)
    x, ctx_1024 = _rec_inputs()

    def _L0_attn_setup():
        import jax, jax.numpy as jnp
        import numpy as np
        D_MODEL = 256
        D_STATE = 64
        BATCH = 4
        SEQ_L = 1024
        LN_EPS = 1e-05

        def _reference_tuple_inner(u, A_log, B, C, D, delta, gamma, beta, freq_align, reward):
            b, L, d = u.shape
            A = -jnp.exp(A_log)
            k_idx = jnp.arange(L, dtype=u.dtype)
            powers = jnp.exp(k_idx[:, None] * (delta[0] * A)[None, :])
            K = jnp.einsum('ln,dn->ld', powers, C)
            fft_size = 1 << int(np.ceil(np.log2(2 * L)))
            u_fft = jnp.fft.fft(u, n=fft_size, axis=1)
            K_fft = jnp.fft.fft(K, n=fft_size, axis=0)
            y = jnp.fft.ifft(u_fft * K_fft[None], axis=1).real[:, :L, :]
            y = y + u * D
            y_fft = jnp.fft.fft(y, axis=1)
            y = jnp.fft.ifft(y_fft * freq_align + reward, axis=1).real
            mean = y.mean(-1, keepdims=True)
            var = y.var(-1, keepdims=True)
            y = (y - mean) / jnp.sqrt(var + LN_EPS) * gamma + beta
            delta_mean = delta.mean()
            A_bar_s = jnp.exp(delta_mean * A)
            A_safe = A + 1e-08 * jnp.sign(A)
            B_bar = ((A_bar_s - 1.0) / A_safe)[:, None] * B
            state = jnp.zeros((b, A.shape[0]), u.dtype)
            final_state = A_bar_s * state + jnp.einsum('nd,bd->bn', B_bar, u[:, -1, :])
            return (y, final_state)
        key = jax.random.key(seed)
        ks = jax.random.split(key, 8)
        u = jax.random.normal(ks[0], (BATCH, SEQ_L, D_MODEL), jnp.float32)
        A_log = jax.random.uniform(ks[1], (D_STATE,), jnp.float32, -2.0, -0.1)
        xav = float(np.sqrt(6.0 / (D_STATE + D_MODEL)))
        B = jax.random.uniform(ks[2], (D_STATE, D_MODEL), jnp.float32, -xav, xav) * 0.1
        C = jax.random.uniform(ks[3], (D_MODEL, D_STATE), jnp.float32, -xav, xav) * 0.1
        D = jnp.zeros((D_MODEL,), jnp.float32)
        delta = jax.random.uniform(ks[4], (D_MODEL,), jnp.float32, 0.001, 0.1)
        gamma = jnp.ones((D_MODEL,), jnp.float32)
        beta = jnp.zeros((D_MODEL,), jnp.float32)
        freq_align = jax.random.normal(ks[5], (D_MODEL,), jnp.float32)
        reward = jax.random.normal(ks[6], (D_MODEL,), jnp.float32)
        return dict(u=u, A_log=A_log, B=B, C=C, D=D, delta=delta, gamma=gamma, beta=beta, freq_align=freq_align, reward=reward)
    _L0_attn_all = _L0_attn_setup()
    _L0_attn_in = {k: v for k, v in _L0_attn_all.items() if k in ('A_log', 'B', 'C', 'D', 'delta', 'gamma', 'beta', 'freq_align', 'reward')}
    del _L0_attn_all

    def _L0_xattn_setup():
        import jax, jax.numpy as jnp
        import numpy as np
        HEADS = 16
        key = jax.random.key(seed)
        ks = jax.random.split(key, 6)
        b, n, m, dim = (2, 512, 128, 256)
        s = dim ** (-0.5)
        return {'x': jax.random.normal(ks[0], (b, n, dim), jnp.float32), 'mem': jax.random.normal(ks[1], (b, m, dim), jnp.float32), 'Wq': jax.random.normal(ks[2], (dim, dim), jnp.float32) * s, 'Wkv': jax.random.normal(ks[3], (dim, 2 * dim), jnp.float32) * s, 'Wout': jax.random.normal(ks[4], (dim, dim), jnp.float32) * s, 'bout': jnp.zeros((dim,), jnp.float32)}
    _L0_xattn_all = _L0_xattn_setup()
    _L0_xattn_in = {k: v for k, v in _L0_xattn_all.items() if k in ('Wq', 'Wkv', 'Wout', 'bout')}
    del _L0_xattn_all

    def _L0_ffn_setup():
        import jax, jax.numpy as jnp
        import numpy as np
        D_IN, D_HID = (256, 1024)

        def _ternary(key, shape):
            return jax.random.randint(key, shape, -1, 2).astype(jnp.float32)

        def _tlin(x, w, s):
            return jnp.einsum('bsi,oi->bso', x, w) * s
        key = jax.random.key(seed)
        ks = jax.random.split(key, 12)
        inv = lambda fan: 1.0 / np.sqrt(fan).astype(np.float32)
        return {'x': jax.random.normal(ks[0], (4, 512, D_IN), dtype=jnp.float32), 'w1_w': _ternary(ks[1], (D_HID, D_IN)), 'w1_s': jax.random.uniform(ks[2], (D_HID,), dtype=jnp.float32) * inv(D_IN), 'w2_w': _ternary(ks[3], (D_HID, D_IN)), 'w2_s': jax.random.uniform(ks[4], (D_HID,), dtype=jnp.float32) * inv(D_IN), 'h1_w': _ternary(ks[5], (D_HID, D_HID)), 'h1_s': jax.random.uniform(ks[6], (D_HID,), dtype=jnp.float32) * inv(D_HID), 'h2_w': _ternary(ks[7], (D_HID, D_HID)), 'h2_s': jax.random.uniform(ks[8], (D_HID,), dtype=jnp.float32) * inv(D_HID), 'w3_w': _ternary(ks[9], (D_IN, D_HID)), 'w3_s': jax.random.uniform(ks[10], (D_IN,), dtype=jnp.float32) * inv(D_HID)}
    _L0_ffn_all = _L0_ffn_setup()
    _L0_ffn_in = {k: v for k, v in _L0_ffn_all.items() if k in ('w1_w', 'w1_s', 'w2_w', 'w2_s', 'h1_w', 'h1_s', 'h2_w', 'h2_s', 'w3_w', 'w3_s')}
    del _L0_ffn_all
    return {'x': x, 'ctx_1024': ctx_1024, 'L0_attn_A_log': _L0_attn_in['A_log'], 'L0_attn_B': _L0_attn_in['B'], 'L0_attn_C': _L0_attn_in['C'], 'L0_attn_D': _L0_attn_in['D'], 'L0_attn_delta': _L0_attn_in['delta'], 'L0_attn_gamma': _L0_attn_in['gamma'], 'L0_attn_beta': _L0_attn_in['beta'], 'L0_attn_freq_align': _L0_attn_in['freq_align'], 'L0_attn_reward': _L0_attn_in['reward'], 'L0_xattn_Wq': _L0_xattn_in['Wq'], 'L0_xattn_Wkv': _L0_xattn_in['Wkv'], 'L0_xattn_Wout': _L0_xattn_in['Wout'], 'L0_xattn_bout': _L0_xattn_in['bout'], 'L0_ffn_w1_w': _L0_ffn_in['w1_w'], 'L0_ffn_w1_s': _L0_ffn_in['w1_s'], 'L0_ffn_w2_w': _L0_ffn_in['w2_w'], 'L0_ffn_w2_s': _L0_ffn_in['w2_s'], 'L0_ffn_h1_w': _L0_ffn_in['h1_w'], 'L0_ffn_h1_s': _L0_ffn_in['h1_s'], 'L0_ffn_h2_w': _L0_ffn_in['h2_w'], 'L0_ffn_h2_s': _L0_ffn_in['h2_s'], 'L0_ffn_w3_w': _L0_ffn_in['w3_w'], 'L0_ffn_w3_s': _L0_ffn_in['w3_s']}

def reference(x, ctx_1024, L0_attn_A_log, L0_attn_B, L0_attn_C, L0_attn_D, L0_attn_delta, L0_attn_gamma, L0_attn_beta, L0_attn_freq_align, L0_attn_reward, L0_xattn_Wq, L0_xattn_Wkv, L0_xattn_Wout, L0_xattn_bout, L0_ffn_w1_w, L0_ffn_w1_s, L0_ffn_w2_w, L0_ffn_w2_s, L0_ffn_h1_w, L0_ffn_h1_s, L0_ffn_h2_w, L0_ffn_h2_s, L0_ffn_w3_w, L0_ffn_w3_s):
    import jax
    import jax.numpy as jnp

    def _L0_attn_ref(u, A_log, B, C, D, delta, gamma, beta, freq_align, reward):
        import jax, jax.numpy as jnp
        import numpy as np
        D_MODEL = 256
        D_STATE = 64
        BATCH = 4
        SEQ_L = 1024
        LN_EPS = 1e-05

        def _reference_tuple_inner(u, A_log, B, C, D, delta, gamma, beta, freq_align, reward):
            b, L, d = u.shape
            A = -jnp.exp(A_log)
            k_idx = jnp.arange(L, dtype=u.dtype)
            powers = jnp.exp(k_idx[:, None] * (delta[0] * A)[None, :])
            K = jnp.einsum('ln,dn->ld', powers, C)
            fft_size = 1 << int(np.ceil(np.log2(2 * L)))
            u_fft = jnp.fft.fft(u, n=fft_size, axis=1)
            K_fft = jnp.fft.fft(K, n=fft_size, axis=0)
            y = jnp.fft.ifft(u_fft * K_fft[None], axis=1).real[:, :L, :]
            y = y + u * D
            y_fft = jnp.fft.fft(y, axis=1)
            y = jnp.fft.ifft(y_fft * freq_align + reward, axis=1).real
            mean = y.mean(-1, keepdims=True)
            var = y.var(-1, keepdims=True)
            y = (y - mean) / jnp.sqrt(var + LN_EPS) * gamma + beta
            delta_mean = delta.mean()
            A_bar_s = jnp.exp(delta_mean * A)
            A_safe = A + 1e-08 * jnp.sign(A)
            B_bar = ((A_bar_s - 1.0) / A_safe)[:, None] * B
            state = jnp.zeros((b, A.shape[0]), u.dtype)
            final_state = A_bar_s * state + jnp.einsum('nd,bd->bn', B_bar, u[:, -1, :])
            return (y, final_state)
        return _reference_tuple_inner(u, A_log, B, C, D, delta, gamma, beta, freq_align, reward)[0]

    def _L0_xattn_ref(x, mem, Wq, Wkv, Wout, bout):
        import jax, jax.numpy as jnp
        import numpy as np
        HEADS = 16
        b, n, dim = x.shape
        h = HEADS
        d = dim // h
        scale = d ** (-0.5)
        mem_len = mem.shape[1]
        q = x @ Wq
        xc = jnp.concatenate((mem, x), axis=1)
        kv = xc @ Wkv
        k, v = jnp.split(kv, 2, axis=-1)

        def to_heads(t):
            bb, nn, _ = t.shape
            return t.reshape(bb, nn, h, d).transpose(0, 2, 1, 3)
        q, k, v = (to_heads(q), to_heads(k), to_heads(v))
        dots = jnp.einsum('bhid,bhjd->bhij', q, k) * scale
        j = dots.shape[-1]
        i_idx = jnp.arange(n)[:, None]
        j_idx = jnp.arange(j)[None, :]
        mask = j_idx > i_idx + mem_len
        dots = jnp.where(mask[None, None], -jnp.inf, dots)
        attn = jax.nn.softmax(dots, axis=-1)
        out = jnp.einsum('bhij,bhjd->bhid', attn, v)
        out = out.transpose(0, 2, 1, 3).reshape(b, n, dim)
        return out @ Wout + bout

    def _L0_ffn_ref(x, w1_w, w1_s, w2_w, w2_s, h1_w, h1_s, h2_w, h2_s, w3_w, w3_s):
        import jax, jax.numpy as jnp
        import numpy as np
        D_IN, D_HID = (256, 1024)

        def _ternary(key, shape):
            return jax.random.randint(key, shape, -1, 2).astype(jnp.float32)

        def _tlin(x, w, s):
            return jnp.einsum('bsi,oi->bso', x, w) * s
        h = jax.nn.silu(_tlin(x, w1_w, w1_s)) * _tlin(x, w2_w, w2_s)
        h = jax.nn.gelu(_tlin(h, h1_w, h1_s), approximate=False)
        h = jax.nn.gelu(_tlin(h, h2_w, h2_s), approximate=False)
        return _tlin(h, w3_w, w3_s)
    x = _layernorm(x + _L0_attn_ref(x, L0_attn_A_log, L0_attn_B, L0_attn_C, L0_attn_D, L0_attn_delta, L0_attn_gamma, L0_attn_beta, L0_attn_freq_align, L0_attn_reward), axis=-1)
    x = _layernorm(x + _L0_xattn_ref(x, ctx_1024, L0_xattn_Wq, L0_xattn_Wkv, L0_xattn_Wout, L0_xattn_bout), axis=-1)
    x = _layernorm(x + _L0_ffn_ref(x, L0_ffn_w1_w, L0_ffn_w1_s, L0_ffn_w2_w, L0_ffn_w2_s, L0_ffn_h1_w, L0_ffn_h1_s, L0_ffn_h2_w, L0_ffn_h2_s, L0_ffn_w3_w, L0_ffn_w3_s), axis=-1)
    return x

_drawn_inputs = setup_inputs


def setup_inputs(seed=0):
    import zlib

    import numpy as np

    out = dict(_drawn_inputs(seed))
    spreads = {'L0_attn_D': (0.0, 0.1),
     'L0_attn_gamma': (1.0, 0.2),
     'L0_attn_beta': (0.0, 0.1),
     'L0_xattn_bout': (0.0, 0.1)}
    factors = {'L0_attn_delta': 8.0,
     'L0_attn_reward': 2.748,
     'L0_ffn_w1_w': 8.0,
     'L0_ffn_w1_s': 8.0,
     'L0_ffn_w2_w': 8.0,
     'L0_ffn_w2_s': 8.0,
     'L0_ffn_h1_w': 8.0,
     'L0_ffn_h1_s': 8.0,
     'L0_ffn_h2_w': 8.0,
     'L0_ffn_h2_s': 8.0,
     'L0_ffn_w3_w': 8.0,
     'L0_ffn_w3_s': 8.0}
    for name, (base, spread) in spreads.items():
        noise = np.random.default_rng([zlib.crc32(name.encode()), seed]).standard_normal(out[name].shape)
        drawn = base * np.exp(spread * noise) if base else spread * noise
        out[name] = jnp.asarray(drawn.astype(out[name].dtype))
    for name, factor in factors.items():
        out[name] = (out[name] * factor).astype(out[name].dtype)
    return out
```

```python
import numpy as np
from contextlib import ExitStack

import concourse.bass as bass
from concourse import mybir

ALU = mybir.AluOpType
ACT = mybir.ActivationFunctionType
AX_X = mybir.AxisListType.X
F32 = mybir.dt.float32
F32R = mybir.dt.float32r
BF16 = mybir.dt.bfloat16

P = 128
B, L, D = 4, 1024, 256
NT = B * L // P
CH = L // P
NS = 64
M = 154
H, DH = 16, 16
HG = 4
NG = H // HG
IT = B * NG
KEYS = L + M
KP = 1184
KT = 10
F = 1024
EPS = 1e-5
NEG = -1.0e30
LOWEST = -3.0e38


class Mem:
    pass


def tensors(nc, stack):
    def sb(name, shape, dtype=F32):
        return stack.enter_context(nc.sbuf_tensor(name, shape, dtype))

    def sem(name):
        return stack.enter_context(nc.semaphore(name))
    return sb, sem


def phase_convolution(nc, m, a):
    GR = 16
    NGR = D // GR
    RING = 4
    with ExitStack() as st:
        sb, sem = tensors(nc, st)
        U = sb("x_reversed", [P, NT, D])
        Y = sb("conv_out", [P, NT, D])
        TZ = sb("toeplitz", [P, RING, GR, P])
        HS = sb("states", [NS, 2, B, D])
        CHs = sb("states_times_c", [NS, CH - 1, B, D])
        kpad = sb("k_padded", [P, 2, 256])
        alog_col = sb("alog_col", [NS, 1])
        alog_row = sb("alog_row", [P, NS])
        delta0 = sb("delta0", [P, 1])
        ct = sb("c_transposed", [NS, D])
        fa_row = sb("freq_align_row", [NS, D])
        fa_col = sb("freq_align_col", [P, 2])
        d_col = sb("d_col", [P, 2])
        rew = sb("reward", [1, D])
        gam = sb("gamma", [P, D])
        bet = sb("beta", [P, D])
        e_col = sb("exp_alog_col", [NS, 1])
        z_col = sb("z_col", [NS, 1])
        e_row = sb("exp_alog_row", [P, NS])
        z_row = sb("z_row", [P, NS])
        l_row = sb("l_row", [NS, P + 1])
        p1_col = sb("p_plus_1", [P, 1])
        pw = sb("powers", [NS, P + 1])
        prev = sb("powers_to_chunk_end", [P, NS])
        cta = sb("c_times_fa", [NS, D])
        dfa = sb("d_times_fa", [P, 2])
        stats = sb("ln_stats", [P, NT, 6])
        mv = sb("ln_mean_var", [P, NT, 2])
        sd = sb("ln_sd", [P, NT])
        rs = sb("ln_rs", [P, NT])

        par = sem("params_loaded")
        u_ld = sem("x_reversed_loaded")
        x_ld = sem("x_loaded")
        io = sem("iota_ready")
        a_dn = sem("act_done")
        v_dn = sem("dve_done")
        k_mm = sem("k_matmul_done")
        k_rd = sem("k_padded_ready")
        k_wr = sem("k_written")
        t_ld = [sem(f"toeplitz_loaded_{i}") for i in range(RING)]
        t_us = sem("toeplitz_group_done")
        g_mm = sem("chunk_sum_matmul_done")
        g_rd = sem("state_updated")
        c_rd = sem("states_times_c_ready")
        y_mm = sem("carry_matmul_done")
        y_cp = sem("carry_copied")
        t_ev = sem("toeplitz_bank_read")
        ln_v = sem("ln_variance_ready")
        ln_s = sem("ln_sd_ready")
        n_rd = sem("normalised_ready")
        n_gb = sem("residual_ready")
        pool = sem("pool_step")
        x1_rd = sem("x1_ready")
        st_rd = sem("bn_stats_ready")
        rs_rd = sem("ln_rs_ready")
        blk = st.enter_context(nc.Block())
        Yv = Y[:, :, :].rearrange("p (b c) d -> p b c d", b=B)
        Uv = U[:, :, :].rearrange("p (b c) d -> p b c d", b=B)
        PARAMS = 11

        def layer_norm_tiles(v, r):
            for h in range(2):
                for t in range(16 * h, 16 * h + 16):
                    if r == 1:
                        v.wait_ge(n_gb, t // 8 + 1)
                    v.bn_stats(stats[:, t, :], Y[:, t, :]).then_inc(st_rd, 1)
                for t in range(16 * h, 16 * h + 16):
                    v.wait_ge(st_rd, NT * r + t + 1)
                    v.bn_aggr(mv[:, t, :], stats[:, t, :]).then_inc(ln_v, 1)
            for h in range(2):
                v.wait_ge(ln_s, 2 * r + h + 1)
                sl = slice(16 * h, 16 * h + 16)
                v.reciprocal(rs[:, sl], sd[:, sl]).then_inc(rs_rd, 1)
                v.wait_ge(rs_rd, 2 * r + h + 1)
                for t in range(16 * h, 16 * h + 16):
                    out = Y[:, t, :] if r == 0 else m.x1[:, t, :]
                    v.tensor_scalar(out, Y[:, t, :], mv[:, t, 0:1], rs[:, t:t + 1], ALU.subtract,
                                    ALU.mult).then_inc(n_rd if r == 0 else x1_rd, 1)

        @blk.sync
        def _(sp):
            sp.dma_start(alog_col[:, :], a["A_log"].rearrange("(n a) -> n a", a=1)).then_inc(par, 16)
            sp.dma_start(alog_row[:, :], a["A_log"].partition_broadcast(P)).then_inc(par, 16)
            sp.dma_start(delta0[:, :], a["delta"][0:1].partition_broadcast(P)).then_inc(par, 16)
            sp.dma_start(ct[:, :], a["C_T"]).then_inc(par, 16)
            sp.dma_start(fa_row[:, :], a["freq_align"].partition_broadcast(NS)).then_inc(par, 16)
            sp.dma_start(fa_col[:, :], a["fa_cols"]).then_inc(par, 16)
            sp.dma_start(d_col[:, :], a["d_cols"]).then_inc(par, 16)
            sp.dma_start(rew[:, :], a["reward"].partition_broadcast(1)).then_inc(par, 16)
            sp.dma_start(gam[:, :], a["gamma"].partition_broadcast(P)).then_inc(par, 16)
            sp.dma_start(bet[:, :], a["beta"].partition_broadcast(P)).then_inc(par, 16)
            sp.dma_start(m.bout[:, :], a["bout"].partition_broadcast(P)).then_inc(par, 16)
            sp.dma_start(U[:, :, :], a["x_rev"].rearrange("(t p) d -> p t d", p=P)).then_inc(u_ld, 16)
            sp.wait_ge(k_rd, 1)
            sp.dma_start(m.kpad_dram.rearrange("(m p) l -> p m l", p=P), kpad[:, :, :]).then_inc(k_wr, 16)
            sp.wait_ge(k_wr, 16)
            for g in range(NGR):
                if g >= RING:
                    sp.wait_ge(t_us, g - RING + 1)
                src = bass.AP(m.kpad_dram.tensor, g * GR * 256, [[1, P], [256, GR], [1, P]])
                sp.dma_start(TZ[:, g % RING, :, :], src).then_inc(t_ld[g % RING], 16)
            sp.dma_start(m.x1[:, :, :], a["x"].rearrange("(t p) d -> p t d", p=P)).then_inc(x_ld, 16)

        @blk.gpsimd
        def _(gp):
            gp.iota(l_row[:, :], [[1, P + 1]], base=0, channel_multiplier=0,
                    allow_small_or_imprecise_dtypes=True).then_inc(io, 1)
            gp.iota(p1_col[:, :], [[0, 1]], base=1, channel_multiplier=1,
                    allow_small_or_imprecise_dtypes=True).then_inc(io, 1)
            gp.memset(kpad[:, :, :], 0.0).then_inc(io, 1)
            gp.memset(Yv[:, :, 0, :], 0.0).then_inc(io, 1)
            gp.memset(m.ident[:, :], 0.0).then_inc(pool, 1)
            gp.memset(m.ident_bf[:, :], 0.0).then_inc(pool, 1)
            gp.memset(m.mask_bf[:, :], 0.0).then_inc(pool, 1)
            gp.memset(m.eps[:, :], EPS).then_inc(pool, 1)
            gp.wait_ge(pool, 4)
            gp.affine_select(out=m.ident[:, :], in_=m.ident[:, :], compare_op=ALU.not_equal, fill=1.0,
                             base=0, pattern=[[-1, P]], channel_multiplier=1).then_inc(pool, 1)
            gp.affine_select(out=m.ident_bf[:, :], in_=m.ident_bf[:, :], compare_op=ALU.not_equal, fill=1.0,
                             base=0, pattern=[[-1, P]], channel_multiplier=1).then_inc(pool, 1)
            gp.affine_select(out=m.mask_bf[:, :], in_=m.mask_bf[:, :], compare_op=ALU.is_ge, fill=NEG,
                             base=0, pattern=[[-1, P]], channel_multiplier=1).then_inc(pool, 1)
            gp.wait_ge(par, 16 * PARAMS)
            gp.wait_ge(x_ld, 16)
            steps = 7
            for q in range(4):
                t0 = 8 * q
                v = Y[:, t0:t0 + 8, :]
                gp.wait_ge(n_rd, 8 * (q + 1))
                gp.tensor_tensor(v, v, gam[:, :].unsqueeze(1).to_broadcast([P, 8, D]), ALU.mult).then_inc(pool, 1)
                gp.wait_ge(pool, steps + 1)
                gp.tensor_tensor(v, v, bet[:, :].unsqueeze(1).to_broadcast([P, 8, D]), ALU.add).then_inc(pool, 1)
                gp.wait_ge(pool, steps + 2)
                steps += 2
                gp.tensor_tensor(v, v, m.x1[:, t0:t0 + 8, :], ALU.add).then_inc(n_gb, 1)

        @blk.scalar
        def _(act):
            act.wait_ge(par, 16 * PARAMS)
            act.activation(e_col[:, :], alog_col[:, :], ACT.Exp).then_inc(a_dn, 1)
            act.activation(e_row[:, :], alog_row[:, :], ACT.Exp).then_inc(a_dn, 1)
            act.wait_ge(io, 2)
            act.wait_ge(v_dn, 2)
            act.activation(pw[:, :], l_row[:, :], ACT.Exp, scale=z_col[:, 0:1]).then_inc(a_dn, 1)
            act.activation(prev[:, :], z_row[:, :], ACT.Exp, scale=p1_col[:, 0:1]).then_inc(a_dn, 1)
            for i in range(2 * (CH - 1)):
                c, half = i // 2, i % 2
                act.wait_ge(y_mm, i + 1)
                act.activation(Yv[:, 2 * half:2 * half + 2, c + 1, :],
                               m.ps[:, 2 + i % 2, :].rearrange("p (b d) -> p b d", b=2), ACT.Copy).then_inc(y_cp, 1)
            act.wait_ge(pool, 4)
            for r in range(2):
                for h in range(2):
                    act.wait_ge(ln_v, 16 * (2 * r + h + 1))
                    sl = slice(16 * h, 16 * h + 16)
                    act.activation(sd[:, sl], mv[:, sl, 1], ACT.Sqrt, bias=m.eps[:, 0:1]).then_inc(ln_s, 1)

        @blk.vector
        def _(v):
            v.wait_ge(par, 16 * PARAMS)
            v.wait_ge(a_dn, 2)
            v.tensor_scalar(z_col[:, :], e_col[:, :], delta0[0:NS, 0:1], -1.0, ALU.mult, ALU.mult).then_inc(v_dn, 1)
            v.tensor_scalar(z_row[:, :], e_row[:, :], delta0[:, 0:1], -1.0, ALU.mult, ALU.mult).then_inc(v_dn, 1)
            v.tensor_tensor(cta[:, :], ct[:, :], fa_row[:, :], ALU.mult).then_inc(v_dn, 1)
            v.tensor_tensor(dfa[:, :], d_col[:, :], fa_col[:, :], ALU.mult).then_inc(v_dn, 1)
            v.wait_ge(k_mm, 1)
            v.wait_ge(io, 3)
            v.tensor_copy(kpad[:, :, P - 1:2 * P - 1],
                          m.ps[:, 0, 0:256].rearrange("p (m l) -> p m l", m=2)).then_inc(v_dn, 1)
            v.wait_ge(v_dn, 5)
            v.tensor_tensor(kpad[:, :, P - 1], kpad[:, :, P - 1], dfa[:, :], ALU.add).then_inc(k_rd, 1)
            for i in range(2 * (CH - 1)):
                c, half = i // 2, i % 2
                bs = slice(2 * half, 2 * half + 2)
                v.wait_ge(g_mm, i + 1)
                g = m.ps[0:NS, i % 2, :].rearrange("p (b d) -> p b d", b=2)
                if c == 0:
                    v.tensor_copy(HS[:, c % 2, bs, :], g).then_inc(g_rd, 1)
                else:
                    v.wait_ge(g_rd, i - 1)
                    v.scalar_tensor_tensor(HS[:, c % 2, bs, :].rearrange("p b d -> p (b d)"),
                                           HS[:, (c - 1) % 2, bs, :].rearrange("p b d -> p (b d)"), pw[:, P:P + 1],
                                           m.ps[0:NS, i % 2, :], ALU.mult, ALU.add).then_inc(g_rd, 1)
                v.wait_ge(g_rd, i + 1)
                v.tensor_tensor(CHs[:, c, bs, :], HS[:, c % 2, bs, :],
                                cta[:, :].unsqueeze(1).to_broadcast([NS, 2, D]), ALU.mult).then_inc(c_rd, 1)
            v.wait_ge(y_cp, 2 * (CH - 1))
            v.wait_ge(io, 4)
            for g in range(NGR):
                v.wait_ge(t_us, g + 1)
                yd = Y[:, :, GR * g:GR * g + GR].rearrange("p t d -> p d t")
                v.tensor_tensor(yd, m.ps[:, 4 + g % 4, :].rearrange("p (d t) -> p d t", d=GR), yd,
                                ALU.add).then_inc(t_ev, 1)
            v.wait_ge(t_ev, NGR)
            v.tensor_tensor(Yv[0:1, :, 0, :], Yv[0:1, :, 0, :],
                            rew[0:1, :].unsqueeze(1).to_broadcast([1, B, D]), ALU.add).then_inc(v_dn, 1)
            v.wait_ge(v_dn, 6)
            layer_norm_tiles(v, 0)
            layer_norm_tiles(v, 1)

        @blk.tensor
        def _(pe):
            pe.wait_ge(a_dn, 4)
            pe.wait_ge(v_dn, 3)
            for mt in range(2):
                mm = nc.tensor.matmul(m.ps[:, 0, P * mt:P * mt + P], cta[:, P * mt:P * mt + P], pw[:, 0:P],
                                      start=True, stop=True)
            mm.then_inc(k_mm, 1)
            pe.wait_ge(u_ld, 16)
            pe.wait_ge(k_rd, 1)

            def carry(i):
                c, half = i // 2, i % 2
                pe.wait_ge(c_rd, i + 1)
                if i >= 2:
                    pe.wait_ge(y_cp, i - 1)
                nc.tensor.matmul(m.ps[:, 2 + i % 2, :], pw[:, 0:P],
                                 CHs[:, c, 2 * half:2 * half + 2, :].rearrange("p b d -> p (b d)"),
                                 start=True, stop=True).then_inc(y_mm, 1)
            for i in range(2 * (CH - 1)):
                c, half = i // 2, i % 2
                if i >= 2:
                    pe.wait_ge(g_rd, i - 1)
                nc.tensor.matmul(m.ps[0:NS, i % 2, :], prev[:, :], Uv[:, 2 * half:2 * half + 2, c, :],
                                 start=True, stop=True).then_inc(g_mm, 1)
                if i >= 2:
                    carry(i - 2)
            carry(2 * CH - 4)
            carry(2 * CH - 3)
            for g in range(NGR):
                pe.wait_ge(t_ld[g % RING], 16 * (g // RING + 1))
                if g >= 4:
                    pe.wait_ge(t_ev, g - 3)
                for j in range(GR):
                    mm = nc.tensor.matmul(m.ps[:, 4 + g % 4, NT * j:NT * j + NT], TZ[:, g % RING, j, :],
                                          U[:, :, GR * g + j], start=True, stop=True)
                mm.then_inc(t_us, 1)


def phase_transpose(nc, m):
    with ExitStack() as st:
        sb, sem = tensors(nc, st)
        tr = sem("transposes_done")
        tr_h = sem("high_part_ready")
        tr_l = sem("low_part_ready")
        blk = st.enter_context(nc.Block())

        @blk.tensor
        def _(pe):
            for i in range(16):
                kt, tg = i % 2, i // 2
                if i >= 4:
                    pe.wait_ge(tr_l, i - 3)
                for j in range(4):
                    mm = nc.tensor.transpose(m.ps[:, i % 4, P * j:P * j + P],
                                             m.x1[:, 4 * tg + j, P * kt:P * kt + P], m.ident[:, :])
                mm.then_inc(tr, 1)

        @blk.scalar
        def _(act):
            for i in range(16):
                act.wait_ge(tr, i + 1)
                kt, tg = i % 2, i // 2
                act.activation(m.x1h[:, kt, 512 * tg:512 * tg + 512], m.ps[:, i % 4, :], ACT.Copy).then_inc(tr_h, 1)

        @blk.vector
        def _(v):
            for i in range(16):
                kt, tg = i % 2, i // 2
                v.wait_ge(tr_h, i + 1)
                v.tensor_tensor(m.x1l[:, kt, 512 * tg:512 * tg + 512], m.ps[:, i % 4, :],
                                m.x1h[:, kt, 512 * tg:512 * tg + 512].bitcast(F32), ALU.subtract).then_inc(tr_l, 1)


def split_plan():
    plan = [("q", mt, 512 * tb, 512) for mt in range(2) for tb in range(8)]
    plan += [("k", mt, 512 * tb, 512) for mt in range(2) for tb in range(8)]
    plan += [("c", mt, 2 * M * hb, 2 * M) for mt in range(2) for hb in range(2)]
    return plan


def phase_projections(nc, m, a):
    SLOTS = 4
    with ExitStack() as st:
        sb, sem = tensors(nc, st)
        w = sb("qkv_weights", [P, 2, 3 * D])
        wh = sb("qkv_high", [P, 2, 3 * D], F32R)
        wl = sb("qkv_low", [P, 2, 3 * D], F32R)
        c = sb("context_t", [P, 2, B * M])
        ch = sb("context_high", [P, 2, B * M], F32R)
        cl = sb("context_low", [P, 2, B * M], F32R)
        parts = sb("parts", [P, SLOTS, 3, 512], BF16)
        rest = sb("rest", [P, SLOTS, 512])
        vt = sb("v_tiles", [P, SLOTS, H, 32])
        ld = sem("weights_loaded")
        wsp = sem("weights_split")
        ones = sem("ones_ready")
        qk_mm = sem("qk_matmul_done")
        p1 = sem("part1_ready")
        r1 = sem("rest_ready")
        p2 = sem("part2_ready")
        p3 = sem("part3_ready")
        wr = [sem(f"parts_written_{i}") for i in range(SLOTS)]
        v_mm = sem("v_matmul_done")
        v_cp = sem("v_copied")
        v_wr = [sem(f"v_written_{i}") for i in range(SLOTS)]
        plan = split_plan()
        v_plan = [(b, t, P) for b in range(B) for t in range(CH)] + \
                 [(b, t, n) for b in range(B) for t, n in ((CH, P), (CH + 1, M - P))]
        done = [0] * SLOTS
        before = []
        for n, (kind, mt, c0, cols) in enumerate(plan):
            before.append(done[n % SLOTS])
            done[n % SLOTS] += 16 * (4 if kind == "c" else 2)
        blk = st.enter_context(nc.Block())

        @blk.sync
        def _(sp):
            sp.dma_start(w[:, :, 0:D], a["Wq"].rearrange("(k p) n -> p k n", p=P)).then_inc(ld, 16)
            sp.dma_start(w[:, :, D:3 * D], a["Wkv"].rearrange("(k p) n -> p k n", p=P)).then_inc(ld, 16)
            sp.dma_start(c[:, :, :], a["ctx_T"].rearrange("(k p) n -> p k n", p=P)).then_inc(ld, 16)
            for n, (kind, mt, c0, cols) in enumerate(plan):
                s = n % SLOTS
                sp.wait_ge(p3, n + 1)
                for hg in range(2):
                    rows = parts[64 * hg:64 * hg + 64, s, :, :]
                    dram = m.q_dram if kind == "q" else m.k_dram
                    if kind == "c":
                        for j in range(2):
                            b = c0 // M + j
                            sp.dma_start(dram[NG * b + 2 * mt + hg, :, :, L:KEYS],
                                         rows[:, :, M * j:M * j + M]).then_inc(wr[s], 16)
                    else:
                        b, l0 = c0 // L, c0 % L
                        sp.dma_start(dram[NG * b + 2 * mt + hg, :, :, l0:l0 + 512], rows).then_inc(wr[s], 16)
            for s in range(SLOTS):
                sp.wait_ge(wr[s], done[s])

        @blk.gpsimd
        def _(gp):
            gp.memset(vt[:, :, :, DH:32], 1.0).then_inc(ones, 1)
            for n, (kind, mt, c0, cols) in enumerate(plan):
                s = n % SLOTS
                gp.wait_ge(r1, n + 1)
                if before[n]:
                    gp.wait_ge(wr[s], before[n])
                gp.tensor_copy(parts[:, s, 1, 0:cols], rest[:, s, 0:cols]).then_inc(p2, 1)
                gp.wait_ge(p2, n + 1)
                gp.tensor_tensor(parts[:, s, 2, 0:cols], rest[:, s, 0:cols], parts[:, s, 1, 0:cols],
                                 ALU.subtract).then_inc(p3, 1)

        @blk.scalar
        def _(act):
            for n, (kind, mt, c0, cols) in enumerate(plan):
                s = n % SLOTS
                act.wait_ge(qk_mm, n + 1)
                if before[n]:
                    act.wait_ge(wr[s], before[n])
                act.activation(parts[:, s, 0, 0:cols], m.ps[:, s, 0:cols], ACT.Copy,
                               scale=DH ** -0.5 if kind == "q" else 1.0).then_inc(p1, 1)
            act.wait_ge(ones, 1)
            for n, (b, t, rows) in enumerate(v_plan):
                s = n % SLOTS
                act.wait_ge(v_mm, n + 1)
                if n >= SLOTS:
                    act.wait_ge(v_wr[s], 16 * (n // SLOTS))
                act.activation(vt[0:rows, s, :, 0:DH],
                               m.ps[0:rows, 4 + s, 0:D].rearrange("p (h d) -> p h d", h=H),
                               ACT.Copy).then_inc(v_cp, 1)
                act.wait_ge(v_cp, n + 1)
                act.dma_start(m.v_dram[NG * b:NG * b + NG, P * t:P * t + rows, :].rearrange("g p c -> p g c"),
                              vt[0:rows, s, :, :].rearrange("p (g h) c -> p g (h c)", g=NG)).then_inc(v_wr[s], 16)
            for s in range(SLOTS):
                act.wait_ge(v_wr[s], 16 * (len(v_plan) // SLOTS))

        @blk.vector
        def _(v):
            v.wait_ge(ld, 48)
            v.tensor_copy(wh[:, :, :], w[:, :, :]).then_inc(wsp, 1)
            v.tensor_copy(ch[:, :, :], c[:, :, :]).then_inc(wsp, 1)
            v.wait_ge(wsp, 2)
            v.tensor_tensor(wl[:, :, :], w[:, :, :], wh[:, :, :].bitcast(F32), ALU.subtract).then_inc(wsp, 1)
            v.tensor_tensor(cl[:, :, :], c[:, :, :], ch[:, :, :].bitcast(F32), ALU.subtract).then_inc(wsp, 1)
            for n, (kind, mt, c0, cols) in enumerate(plan):
                s = n % SLOTS
                v.wait_ge(p1, n + 1)
                if n >= SLOTS:
                    v.wait_ge(p3, n - SLOTS + 1)
                v.scalar_tensor_tensor(rest[:, s, 0:cols], m.ps[:, s, 0:cols], DH ** -0.5 if kind == "q" else 1.0,
                                       parts[:, s, 0, 0:cols], ALU.mult, ALU.subtract).then_inc(r1, 1)

        @blk.tensor
        def _(pe):
            pe.wait_ge(wsp, 4)
            for n, (kind, mt, c0, cols) in enumerate(plan):
                if n >= 4:
                    pe.wait_ge(r1, n - 3)
                w0 = (0 if kind == "q" else D) + P * mt
                xh, xl = (ch, cl) if kind == "c" else (m.x1h, m.x1l)
                for i, (kt, wt, xt) in enumerate((kt, wt, xt) for kt in range(2)
                                                 for wt, xt in ((wh, xl), (wl, xh), (wh, xh))):
                    mm = nc.tensor.matmul(m.ps[:, n % 4, 0:cols], wt[:, kt, w0:w0 + P], xt[:, kt, c0:c0 + cols],
                                          start=(i == 0), stop=(i == 5))
                mm.then_inc(qk_mm, 1)
            for n, (b, t, rows) in enumerate(v_plan):
                if n >= 4:
                    pe.wait_ge(v_cp, n - 3)
                if t < CH:
                    xh, xl, c0 = m.x1h, m.x1l, L * b + P * t
                else:
                    xh, xl, c0 = ch, cl, M * b + P * (t - CH)
                for i, (kt, wt, xt) in enumerate((kt, wt, xt) for kt in range(2)
                                                 for wt, xt in ((wh, xl), (wl, xh), (wh, xh))):
                    mm = nc.tensor.matmul(m.ps[0:rows, 4 + n % 4, 0:D], xt[:, kt, c0:c0 + rows],
                                          wt[:, kt, 2 * D:3 * D], start=(i == 0), stop=(i == 5))
                mm.then_inc(v_mm, 1)


def score_plan():
    steps = []
    for c in range(2):
        for kt in range(4 * (c + 1)):
            steps.append((c, kt, P, max(0, P * kt - 512 * c)))
        steps += [(c, CH, P, 0), (c, CH + 1, M - P, 0)]
    return steps


def max_plan():
    units = []
    for h in range(HG):
        for i in range(CH):
            xk = P * (i + 1)
            cut = [(0, min(xk, 512), xk <= 512)] + ([(512, xk - 512, True)] if xk > 512 else [])
            chunks = [[(0, k0, kn, dg)] for k0, kn, dg in cut]
            if chunks[-1][0][2] + M <= 512:
                chunks[-1].append((chunks[-1][0][2], L, M, False))
            else:
                chunks.append([(0, L, M, False)])
            units += [(h, i, c, pc) for c, pc in enumerate(chunks)]
    return units


TERMS = ((0, 0), (0, 1), (1, 0), (0, 2), (2, 0), (1, 1))
TR = 16 * len(TERMS)
MR = TR + 3


def phase_attention(nc, m, a):
    S = 3
    with ExitStack() as st:
        sb, sem = tensors(nc, st)
        Q = [sb(f"q_rows_{s}", [MR, HG, L], BF16) for s in range(S)]
        K = [sb(f"k_rows_{s}", [MR, HG, KP], BF16) for s in range(S)]
        V = [sb(f"v_rows_{s}", [P, KT, HG * 32]) for s in range(S)]
        PR = sb("probabilities", [P, 4, 2, 512])
        OT = sb("out_transposed", [P, 2, 512])
        O = sb("out_heads", [P, 2, 4, HG, DH])
        rc = sb("denominator_inverse", [P, 4, HG])
        mxp = sb("max_partial", [P, HG * CH, 3])
        negm = sb("minus_max", [P, HG * CH])
        rst = sb("minus_max_rest", [P, HG * CH])
        M3 = sb("minus_max_parts", [P, 3, HG * CH], BF16)
        MT = sb("minus_max_rows", [3 * HG * CH, P], BF16)

        ini = sem("constants_ready")
        ld = [sem(f"step_loaded_{s}") for s in range(S)]
        mr = [sem(f"max_rows_loaded_{s}") for s in range(S)]
        nat = sem("max_scores_done")
        red = sem("max_bank_read")
        mx = sem("max_chain")
        t_mm = sem("small_transpose_done")
        mt_rd = sem("max_rows_ready")
        mw = sem("max_rows_written")
        s_mm = sem("score_pair_done")
        e_dn = sem("exp_pair_done")
        k_dn = sem("pair_masked")
        p_dn = sem("pv_step_done")
        o_cp = sem("pv_bank_read")
        r_dn = sem("inverse_ready")
        o_rd = sem("out_ready")
        turn = sem("waits_carried")
        o_wr = [sem(f"out_written_{c}") for c in range(2)]

        steps = score_plan()
        units = max_plan()
        NU, NSP = len(units), len(steps)
        NSC = 2 * NSP
        MAXED = 14
        LOADS = 16 * 14
        diag = [si for si, (c, kt, rows, off) in enumerate(steps) if kt < CH and kt >= 4 * c]

        def unit_range(si):
            return range(NU * si // MAXED, NU * (si + 1) // MAXED) if si < MAXED else range(0)

        blk = st.enter_context(nc.Block())

        def loop(eng, body):
            with eng.Fori(0, (IT - 1) // S) as i:
                for s in range(S):
                    body(i * S + s, s, i, True)
            body(IT - 1, (IT - 1) % S, (IT - 1) // S, False)

        @blk.sync
        def _(sp):
            def load(n, s):
                for t, (pq, pk) in enumerate(TERMS):
                    sp.dma_start(Q[s][DH * t:DH * t + DH, :, :],
                                 m.q_dram[n, :, pq, :].rearrange("(h r) l -> r h l", r=DH)).then_inc(ld[s], 16)
                    sp.dma_start(K[s][DH * t:DH * t + DH, :, 0:KEYS],
                                 m.k_dram[n, :, pk, 0:KEYS].rearrange("(h r) l -> r h l", r=DH)).then_inc(ld[s], 16)
                sp.dma_start(V[s][:, 0:KT - 1, :],
                             m.v_dram[n, 0:P * (KT - 1), :].rearrange("(t p) c -> p t c", p=P)).then_inc(ld[s], 16)
                sp.dma_start(V[s][0:M - P, KT - 1, :],
                             m.v_dram[n, P * (KT - 1):P * (KT - 1) + M - P, :]).then_inc(ld[s], 16)

            def max_rows(n, s):
                sp.wait_ge(mt_rd, n + 1)
                sp.dma_start(m.max_dram[:, :], MT[:, :]).then_inc(mw, 16)
                sp.wait_ge(mw, n * 16 + 16)
                sp.dma_start(Q[s][TR:MR, :, :].rearrange("o h l -> o (h l)"),
                             m.max_dram.rearrange("(o k) p -> o (k p)", o=3)).then_inc(mr[s], 16)

            def step(n, s, i, more, load_more):
                if load_more:
                    sp.wait_ge(p_dn, n * NSP + 2)
                    load(n + 2, (s + 2) % S)
                for c in range(2):
                    sp.wait_ge(o_rd, 2 * n + c + 2)
                    sp.dma_start(m.o_dram[n, c, :, :, :],
                                 O[:, c, :, :, :].rearrange("p q h d -> p q (h d)")).then_inc(o_wr[c], 16)
                    if c == 0 and more:
                        max_rows(n + 1, (s + 1) % S)

            for c in range(2):
                sp.sem_inc(o_wr[c], 16)
            load(0, 0)
            load(1, 1)
            max_rows(0, 0)
            with sp.Fori(0, 4) as i:
                for s in range(S):
                    step(i * S + s, s, i, True, True)
            for n in range(12, IT):
                step(n, n % S, n // S, n < IT - 1, n < IT - 2)
            for c in range(2):
                sp.wait_ge(o_wr[c], 16 * IT + 16)

        @blk.gpsimd
        def _(gp):
            gp.memset(mxp[:, :, :], LOWEST).then_inc(ini, 1)

            def body(n, s, i, more):
                for d, si in enumerate(diag):
                    c, kt, rows, off = steps[si]
                    for pr in range(2):
                        u = 2 * si + pr
                        gp.wait_ge(e_dn, n * NSC + u + 3)
                        gp.sem_inc(turn, 1)
                        blk_ = PR[:, u % 4, :, off:off + P]
                        gp.affine_select(out=blk_, in_=blk_, compare_op=ALU.is_ge, fill=0.0, base=0,
                                         pattern=[[0, 2], [1, P]], channel_multiplier=-1).then_inc(k_dn, 1)
            loop(gp, body)

        @blk.scalar
        def _(act):
            act.sem_inc(e_dn, 2)
            act.sem_inc(o_cp, 1)

            def body(n, s, i, more):
                def out_copy(c):
                    act.wait_ge(p_dn, n * NSP + (6 if c == 0 else NSP) + 2)
                    act.wait_ge(t_mm, 3 * n + 1 + c)
                    act.activation(OT[:, c, :], m.ps[:, 6, :], ACT.Copy).then_inc(o_cp, 1)

                for si, (c, kt, rows, off) in enumerate(steps):
                    for pr in range(2):
                        u = 2 * si + pr
                        act.wait_ge(s_mm, n * NSC + u + 1)
                        act.wait_ge(p_dn, n * NSP + si + 1)
                        b0 = 2 + 2 * (u % 2)
                        act.activation(PR[0:rows, u % 4, :, off:512], m.ps[0:rows, b0:b0 + 2, off:512],
                                       ACT.Exp).then_inc(e_dn, 1)
                    if si == 6:
                        out_copy(0)
                out_copy(1)
            loop(act, body)

        @blk.vector
        def _(v):
            for s in range(S):
                v.memset(K[s][TR:MR, :, :], 1.0).then_inc(ini, 1)
            v.sem_inc(o_rd, 1)
            v.wait_ge(ini, 1 + S)

            def unit(n, u):
                h, i, c, pieces = units[u]
                v.wait_ge(nat, n * NU + u + 1)
                width = pieces[-1][0] + pieces[-1][2]
                j = CH * h + i
                v.tensor_reduce(mxp[:, j, c:c + 1], m.ps[:, u % 2, 0:width], AX_X, ALU.max).then_inc(red, 1)

            def maximum(n):
                v.wait_ge(red, (n + 1) * NU)
                v.tensor_reduce(negm[:, :], mxp[:, :, :], AX_X, ALU.max, negate=True).then_inc(mx, 1)
                v.wait_ge(mx, n * 5 + 1)
                v.tensor_copy(M3[:, 0, :], negm[:, :]).then_inc(mx, 1)
                v.wait_ge(mx, n * 5 + 2)
                v.tensor_tensor(rst[:, :], negm[:, :], M3[:, 0, :], ALU.subtract).then_inc(mx, 1)
                v.wait_ge(mx, n * 5 + 3)
                v.tensor_copy(M3[:, 1, :], rst[:, :]).then_inc(mx, 1)
                v.wait_ge(mx, n * 5 + 4)
                v.tensor_tensor(M3[:, 2, :], rst[:, :], M3[:, 1, :], ALU.subtract).then_inc(mx, 1)

            def max_rows(n, s, use, first=False):
                v.wait_ge(t_mm, 1 if first else n * 3)
                if not first:
                    ps_, pu = (s - 1) % S, use if s else use - 1
                    v.wait_ge(mr[ps_], (pu + 1) * 16)
                v.tensor_copy(MT[:, :], m.ps[0:3 * HG * CH, 7, 0:P // 2].bitcast(BF16)).then_inc(mt_rd, 1)

            def normalise(n, c, more):
                v.wait_ge(t_mm, n * 3 + (2 if c == 0 else 4 if more else 3))
                q = m.ps[:, 7, :].rearrange("p (q h e) -> p q h e", q=4, h=HG)
                v.wait_ge(o_rd, 2 * n + c + 1)
                v.reciprocal(rc[:, :, :], q[:, :, :, DH]).then_inc(r_dn, 1)
                v.wait_ge(r_dn, 2 * n + c + 1)
                v.wait_ge(o_wr[c], n * 16 + 16)
                v.tensor_tensor(O[:, c, :, :, :], q[:, :, :, 0:DH],
                                rc[:, :, :].unsqueeze(3).to_broadcast([P, 4, HG, DH]), ALU.mult).then_inc(o_rd, 1)

            for u in range(NU):
                unit(0, u)
            maximum(0)
            max_rows(0, 0, 0, first=True)

            def body(n, s, i, more):
                for si in range(NSP):
                    if more:
                        for u in unit_range(si):
                            unit(n + 1, u)
                        if si == MAXED - 1:
                            maximum(n + 1)
                        if si == MAXED:
                            s1 = (s + 1) % S
                            max_rows(n + 1, s1, i + (1 if s == S - 1 else 0))
                    if si == 8:
                        normalise(n, 0, more)
                normalise(n, 1, more)
            loop(v, body)

        @blk.tensor
        def _(pe):
            pe.sem_inc(p_dn, 2)

            def unit(n, u, s, first=False):
                h, i, c, pieces = units[u]
                if not first or u >= 2:
                    pe.wait_ge(red, n * NU + u - 1)
                bank = u % 2
                for col, k0, kn, masked in pieces:
                    mm = nc.tensor.matmul(m.ps[:, bank, col:col + kn], Q[s][0:TR, h, P * i:P * i + P],
                                          K[s][0:TR, h, k0:k0 + kn], start=True, stop=not masked)
                    if masked:
                        mm = nc.tensor.matmul(m.ps[:, bank, col + kn - P:col + kn], m.ident_bf[:, :],
                                              m.mask_bf[:, :], start=False, stop=True)
                mm.then_inc(nat, 1)

            def max_rows(n, first=False):
                pe.wait_ge(mx, n * 5 + 5)
                if not first:
                    pe.wait_ge(o_rd, 2 * n)
                nc.tensor.transpose(m.ps[0:3 * HG * CH, 7, 0:P // 2].bitcast(BF16),
                                    M3[:, :, :].rearrange("p a b -> p (a b)"), m.ident_bf[:, :]).then_inc(t_mm, 1)

            def out_rows(n, c, more):
                pe.wait_ge(o_cp, 2 * n + c + 2)
                if c == 0:
                    pe.wait_ge(mt_rd, n + 1)
                    pe.wait_ge(o_rd, 2 * n + 1)
                elif more:
                    pe.wait_ge(mt_rd, n + 2)
                else:
                    pe.wait_ge(o_rd, 2 * n + 2)
                for q in range(4):
                    mm = nc.tensor.transpose(m.ps[:, 7, P * q:P * q + P], OT[:, c, P * q:P * q + P], m.ident[:, :])
                mm.then_inc(t_mm, 1)

            def scores(n, si, s, use):
                c, kt, rows, off = steps[si]
                if si == 0:
                    pe.wait_ge(mr[s], (use + 1) * 16)
                for pr in range(2):
                    u = 2 * si + pr
                    pe.wait_ge(e_dn, n * NSC + u + 1)
                    b0 = 2 + 2 * (u % 2)
                    for j in range(2):
                        mm = nc.tensor.matmul(m.ps[0:rows, b0 + j, off:512],
                                              K[s][:, 2 * pr + j, P * kt:P * kt + rows],
                                              Q[s][:, 2 * pr + j, 512 * c + off:512 * c + 512],
                                              start=True, stop=True)
                    mm.then_inc(s_mm, 1)

            def pv(n, si, s):
                c, kt, rows, off = steps[si]
                pe.wait_ge(e_dn, n * NSC + 2 * si + 4)
                if si in diag:
                    pe.wait_ge(k_dn, n * 2 * len(diag) + 2 * diag.index(si) + 2)
                first = kt == 0
                last = kt == KT - 1
                if first:
                    pe.wait_ge(o_cp, 2 * n + c + 1)
                if rows < P:
                    pe.sem_inc(turn, 1)
                for h in range(HG):
                    mm = nc.tensor.matmul(m.ps[32 * h:32 * h + 32, 6, off:512], V[s][0:rows, kt, 32 * h:32 * h + 32],
                                          PR[0:rows, (2 * si + h // 2) % 4, h % 2, off:512],
                                          start=first, stop=last, tile_position=(0, 32 * h))
                mm.then_inc(p_dn, 1)

            pe.wait_ge(ini, 1 + S)
            pe.wait_ge(ld[0], LOADS)
            for u in range(NU):
                unit(0, u, 0, first=True)
            max_rows(0, first=True)

            def body(n, s, i, more):
                s1 = (s + 1) % S
                if more:
                    pe.wait_ge(ld[s1], (i + 1 + (1 if s == S - 1 else 0)) * LOADS)
                for si in range(NSP):
                    scores(n, si, s, i)
                    if more:
                        for u in unit_range(si):
                            unit(n + 1, u, s1)
                        if si == MAXED:
                            max_rows(n + 1)
                    if si:
                        pv(n, si - 1, s)
                    if si == 8:
                        out_rows(n, 0, more)
                pv(n, NSP - 1, s)
                out_rows(n, 1, more)
            loop(pe, body)


def phase_output(nc, m, a):
    NB = NT // 4
    with ExitStack() as st:
        sb, sem = tensors(nc, st)
        w = sb("wout", [P, 2, D])
        wh = sb("wout_high", [P, 2, D], F32R)
        wl = sb("wout_low", [P, 2, D], F32R)
        o = sb("attention_out", [P, 2, 4, NG, HG * DH])
        oh = sb("attention_t_high", [P, 2, 2, 512], F32R)
        ol = sb("attention_t_low", [P, 2, 2, 512], F32R)
        xt = sb("x2_t", [P, 2, 2, 512])
        stats = sb("ln_stats_d", [P, NT, 6])
        mv = sb("ln_mean_var_d", [P, NT, 2])
        sd = sb("ln_sd_d", [P, NT])
        rs = sb("ln_rs_d", [P, NT])
        ld = sem("wout_loaded")
        wsp = sem("wout_split")
        o_ld = [sem(f"attention_out_loaded_{i}") for i in range(2)]
        xb = sem("x1_with_bias")
        tr = sem("attention_transposed")
        oh_r = sem("attention_high_ready")
        ol_r = sem("attention_low_ready")
        pj = sem("projected")
        z_r = sem("residual_sum_ready")
        bs = sem("ln_stats_ready_d")
        ba = sem("ln_variance_ready_d")
        sq = sem("ln_sd_ready_d")
        rr = sem("ln_rs_ready_d")
        x2r = sem("x2_ready")
        x_tr = sem("x2_transposed")
        x_cp = sem("x2_t_ready")
        x_wr = sem("x2_written")
        t_wr = [sem(f"x2_t_written_{i}") for i in range(2)]
        blk = st.enter_context(nc.Block())

        @blk.sync
        def _(sp):
            sp.dma_start(w[:, :, :], a["Wout"].rearrange("(k p) n -> p k n", p=P)).then_inc(ld, 16)

            def store(g):
                sp.wait_ge(x2r, 4 * g + 4)
                sp.dma_start(m.x2_dram[512 * g:512 * g + 512, :].rearrange("(t p) d -> p t d", p=P),
                             m.x1[:, 4 * g:4 * g + 4, :]).then_inc(x_wr, 16)
                sp.wait_ge(x_cp, 2 * g + 2)
                sp.dma_start(m.x2t_dram[:, 512 * g:512 * g + 512].rearrange("(k p) t -> p k t", p=P),
                             xt[:, g % 2, :, :]).then_inc(t_wr[g % 2], 16)
            for g in range(NB):
                b, c = g // 2, g % 2
                if g >= 2:
                    sp.wait_ge(tr, 2 * g - 2)
                for hg in range(NG):
                    sp.dma_start(o[:, g % 2, :, hg, :], m.o_dram[NG * b + hg, c, :, :, :]).then_inc(o_ld[g % 2], 16)
                if g >= 2:
                    store(g - 2)
            store(NB - 2)
            store(NB - 1)
            sp.wait_ge(x_wr, 16 * NB)
            for i in range(2):
                sp.wait_ge(t_wr[i], 16 * NB // 2)

        @blk.gpsimd
        def _(gp):
            for g in range(NB):
                v = m.x1[:, 4 * g:4 * g + 4, :]
                gp.tensor_tensor(v, v, m.bout[:, :].unsqueeze(1).to_broadcast([P, 4, D]), ALU.add).then_inc(xb, 1)

        @blk.scalar
        def _(act):
            def transposed_copy(g):
                for kt in range(2):
                    act.wait_ge(x_tr, 2 * g + kt + 1)
                    if g >= 2:
                        act.wait_ge(t_wr[g % 2], 16 * (g // 2))
                    act.activation(xt[:, g % 2, kt, :], m.ps[:, 6 + kt, :], ACT.Copy).then_inc(x_cp, 1)
            for g in range(NB):
                for kt in range(2):
                    act.wait_ge(tr, 2 * g + kt + 1)
                    if g >= 2:
                        act.wait_ge(pj, 2 * g - 2)
                    act.activation(oh[:, g % 2, kt, :], m.ps[:, kt, :], ACT.Copy).then_inc(oh_r, 1)
                if g >= 1:
                    transposed_copy(g - 1)
                act.wait_ge(ba, 4 * g + 4)
                act.activation(sd[:, 4 * g:4 * g + 4], mv[:, 4 * g:4 * g + 4, 1], ACT.Sqrt,
                               bias=m.eps[:, 0:1]).then_inc(sq, 1)
            transposed_copy(NB - 1)

        @blk.vector
        def _(v):
            v.wait_ge(ld, 16)
            v.tensor_copy(wh[:, :, :], w[:, :, :]).then_inc(wsp, 1)
            v.wait_ge(wsp, 1)
            v.tensor_tensor(wl[:, :, :], w[:, :, :], wh[:, :, :].bitcast(F32), ALU.subtract).then_inc(wsp, 1)
            for g in range(NB):
                for kt in range(2):
                    v.wait_ge(oh_r, 2 * g + kt + 1)
                    v.tensor_tensor(ol[:, g % 2, kt, :], m.ps[:, kt, :], oh[:, g % 2, kt, :].bitcast(F32),
                                    ALU.subtract).then_inc(ol_r, 1)
                v.wait_ge(xb, g + 1)
                for j in range(2):
                    z = m.x1[:, 4 * g + 2 * j:4 * g + 2 * j + 2, :]
                    v.wait_ge(pj, 2 * g + j + 1)
                    v.tensor_tensor(z, m.ps[:, 2 + 2 * (g % 2) + j, :].rearrange("p (t d) -> p t d", t=2), z,
                                    ALU.add).then_inc(z_r, 1)
                for t in range(4 * g, 4 * g + 4):
                    v.wait_ge(z_r, t // 2 + 1)
                    v.bn_stats(stats[:, t, :], m.x1[:, t, :]).then_inc(bs, 1)
                for t in range(4 * g, 4 * g + 4):
                    v.wait_ge(bs, t + 1)
                    v.bn_aggr(mv[:, t, :], stats[:, t, :]).then_inc(ba, 1)
                v.wait_ge(sq, g + 1)
                v.reciprocal(rs[:, 4 * g:4 * g + 4], sd[:, 4 * g:4 * g + 4]).then_inc(rr, 1)
                v.wait_ge(rr, g + 1)
                for t in range(4 * g, 4 * g + 4):
                    v.tensor_scalar(m.x1[:, t, :], m.x1[:, t, :], mv[:, t, 0:1], rs[:, t:t + 1], ALU.subtract,
                                    ALU.mult).then_inc(x2r, 1)

        @blk.tensor
        def _(pe):
            def in_transposes(g):
                pe.wait_ge(o_ld[g % 2], 64 * (g // 2 + 1))
                for kt in range(2):
                    if g >= 1:
                        pe.wait_ge(ol_r, 2 * g - 1 + kt)
                    for q in range(4):
                        mm = nc.tensor.transpose(
                            m.ps[:, kt, P * q:P * q + P],
                            o[:, g % 2, q, 2 * kt:2 * kt + 2, :].rearrange("p g d -> p (g d)"), m.ident[:, :])
                    mm.then_inc(tr, 1)

            def out_transposes(g):
                for kt in range(2):
                    if g >= 1:
                        pe.wait_ge(x_cp, 2 * g - 1 + kt)
                    pe.wait_ge(x2r, 4 * g + 4)
                    for q in range(4):
                        mm = nc.tensor.transpose(m.ps[:, 6 + kt, P * q:P * q + P],
                                                 m.x1[:, 4 * g + q, P * kt:P * kt + P], m.ident[:, :])
                    mm.then_inc(x_tr, 1)

            pe.wait_ge(wsp, 2)
            in_transposes(0)
            for g in range(NB):
                if g + 1 < NB:
                    in_transposes(g + 1)
                pe.wait_ge(ol_r, 2 * g + 2)
                for j in range(2):
                    if g >= 2:
                        pe.wait_ge(z_r, 2 * g - 3 + j)
                    for q in range(2 * j, 2 * j + 2):
                        for i, (kt, x, y) in enumerate((kt, x, y) for kt in range(2)
                                                       for x, y in ((ol, wh), (oh, wl), (oh, wh))):
                            mm = nc.tensor.matmul(m.ps[:, 2 + 2 * (g % 2) + j, D * (q % 2):D * (q % 2) + D],
                                                  x[:, g % 2, kt, P * q:P * q + P], y[:, kt, :],
                                                  start=(i == 0), stop=(i == 5))
                    mm.then_inc(pj, 1)
                if g >= 1:
                    out_transposes(g - 1)
            out_transposes(NB - 1)


def weight_stream(nc, m, st, tag, jobs, done):
    RING = 2
    sb, sem = tensors(nc, st)
    width = jobs[0][0].shape[1]
    stage = sb(f"weight_stage_{tag}", [P, RING, width])
    s_ld = [sem(f"weight_rows_loaded_{tag}_{i}") for i in range(RING)]
    s_hi = sem(f"weight_high_ready_{tag}")

    def sync(sp):
        for n, (rows, hi, lo) in enumerate(jobs):
            if n >= RING:
                sp.wait_ge(done, n - RING + 1)
            sp.dma_start(stage[:, n % RING, 0:rows.shape[1]], rows).then_inc(s_ld[n % RING], 16)

    def vector(v):
        for n, (rows, hi, lo) in enumerate(jobs):
            v.wait_ge(s_ld[n % RING], 16 * (n // RING + 1))
            v.tensor_copy(hi, stage[:, n % RING, 0:rows.shape[1]]).then_inc(s_hi, 1)

    def gpsimd(gp):
        for n, (rows, hi, lo) in enumerate(jobs):
            gp.wait_ge(s_hi, n + 1)
            gp.tensor_tensor(lo, stage[:, n % RING, 0:rows.shape[1]], hi.bitcast(F32), ALU.subtract).then_inc(done, 1)
    return sync, vector, gpsimd


def phase_ffn_first(nc, m, a):
    NB = 8
    with ExitStack() as st:
        sb, sem = tensors(nc, st)
        w1 = [sb(f"w1_{p}", [P, 2, F], F32R) for p in ("high", "low")]
        w2 = [sb(f"w2_{p}", [P, 2, F], F32R) for p in ("high", "low")]
        h1 = [sb(f"h1_{p}", [P, 8, F], F32R) for p in ("high", "low")]
        s1 = sb("w1_scale", [P, 8])
        s2 = sb("w2_scale", [P, 8])
        s3 = sb("h1_scale", [P, 8])
        x = sb("x2_block", [P, 2, 512])
        xh = sb("x2_high", [P, 2, 512], F32R)
        xl = sb("x2_low", [P, 2, 512], F32R)
        g = sb("silu_out", [P, 2, 512])
        h = sb("gated", [P, 2, 512])
        hh = sb("gated_high", [P, 2, 8, 512], F32R)
        hl = sb("gated_low", [P, 2, 8, 512], F32R)
        y = sb("gelu_out", [P, 4, 512])
        sc = sem("scales_loaded")
        w_dn = sem("weight_rows_split")
        x_ld = sem("x2_block_loaded")
        x_hi = sem("x2_high_ready")
        x_lo = sem("x2_low_ready")
        u_mm = sem("up_pair_done")
        g_r = sem("silu_ready")
        h_r = sem("gated_ready")
        hh_r = sem("gated_high_ready")
        hl_r = sem("gated_low_ready")
        y_mm = sem("hidden_tile_done")
        y_r = sem("gelu_ready")
        y_wr = [sem(f"gelu_written_{i}") for i in range(4)]
        jobs = []
        for name, w in (("w1_T", w1), ("w2_T", w2), ("h1_T", h1)):
            for k in range(a[name].shape[0] // P):
                jobs.append((a[name][P * k:P * k + P, :], w[0][:, k, :], w[1][:, k, :]))
        w_sync, w_vec, w_pool = weight_stream(nc, m, st, "a", jobs, w_dn)
        hd = m.h_dram.rearrange("(k p) (b t) -> b k p t", p=P, t=512)
        blk = st.enter_context(nc.Block())

        def block_loop(eng, up, down):
            up(0, 0)
            with eng.Fori(0, NB // 2 - 1) as i:
                for p in range(2):
                    up(i * 2 + (p + 1), (p + 1) % 2)
                    down(i * 2 + p, p)
            up(NB - 1, 1)
            down(NB - 2, 0)
            down(NB - 1, 1)

        @blk.sync
        def _(sp):
            for t, n in ((s1, "w1_s"), (s2, "w2_s"), (s3, "h1_s")):
                sp.dma_start(t[:, :], a[n]).then_inc(sc, 16)
            sp.dma_start(x[:, :, :], m.x2t_dram[:, 0:512].rearrange("(k p) t -> p k t", p=P)).then_inc(x_ld, 16)
            w_sync(sp)
            x2t = m.x2t_dram.rearrange("(k p) (b t) -> b p k t", p=P, t=512)
            with sp.Fori(1, NB) as t:
                sp.wait_ge(x_lo, t)
                sp.dma_start(x[:, :, :], x2t[t, :, :, :]).then_inc(x_ld, 16)

        @blk.gpsimd
        def _(gp):
            gp.sem_inc(hl_r, 2)
            w_pool(gp)

            def up(t, p):
                for mt in range(8):
                    gp.wait_ge(hh_r, t * 8 + (mt + 1))
                    gp.tensor_tensor(hl[:, p, mt, :], h[:, mt % 2, :], hh[:, p, mt, :].bitcast(F32),
                                     ALU.subtract).then_inc(hl_r, 1)
            block_loop(gp, up, lambda t, p: None)

        @blk.scalar
        def _(act):
            act.sem_inc(y_r, 4)
            for s in range(4):
                act.sem_inc(y_wr[s], 16)
            act.wait_ge(sc, 48)

            def up(t, p):
                act.wait_ge(x_ld, t * 16 + 16)
                act.wait_ge(u_mm, t * 8)
                act.activation(xh[:, :, :], x[:, :, :], ACT.Copy).then_inc(x_hi, 1)

                def high(mt):
                    act.wait_ge(h_r, t * 8 + (mt + 3))
                    act.activation(hh[:, p, mt, :], h[:, mt % 2, :], ACT.Copy).then_inc(hh_r, 1)
                for mt in range(8):
                    act.wait_ge(u_mm, t * 8 + (mt + 1))
                    act.wait_ge(h_r, t * 8 + (mt + 1))
                    act.activation(g[:, mt % 2, :], m.ps[:, 2 * (mt % 2), :], ACT.Silu,
                                   scale=s1[:, mt:mt + 1]).then_inc(g_r, 1)
                    if mt:
                        high(mt - 1)
                high(7)

            def down(t, p):
                for mt in range(8):
                    s = mt % 4
                    act.wait_ge(y_mm, t * 8 + (mt + 1))
                    act.wait_ge(y_wr[s], t * 32 + 16 * (mt // 4 + 1))
                    act.activation(y[:, s, :], m.ps[:, 4 + s, :], ACT.Gelu, scale=s3[:, mt:mt + 1]).then_inc(y_r, 1)
                    act.wait_ge(y_r, t * 8 + (mt + 5))
                    act.dma_start(hd[t, mt, :, :], y[:, s, :]).then_inc(y_wr[s], 16)
            block_loop(act, up, down)
            for s in range(4):
                act.wait_ge(y_wr[s], NB * 32 + 16)

        @blk.vector
        def _(v):
            v.sem_inc(h_r, 2)
            w_vec(v)
            v.wait_ge(sc, 48)

            def up(t, p):
                v.wait_ge(x_hi, t + 1)
                v.tensor_tensor(xl[:, :, :], x[:, :, :], xh[:, :, :].bitcast(F32), ALU.subtract).then_inc(x_lo, 1)
                for mt in range(8):
                    v.wait_ge(g_r, t * 8 + (mt + 1))
                    v.wait_ge(hl_r, t * 8 + (mt + 1))
                    v.scalar_tensor_tensor(h[:, mt % 2, :], m.ps[:, 2 * (mt % 2) + 1, :], s2[:, mt:mt + 1],
                                           g[:, mt % 2, :], ALU.mult, ALU.mult).then_inc(h_r, 1)
            block_loop(v, up, lambda t, p: None)

        @blk.tensor
        def _(pe):
            def up(t, p):
                pe.wait_ge(x_lo, t + 1)
                for mt in range(8):
                    pe.wait_ge(h_r, t * 8 + (mt + 1))
                    for j, w in enumerate((w1, w2)):
                        for i, (kt, wi, xx) in enumerate((kt, wi, xx) for kt in range(2)
                                                         for wi, xx in ((0, xl), (1, xh), (0, xh))):
                            mm = nc.tensor.matmul(m.ps[:, 2 * (mt % 2) + j, :], w[wi][:, kt, P * mt:P * mt + P],
                                                  xx[:, kt, :], start=(i == 0), stop=(i == 5))
                    mm.then_inc(u_mm, 1)

            def down(t, p):
                pe.wait_ge(hl_r, t * 8 + 10)
                for mt in range(8):
                    pe.wait_ge(y_r, t * 8 + (mt + 1))
                    for i, (kt, wi, xx) in enumerate((kt, wi, xx) for kt in range(8)
                                                     for wi, xx in ((0, hl), (1, hh), (0, hh))):
                        mm = nc.tensor.matmul(m.ps[:, 4 + mt % 4, :], h1[wi][:, kt, P * mt:P * mt + P],
                                              xx[:, p, kt, :], start=(i == 0), stop=(i == 23))
                    mm.then_inc(y_mm, 1)
            pe.wait_ge(w_dn, len(jobs))
            block_loop(pe, up, down)


def phase_ffn_second(nc, m, a, out):
    NB = 8
    with ExitStack() as st:
        sb, sem = tensors(nc, st)
        h2 = [sb(f"h2_{p}", [P, 8, F], F32R) for p in ("high", "low")]
        w3 = [sb(f"w3_{p}", [P, 8, D], F32R) for p in ("high", "low")]
        s4 = sb("h2_scale", [P, 8])
        s5 = sb("w3_scale", [P, D])
        hs = sb("hidden_rows", [P, 4, 512])
        hh = sb("hidden_high", [P, 2, 8, 512], F32R)
        hl = sb("hidden_low", [P, 2, 8, 512], F32R)
        g = sb("gelu2_out", [P, 2, 512])
        gh = sb("gelu2_high", [P, 8, 512], F32R)
        gl = sb("gelu2_low", [P, 8, 512], F32R)
        z = sb("sum", [P, 4, D])
        x2 = sb("x2_tiles", [P, 4, D])
        stats = sb("ln_stats_e", [P, 4, 6])
        mv = sb("ln_mean_var_e", [P, 4, 2])
        sd = sb("ln_sd_e", [P, 4])
        rs = sb("ln_rs_e", [P, 4])
        sc = sem("scales_loaded_e")
        w_dn = sem("weight_rows_split_e")
        r_ld = [sem(f"hidden_row_loaded_{i}") for i in range(4)]
        hh_r = sem("hidden_high_ready")
        hl_r = sem("hidden_low_ready")
        y_mm = sem("hidden2_tile_done")
        g_r = sem("gelu2_ready")
        gh_r = sem("gelu2_high_ready")
        gl_r = sem("gelu2_low_ready")
        o_mm = sem("w3_block_done")
        x_ld = sem("x2_tiles_loaded")
        z_m = sem("scaled_ready")
        z_a = sem("sum_ready")
        bs = sem("ln_stats_ready_e")
        ba = sem("ln_variance_ready_e")
        sq = sem("ln_sd_ready_e")
        rr = sem("ln_rs_ready_e")
        o_r = sem("out_tiles_ready")
        turn = sem("waits_carried_e")
        o_wr = sem("out_written")
        jobs = []
        for name, w in (("h2_T", h2), ("w3_T", w3)):
            for k in range(8):
                jobs.append((a[name][P * k:P * k + P, :], w[0][:, k, :], w[1][:, k, :]))
        w_sync, w_vec, w_pool = weight_stream(nc, m, st, "b", jobs, w_dn)
        hd = m.h_dram.rearrange("(k p) (b t) -> b k p t", p=P, t=512)
        x2d = m.x2_dram.rearrange("(b t p) d -> b p t d", p=P, t=4)
        od = out.rearrange("(b t p) d -> b p t d", p=P, t=4)
        blk = st.enter_context(nc.Block())

        def block_loop(eng, body):
            with eng.Fori(0, NB // 2 - 1) as i:
                for p in range(2):
                    body(i * 2 + p, p, True)
            body(NB - 2, 0, True)
            body(NB - 1, 1, False)

        @blk.sync
        def _(sp):
            sp.sem_inc(o_wr, 16)
            sp.dma_start(s4[:, :], a["h2_s"]).then_inc(sc, 16)
            sp.dma_start(s5[:, :], a["w3_s"].partition_broadcast(P)).then_inc(sc, 16)

            def rows(t):
                for k in range(8):
                    sp.wait_ge(hl_r, t * 8 + (k + 1))
                    sp.dma_start(hs[:, k % 4, :], hd[t, k, :, :]).then_inc(r_ld[k % 4], 16)
            rows(0)
            w_sync(sp)

            def body(t, p, more):
                sp.wait_ge(z_a, t + 1)
                sp.dma_start(x2[:, :, :], x2d[t, :, :, :]).then_inc(x_ld, 16)
                if more:
                    rows(t + 1)
                sp.wait_ge(o_r, t * 4 + 4)
                sp.dma_start(od[t, :, :, :], z[:, :, :]).then_inc(o_wr, 16)
            block_loop(sp, body)
            sp.wait_ge(o_wr, 16 * NB + 16)

        @blk.gpsimd
        def _(gp):
            gp.sem_inc(gl_r, 2)
            gp.sem_inc(z_a, 1)
            w_pool(gp)

            def body(t, p, more):
                for mt in range(8):
                    gp.wait_ge(gh_r, t * 8 + (mt + 1))
                    gp.tensor_tensor(gl[:, mt, :], g[:, mt % 2, :], gh[:, mt, :].bitcast(F32),
                                     ALU.subtract).then_inc(gl_r, 1)
                gp.wait_ge(x_ld, t * 16 + 16)
                gp.wait_ge(z_m, t * 4 + 8)
                gp.tensor_tensor(z[:, :, :], z[:, :, :], x2[:, :, :], ALU.add).then_inc(z_a, 1)
            block_loop(gp, body)

        @blk.scalar
        def _(act):
            act.sem_inc(g_r, 4)

            def high(t, p, k):
                act.wait_ge(r_ld[k % 4], t * 32 + 16 * (k // 4 + 1))
                act.activation(hh[:, p, k, :], hs[:, k % 4, :], ACT.Copy).then_inc(hh_r, 1)
            for k in range(8):
                high(0, 0, k)
            act.wait_ge(sc, 32)

            def body(t, p, more):
                for mt in range(8):
                    act.wait_ge(y_mm, t * 8 + (mt + 1))
                    act.wait_ge(gl_r, t * 8 + (mt + 1))
                    act.activation(g[:, mt % 2, :], m.ps[:, mt % 4, :], ACT.Gelu, scale=s4[:, mt:mt + 1]).then_inc(g_r, 1)
                    if more:
                        high(t + 1, 1 - p, mt)
                act.wait_ge(ba, t * 4 + 4)
                act.activation(sd[:, :], mv[:, :, 1], ACT.Sqrt, bias=m.eps[:, 0:1]).then_inc(sq, 1)
            block_loop(act, body)

        @blk.vector
        def _(v):
            v.sem_inc(hl_r, 4)
            v.sem_inc(z_m, 4)

            def low(t, p, k):
                v.wait_ge(hh_r, t * 8 + (k + 1))
                v.tensor_tensor(hl[:, p, k, :], hs[:, k % 4, :], hh[:, p, k, :].bitcast(F32),
                                ALU.subtract).then_inc(hl_r, 1)
            for k in range(8):
                low(0, 0, k)
            w_vec(v)
            v.wait_ge(sc, 32)

            def body(t, p, more):
                for mt in range(8):
                    v.wait_ge(g_r, t * 8 + (mt + 5))
                    v.tensor_copy(gh[:, mt, :], g[:, mt % 2, :]).then_inc(gh_r, 1)
                    if more:
                        low(t + 1, 1 - p, mt)
                v.wait_ge(o_mm, t + 1)
                v.wait_ge(o_wr, t * 16 + 16)
                for q in range(4):
                    v.tensor_tensor(z[:, q, :], m.ps[:, 4 + q, 0:D], s5[:, :], ALU.mult).then_inc(z_m, 1)
                v.wait_ge(z_a, t + 2)
                for q in range(4):
                    v.bn_stats(stats[:, q, :], z[:, q, :]).then_inc(bs, 1)
                v.wait_ge(bs, t * 4 + 4)
                v.sem_inc(turn, 1)
                for q in range(4):
                    v.bn_aggr(mv[:, q, :], stats[:, q, :]).then_inc(ba, 1)
                v.wait_ge(sq, t + 1)
                v.reciprocal(rs[:, :], sd[:, :]).then_inc(rr, 1)
                v.wait_ge(rr, t + 1)
                for q in range(4):
                    v.tensor_scalar(z[:, q, :], z[:, q, :], mv[:, q, 0:1], rs[:, q:q + 1], ALU.subtract,
                                    ALU.mult).then_inc(o_r, 1)
            block_loop(v, body)

        @blk.tensor
        def _(pe):
            def body(t, p, more):
                pe.wait_ge(hl_r, t * 8 + 12)
                for mt in range(8):
                    pe.wait_ge(g_r, t * 8 + (mt + 1))
                    for i, (kt, wi, xx) in enumerate((kt, wi, xx) for kt in range(8)
                                                     for wi, xx in ((0, hl), (1, hh), (0, hh))):
                        mm = nc.tensor.matmul(m.ps[:, mt % 4, :], h2[wi][:, kt, P * mt:P * mt + P],
                                              xx[:, p, kt, :], start=(i == 0), stop=(i == 23))
                    mm.then_inc(y_mm, 1)
                pe.wait_ge(z_m, t * 4 + 4)
                for kt in range(8):
                    pe.wait_ge(gl_r, t * 8 + (kt + 3))
                    for q in range(4):
                        for i, (xx, wi) in enumerate(((gl, 0), (gh, 1), (gh, 0))):
                            mm = nc.tensor.matmul(m.ps[:, 4 + q, 0:D], xx[:, kt, P * q:P * q + P], w3[wi][:, kt, :],
                                                  start=(kt == 0 and i == 0), stop=(kt == 7 and i == 2))
                mm.then_inc(o_mm, 1)
            pe.wait_ge(w_dn, len(jobs))
            block_loop(pe, body)


def build(nc, a, out):
    m = Mem()
    with ExitStack() as st:
        def sb(name, shape, dtype=F32):
            return st.enter_context(nc.sbuf_tensor(name, shape, dtype))
        m.ps = st.enter_context(nc.psum_tensor("psum", [P, 8, 512], F32))
        m.ident = sb("ident", [P, P])
        m.ident_bf = sb("ident_bf", [P, P], BF16)
        m.mask_bf = sb("causal_mask", [P, P], BF16)
        m.eps = sb("eps", [P, 1])
        m.kpad_dram = nc.dram_tensor("kpad_scratch", [D, 256], F32).ap()
        m.q_dram = nc.dram_tensor("q_scratch", [IT, HG * DH, 3, L], BF16).ap()
        m.k_dram = nc.dram_tensor("k_scratch", [IT, HG * DH, 3, KP], BF16).ap()
        m.v_dram = nc.dram_tensor("v_scratch", [IT, KT * P, HG * 32], F32).ap()
        m.o_dram = nc.dram_tensor("o_scratch", [IT, 2, P, 4, HG * DH], F32).ap()
        m.max_dram = nc.dram_tensor("max_scratch", [3 * HG * CH, P], BF16).ap()
        m.x2t_dram = nc.dram_tensor("x2t_scratch", [D, B * L], F32).ap()
        m.x2_dram = nc.dram_tensor("x2_scratch", [B * L, D], F32).ap()
        m.h_dram = nc.dram_tensor("h_scratch", [F, B * L], F32).ap()
        with ExitStack() as st1:
            m.bout = st1.enter_context(nc.sbuf_tensor("bout", [P, D], F32))
            m.x1 = st1.enter_context(nc.sbuf_tensor("x1", [P, NT, D], F32))
            phase_convolution(nc, m, a)
            with ExitStack() as st2:
                m.x1h = st2.enter_context(nc.sbuf_tensor("x1t_high", [P, 2, B * L], F32R))
                m.x1l = st2.enter_context(nc.sbuf_tensor("x1t_low", [P, 2, B * L], F32R))
                phase_transpose(nc, m)
                phase_projections(nc, m, a)
            phase_attention(nc, m, a)
            phase_output(nc, m, a)
        phase_ffn_first(nc, m, a)
        phase_ffn_second(nc, m, a, out)


def kernel(**inputs):
    import concourse.bacc as _bacc
    from concourse.bass_utils import run_bass_kernel_spmd as _run

    g = {k: np.asarray(v) for k, v in inputs.items()}
    x = g["x"].reshape(B * L, D)
    laid = {
        "x": x,
        "x_rev": x.reshape(NT, P, D)[:, ::-1].reshape(B * L, D),
        "ctx_T": g["ctx_1024"].reshape(B * M, D).T,
        "A_log": g["L0_attn_A_log"],
        "C_T": g["L0_attn_C"].T,
        "delta": g["L0_attn_delta"],
        "freq_align": g["L0_attn_freq_align"],
        "fa_cols": g["L0_attn_freq_align"].reshape(2, P).T,
        "d_cols": g["L0_attn_D"].reshape(2, P).T,
        "reward": g["L0_attn_reward"],
        "gamma": g["L0_attn_gamma"],
        "beta": g["L0_attn_beta"],
        "Wq": g["L0_xattn_Wq"],
        "Wkv": g["L0_xattn_Wkv"],
        "Wout": g["L0_xattn_Wout"],
        "bout": g["L0_xattn_bout"],
    }
    for n in ("w1", "w2", "h1", "h2", "w3"):
        laid[n + "_T"] = g[f"L0_ffn_{n}_w"].T
    for n in ("w1", "w2", "h1", "h2"):
        laid[n + "_s"] = g[f"L0_ffn_{n}_s"].reshape(8, P).T
    laid["w3_s"] = g["L0_ffn_w3_s"]

    nc = _bacc.Bacc("TRN2", target_bir_lowering=False, num_devices=1)
    arrays, aps = {}, {}
    for name, v in laid.items():
        v = np.ascontiguousarray(v)
        arrays[f"in_{name}"] = v
        aps[name] = nc.dram_tensor(f"in_{name}", v.shape, mybir.dt.from_np(v.dtype), kind="ExternalInput").ap()
    out = nc.dram_tensor("out", (B * L, D), F32, kind="ExternalOutput").ap()
    build(nc, aps, out)
    r = _run(nc, [arrays], core_ids=[0])
    return r.results[0]["out"].reshape(B, L, D)
```

```python
import numpy as np
from contextlib import ExitStack

import concourse.bass as bass
from concourse import mybir

ALU = mybir.AluOpType
ACT = mybir.ActivationFunctionType
AX_X = mybir.AxisListType.X
F32 = mybir.dt.float32
F32R = mybir.dt.float32r
BF16 = mybir.dt.bfloat16

P = 128
B, L, D = 4, 1024, 256
NT = B * L // P
CH = L // P
NS = 64
M = 154
H, DH = 16, 16
HG = 4
NG = H // HG
IT = B * NG
KEYS = L + M
KP = 1184
KT = 10
F = 1024
EPS = 1e-5
NEG = -1.0e30
LOWEST = -3.0e38


class Mem:
    pass


def tensors(nc, stack):
    def sb(name, shape, dtype=F32):
        return stack.enter_context(nc.sbuf_tensor(name, shape, dtype))

    def sem(name):
        return stack.enter_context(nc.semaphore(name))
    return sb, sem


def phase_convolution(nc, m, a):
    GR = 16
    NGR = D // GR
    RING = 4
    with ExitStack() as st:
        sb, sem = tensors(nc, st)
        U = sb("x_reversed", [P, NT, D])
        Y = sb("conv_out", [P, NT, D])
        TZ = sb("toeplitz", [P, RING, GR, P])
        HS = sb("states", [NS, 2, B, D])
        CHs = sb("states_times_c", [NS, CH - 1, B, D])
        kpad = sb("k_padded", [P, 2, 256])
        alog_col = sb("alog_col", [NS, 1])
        alog_row = sb("alog_row", [P, NS])
        delta0 = sb("delta0", [P, 1])
        ct = sb("c_transposed", [NS, D])
        fa_row = sb("freq_align_row", [NS, D])
        fa_col = sb("freq_align_col", [P, 2])
        d_col = sb("d_col", [P, 2])
        rew = sb("reward", [1, D])
        gam = sb("gamma", [P, D])
        bet = sb("beta", [P, D])
        e_col = sb("exp_alog_col", [NS, 1])
        z_col = sb("z_col", [NS, 1])
        e_row = sb("exp_alog_row", [P, NS])
        z_row = sb("z_row", [P, NS])
        l_row = sb("l_row", [NS, P + 1])
        p1_col = sb("p_plus_1", [P, 1])
        pw = sb("powers", [NS, P + 1])
        prev = sb("powers_to_chunk_end", [P, NS])
        cta = sb("c_times_fa", [NS, D])
        dfa = sb("d_times_fa", [P, 2])
        stats = sb("ln_stats", [P, NT, 6])
        mv = sb("ln_mean_var", [P, NT, 2])
        sd = sb("ln_sd", [P, NT])
        rs = sb("ln_rs", [P, NT])

        par = sem("params_loaded")
        u_ld = sem("x_reversed_loaded")
        x_ld = sem("x_loaded")
        io = sem("iota_ready")
        a_dn = sem("act_done")
        v_dn = sem("dve_done")
        k_mm = sem("k_matmul_done")
        k_rd = sem("k_padded_ready")
        k_wr = sem("k_written")
        t_ld = [sem(f"toeplitz_loaded_{i}") for i in range(RING)]
        t_us = sem("toeplitz_group_done")
        g_mm = sem("chunk_sum_matmul_done")
        g_rd = sem("state_updated")
        c_rd = sem("states_times_c_ready")
        y_mm = sem("carry_matmul_done")
        y_cp = sem("carry_copied")
        t_ev = sem("toeplitz_bank_read")
        ln_v = sem("ln_variance_ready")
        ln_s = sem("ln_sd_ready")
        n_rd = sem("normalised_ready")
        n_gb = sem("residual_ready")
        pool = sem("pool_step")
        x1_rd = sem("x1_ready")
        st_rd = sem("bn_stats_ready")
        rs_rd = sem("ln_rs_ready")
        blk = st.enter_context(nc.Block())
        Yv = Y[:, :, :].rearrange("p (b c) d -> p b c d", b=B)
        Uv = U[:, :, :].rearrange("p (b c) d -> p b c d", b=B)
        PARAMS = 11

        def layer_norm_tiles(v, r):
            for h in range(2):
                for t in range(16 * h, 16 * h + 16):
                    if r == 1:
                        v.wait_ge(n_gb, t // 8 + 1)
                    v.bn_stats(stats[:, t, :], Y[:, t, :]).then_inc(st_rd, 1)
                for t in range(16 * h, 16 * h + 16):
                    v.wait_ge(st_rd, NT * r + t + 1)
                    v.bn_aggr(mv[:, t, :], stats[:, t, :]).then_inc(ln_v, 1)
            for h in range(2):
                v.wait_ge(ln_s, 2 * r + h + 1)
                sl = slice(16 * h, 16 * h + 16)
                v.reciprocal(rs[:, sl], sd[:, sl]).then_inc(rs_rd, 1)
                v.wait_ge(rs_rd, 2 * r + h + 1)
                for t in range(16 * h, 16 * h + 16):
                    out = Y[:, t, :] if r == 0 else m.x1[:, t, :]
                    v.tensor_scalar(out, Y[:, t, :], mv[:, t, 0:1], rs[:, t:t + 1], ALU.subtract,
                                    ALU.mult).then_inc(n_rd if r == 0 else x1_rd, 1)

        @blk.sync
        def _(sp):
            sp.dma_start(alog_col[:, :], a["A_log"].rearrange("(n a) -> n a", a=1)).then_inc(par, 16)
            sp.dma_start(alog_row[:, :], a["A_log"].partition_broadcast(P)).then_inc(par, 16)
            sp.dma_start(delta0[:, :], a["delta"][0:1].partition_broadcast(P)).then_inc(par, 16)
            sp.dma_start(ct[:, :], a["C_T"]).then_inc(par, 16)
            sp.dma_start(fa_row[:, :], a["freq_align"].partition_broadcast(NS)).then_inc(par, 16)
            sp.dma_start(fa_col[:, :], a["fa_cols"]).then_inc(par, 16)
            sp.dma_start(d_col[:, :], a["d_cols"]).then_inc(par, 16)
            sp.dma_start(rew[:, :], a["reward"].partition_broadcast(1)).then_inc(par, 16)
            sp.dma_start(gam[:, :], a["gamma"].partition_broadcast(P)).then_inc(par, 16)
            sp.dma_start(bet[:, :], a["beta"].partition_broadcast(P)).then_inc(par, 16)
            sp.dma_start(m.bout[:, :], a["bout"].partition_broadcast(P)).then_inc(par, 16)
            sp.dma_start(U[:, :, :], a["x_rev"].rearrange("(t p) d -> p t d", p=P)).then_inc(u_ld, 16)
            sp.wait_ge(k_rd, 1)
            sp.dma_start(m.kpad_dram.rearrange("(m p) l -> p m l", p=P), kpad[:, :, :]).then_inc(k_wr, 16)
            sp.wait_ge(k_wr, 16)
            for g in range(NGR):
                if g >= RING:
                    sp.wait_ge(t_us, g - RING + 1)
                src = bass.AP(m.kpad_dram.tensor, g * GR * 256, [[1, P], [256, GR], [1, P]])
                sp.dma_start(TZ[:, g % RING, :, :], src).then_inc(t_ld[g % RING], 16)
            sp.dma_start(m.x1[:, :, :], a["x"].rearrange("(t p) d -> p t d", p=P)).then_inc(x_ld, 16)

        @blk.gpsimd
        def _(gp):
            gp.iota(l_row[:, :], [[1, P + 1]], base=0, channel_multiplier=0,
                    allow_small_or_imprecise_dtypes=True).then_inc(io, 1)
            gp.iota(p1_col[:, :], [[0, 1]], base=1, channel_multiplier=1,
                    allow_small_or_imprecise_dtypes=True).then_inc(io, 1)
            gp.memset(kpad[:, :, :], 0.0).then_inc(io, 1)
            gp.memset(Yv[:, :, 0, :], 0.0).then_inc(io, 1)
            gp.memset(m.ident[:, :], 0.0).then_inc(pool, 1)
            gp.memset(m.ident_bf[:, :], 0.0).then_inc(pool, 1)
            gp.memset(m.mask_bf[:, :], 0.0).then_inc(pool, 1)
            gp.memset(m.eps[:, :], EPS).then_inc(pool, 1)
            gp.wait_ge(pool, 4)
            gp.affine_select(out=m.ident[:, :], in_=m.ident[:, :], compare_op=ALU.not_equal, fill=1.0,
                             base=0, pattern=[[-1, P]], channel_multiplier=1).then_inc(pool, 1)
            gp.affine_select(out=m.ident_bf[:, :], in_=m.ident_bf[:, :], compare_op=ALU.not_equal, fill=1.0,
                             base=0, pattern=[[-1, P]], channel_multiplier=1).then_inc(pool, 1)
            gp.affine_select(out=m.mask_bf[:, :], in_=m.mask_bf[:, :], compare_op=ALU.is_ge, fill=NEG,
                             base=0, pattern=[[-1, P]], channel_multiplier=1).then_inc(pool, 1)
            gp.wait_ge(par, 16 * PARAMS)
            gp.wait_ge(x_ld, 16)
            steps = 7
            for q in range(4):
                t0 = 8 * q
                v = Y[:, t0:t0 + 8, :]
                gp.wait_ge(n_rd, 8 * (q + 1))
                gp.tensor_tensor(v, v, gam[:, :].unsqueeze(1).to_broadcast([P, 8, D]), ALU.mult).then_inc(pool, 1)
                gp.wait_ge(pool, steps + 1)
                gp.tensor_tensor(v, v, bet[:, :].unsqueeze(1).to_broadcast([P, 8, D]), ALU.add).then_inc(pool, 1)
                gp.wait_ge(pool, steps + 2)
                steps += 2
                gp.tensor_tensor(v, v, m.x1[:, t0:t0 + 8, :], ALU.add).then_inc(n_gb, 1)

        @blk.scalar
        def _(act):
            act.wait_ge(par, 16 * PARAMS)
            act.activation(e_col[:, :], alog_col[:, :], ACT.Exp).then_inc(a_dn, 1)
            act.activation(e_row[:, :], alog_row[:, :], ACT.Exp).then_inc(a_dn, 1)
            act.wait_ge(io, 2)
            act.wait_ge(v_dn, 2)
            act.activation(pw[:, :], l_row[:, :], ACT.Exp, scale=z_col[:, 0:1]).then_inc(a_dn, 1)
            act.activation(prev[:, :], z_row[:, :], ACT.Exp, scale=p1_col[:, 0:1]).then_inc(a_dn, 1)
            for i in range(2 * (CH - 1)):
                c, half = i // 2, i % 2
                act.wait_ge(y_mm, i + 1)
                act.activation(Yv[:, 2 * half:2 * half + 2, c + 1, :],
                               m.ps[:, 2 + i % 2, :].rearrange("p (b d) -> p b d", b=2), ACT.Copy).then_inc(y_cp, 1)
            act.wait_ge(pool, 4)
            for r in range(2):
                for h in range(2):
                    act.wait_ge(ln_v, 16 * (2 * r + h + 1))
                    sl = slice(16 * h, 16 * h + 16)
                    act.activation(sd[:, sl], mv[:, sl, 1], ACT.Sqrt, bias=m.eps[:, 0:1]).then_inc(ln_s, 1)

        @blk.vector
        def _(v):
            v.wait_ge(par, 16 * PARAMS)
            v.wait_ge(a_dn, 2)
            v.tensor_scalar(z_col[:, :], e_col[:, :], delta0[0:NS, 0:1], -1.0, ALU.mult, ALU.mult).then_inc(v_dn, 1)
            v.tensor_scalar(z_row[:, :], e_row[:, :], delta0[:, 0:1], -1.0, ALU.mult, ALU.mult).then_inc(v_dn, 1)
            v.tensor_tensor(cta[:, :], ct[:, :], fa_row[:, :], ALU.mult).then_inc(v_dn, 1)
            v.tensor_tensor(dfa[:, :], d_col[:, :], fa_col[:, :], ALU.mult).then_inc(v_dn, 1)
            v.wait_ge(k_mm, 1)
            v.wait_ge(io, 3)
            v.tensor_copy(kpad[:, :, P - 1:2 * P - 1],
                          m.ps[:, 0, 0:256].rearrange("p (m l) -> p m l", m=2)).then_inc(v_dn, 1)
            v.wait_ge(v_dn, 5)
            v.tensor_tensor(kpad[:, :, P - 1], kpad[:, :, P - 1], dfa[:, :], ALU.add).then_inc(k_rd, 1)
            for i in range(2 * (CH - 1)):
                c, half = i // 2, i % 2
                bs = slice(2 * half, 2 * half + 2)
                v.wait_ge(g_mm, i + 1)
                g = m.ps[0:NS, i % 2, :].rearrange("p (b d) -> p b d", b=2)
                if c == 0:
                    v.tensor_copy(HS[:, c % 2, bs, :], g).then_inc(g_rd, 1)
                else:
                    v.wait_ge(g_rd, i - 1)
                    v.scalar_tensor_tensor(HS[:, c % 2, bs, :].rearrange("p b d -> p (b d)"),
                                           HS[:, (c - 1) % 2, bs, :].rearrange("p b d -> p (b d)"), pw[:, P:P + 1],
                                           m.ps[0:NS, i % 2, :], ALU.mult, ALU.add).then_inc(g_rd, 1)
                v.wait_ge(g_rd, i + 1)
                v.tensor_tensor(CHs[:, c, bs, :], HS[:, c % 2, bs, :],
                                cta[:, :].unsqueeze(1).to_broadcast([NS, 2, D]), ALU.mult).then_inc(c_rd, 1)
            v.wait_ge(y_cp, 2 * (CH - 1))
            v.wait_ge(io, 4)
            for g in range(NGR):
                v.wait_ge(t_us, g + 1)
                yd = Y[:, :, GR * g:GR * g + GR].rearrange("p t d -> p d t")
                v.tensor_tensor(yd, m.ps[:, 4 + g % 4, :].rearrange("p (d t) -> p d t", d=GR), yd,
                                ALU.add).then_inc(t_ev, 1)
            v.wait_ge(t_ev, NGR)
            v.tensor_tensor(Yv[0:1, :, 0, :], Yv[0:1, :, 0, :],
                            rew[0:1, :].unsqueeze(1).to_broadcast([1, B, D]), ALU.add).then_inc(v_dn, 1)
            v.wait_ge(v_dn, 6)
            layer_norm_tiles(v, 0)
            layer_norm_tiles(v, 1)

        @blk.tensor
        def _(pe):
            pe.wait_ge(a_dn, 4)
            pe.wait_ge(v_dn, 3)
            for mt in range(2):
                mm = nc.tensor.matmul(m.ps[:, 0, P * mt:P * mt + P], cta[:, P * mt:P * mt + P], pw[:, 0:P],
                                      start=True, stop=True)
            mm.then_inc(k_mm, 1)
            pe.wait_ge(u_ld, 16)
            pe.wait_ge(k_rd, 1)

            def carry(i):
                c, half = i // 2, i % 2
                pe.wait_ge(c_rd, i + 1)
                if i >= 2:
                    pe.wait_ge(y_cp, i - 1)
                nc.tensor.matmul(m.ps[:, 2 + i % 2, :], pw[:, 0:P],
                                 CHs[:, c, 2 * half:2 * half + 2, :].rearrange("p b d -> p (b d)"),
                                 start=True, stop=True).then_inc(y_mm, 1)
            for i in range(2 * (CH - 1)):
                c, half = i // 2, i % 2
                if i >= 2:
                    pe.wait_ge(g_rd, i - 1)
                nc.tensor.matmul(m.ps[0:NS, i % 2, :], prev[:, :], Uv[:, 2 * half:2 * half + 2, c, :],
                                 start=True, stop=True).then_inc(g_mm, 1)
                if i >= 2:
                    carry(i - 2)
            carry(2 * CH - 4)
            carry(2 * CH - 3)
            for g in range(NGR):
                pe.wait_ge(t_ld[g % RING], 16 * (g // RING + 1))
                if g >= 4:
                    pe.wait_ge(t_ev, g - 3)
                for j in range(GR):
                    mm = nc.tensor.matmul(m.ps[:, 4 + g % 4, NT * j:NT * j + NT], TZ[:, g % RING, j, :],
                                          U[:, :, GR * g + j], start=True, stop=True)
                mm.then_inc(t_us, 1)


def phase_transpose(nc, m):
    with ExitStack() as st:
        sb, sem = tensors(nc, st)
        tr = sem("transposes_done")
        tr_h = sem("high_part_ready")
        tr_l = sem("low_part_ready")
        blk = st.enter_context(nc.Block())

        @blk.tensor
        def _(pe):
            for i in range(16):
                kt, tg = i % 2, i // 2
                if i >= 4:
                    pe.wait_ge(tr_l, i - 3)
                for j in range(4):
                    mm = nc.tensor.transpose(m.ps[:, i % 4, P * j:P * j + P],
                                             m.x1[:, 4 * tg + j, P * kt:P * kt + P], m.ident[:, :])
                mm.then_inc(tr, 1)

        @blk.scalar
        def _(act):
            for i in range(16):
                act.wait_ge(tr, i + 1)
                kt, tg = i % 2, i // 2
                act.activation(m.x1h[:, kt, 512 * tg:512 * tg + 512], m.ps[:, i % 4, :], ACT.Copy).then_inc(tr_h, 1)

        @blk.vector
        def _(v):
            for i in range(16):
                kt, tg = i % 2, i // 2
                v.wait_ge(tr_h, i + 1)
                v.tensor_tensor(m.x1l[:, kt, 512 * tg:512 * tg + 512], m.ps[:, i % 4, :],
                                m.x1h[:, kt, 512 * tg:512 * tg + 512].bitcast(F32), ALU.subtract).then_inc(tr_l, 1)


def split_plan():
    plan = [("q", mt, 512 * tb, 512) for mt in range(2) for tb in range(8)]
    plan += [("k", mt, 512 * tb, 512) for mt in range(2) for tb in range(8)]
    plan += [("c", mt, 2 * M * hb, 2 * M) for mt in range(2) for hb in range(2)]
    return plan


def phase_projections(nc, m, a):
    SLOTS = 4
    with ExitStack() as st:
        sb, sem = tensors(nc, st)
        w = sb("qkv_weights", [P, 2, 3 * D])
        wh = sb("qkv_high", [P, 2, 3 * D], F32R)
        wl = sb("qkv_low", [P, 2, 3 * D], F32R)
        c = sb("context_t", [P, 2, B * M])
        ch = sb("context_high", [P, 2, B * M], F32R)
        cl = sb("context_low", [P, 2, B * M], F32R)
        parts = sb("parts", [P, SLOTS, 3, 512], BF16)
        rest = sb("rest", [P, SLOTS, 512])
        vt = sb("v_tiles", [P, SLOTS, H, 32])
        ld = sem("weights_loaded")
        wsp = sem("weights_split")
        ones = sem("ones_ready")
        qk_mm = sem("qk_matmul_done")
        p1 = sem("part1_ready")
        r1 = sem("rest_ready")
        p2 = sem("part2_ready")
        p3 = sem("part3_ready")
        wr = [sem(f"parts_written_{i}") for i in range(SLOTS)]
        v_mm = sem("v_matmul_done")
        v_cp = sem("v_copied")
        v_wr = [sem(f"v_written_{i}") for i in range(SLOTS)]
        plan = split_plan()
        v_plan = [(b, t, P) for b in range(B) for t in range(CH)] + \
                 [(b, t, n) for b in range(B) for t, n in ((CH, P), (CH + 1, M - P))]
        done = [0] * SLOTS
        before = []
        for n, (kind, mt, c0, cols) in enumerate(plan):
            before.append(done[n % SLOTS])
            done[n % SLOTS] += 16 * (4 if kind == "c" else 2)
        blk = st.enter_context(nc.Block())

        @blk.sync
        def _(sp):
            sp.dma_start(w[:, :, 0:D], a["Wq"].rearrange("(k p) n -> p k n", p=P)).then_inc(ld, 16)
            sp.dma_start(w[:, :, D:3 * D], a["Wkv"].rearrange("(k p) n -> p k n", p=P)).then_inc(ld, 16)
            sp.dma_start(c[:, :, :], a["ctx_T"].rearrange("(k p) n -> p k n", p=P)).then_inc(ld, 16)
            for n, (kind, mt, c0, cols) in enumerate(plan):
                s = n % SLOTS
                sp.wait_ge(p3, n + 1)
                for hg in range(2):
                    rows = parts[64 * hg:64 * hg + 64, s, :, :]
                    dram = m.q_dram if kind == "q" else m.k_dram
                    if kind == "c":
                        for j in range(2):
                            b = c0 // M + j
                            sp.dma_start(dram[NG * b + 2 * mt + hg, :, :, L:KEYS],
                                         rows[:, :, M * j:M * j + M]).then_inc(wr[s], 16)
                    else:
                        b, l0 = c0 // L, c0 % L
                        sp.dma_start(dram[NG * b + 2 * mt + hg, :, :, l0:l0 + 512], rows).then_inc(wr[s], 16)
            for s in range(SLOTS):
                sp.wait_ge(wr[s], done[s])

        @blk.gpsimd
        def _(gp):
            gp.memset(vt[:, :, :, DH:32], 1.0).then_inc(ones, 1)
            for n, (kind, mt, c0, cols) in enumerate(plan):
                s = n % SLOTS
                gp.wait_ge(r1, n + 1)
                if before[n]:
                    gp.wait_ge(wr[s], before[n])
                gp.tensor_copy(parts[:, s, 1, 0:cols], rest[:, s, 0:cols]).then_inc(p2, 1)
                gp.wait_ge(p2, n + 1)
                gp.tensor_tensor(parts[:, s, 2, 0:cols], rest[:, s, 0:cols], parts[:, s, 1, 0:cols],
                                 ALU.subtract).then_inc(p3, 1)

        @blk.scalar
        def _(act):
            for n, (kind, mt, c0, cols) in enumerate(plan):
                s = n % SLOTS
                act.wait_ge(qk_mm, n + 1)
                if before[n]:
                    act.wait_ge(wr[s], before[n])
                act.activation(parts[:, s, 0, 0:cols], m.ps[:, s, 0:cols], ACT.Copy,
                               scale=DH ** -0.5 if kind == "q" else 1.0).then_inc(p1, 1)
            act.wait_ge(ones, 1)
            for n, (b, t, rows) in enumerate(v_plan):
                s = n % SLOTS
                act.wait_ge(v_mm, n + 1)
                if n >= SLOTS:
                    act.wait_ge(v_wr[s], 16 * (n // SLOTS))
                act.activation(vt[0:rows, s, :, 0:DH],
                               m.ps[0:rows, 4 + s, 0:D].rearrange("p (h d) -> p h d", h=H),
                               ACT.Copy).then_inc(v_cp, 1)
                act.wait_ge(v_cp, n + 1)
                act.dma_start(m.v_dram[NG * b:NG * b + NG, P * t:P * t + rows, :].rearrange("g p c -> p g c"),
                              vt[0:rows, s, :, :].rearrange("p (g h) c -> p g (h c)", g=NG)).then_inc(v_wr[s], 16)
            for s in range(SLOTS):
                act.wait_ge(v_wr[s], 16 * (len(v_plan) // SLOTS))

        @blk.vector
        def _(v):
            v.wait_ge(ld, 48)
            v.tensor_copy(wh[:, :, :], w[:, :, :]).then_inc(wsp, 1)
            v.tensor_copy(ch[:, :, :], c[:, :, :]).then_inc(wsp, 1)
            v.wait_ge(wsp, 2)
            v.tensor_tensor(wl[:, :, :], w[:, :, :], wh[:, :, :].bitcast(F32), ALU.subtract).then_inc(wsp, 1)
            v.tensor_tensor(cl[:, :, :], c[:, :, :], ch[:, :, :].bitcast(F32), ALU.subtract).then_inc(wsp, 1)
            for n, (kind, mt, c0, cols) in enumerate(plan):
                s = n % SLOTS
                v.wait_ge(p1, n + 1)
                if n >= SLOTS:
                    v.wait_ge(p3, n - SLOTS + 1)
                v.scalar_tensor_tensor(rest[:, s, 0:cols], m.ps[:, s, 0:cols], DH ** -0.5 if kind == "q" else 1.0,
                                       parts[:, s, 0, 0:cols], ALU.mult, ALU.subtract).then_inc(r1, 1)

        @blk.tensor
        def _(pe):
            pe.wait_ge(wsp, 4)
            for n, (kind, mt, c0, cols) in enumerate(plan):
                if n >= 4:
                    pe.wait_ge(r1, n - 3)
                w0 = (0 if kind == "q" else D) + P * mt
                xh, xl = (ch, cl) if kind == "c" else (m.x1h, m.x1l)
                for i, (kt, wt, xt) in enumerate((kt, wt, xt) for kt in range(2)
                                                 for wt, xt in ((wh, xl), (wl, xh), (wh, xh))):
                    mm = nc.tensor.matmul(m.ps[:, n % 4, 0:cols], wt[:, kt, w0:w0 + P], xt[:, kt, c0:c0 + cols],
                                          start=(i == 0), stop=(i == 5))
                mm.then_inc(qk_mm, 1)
            for n, (b, t, rows) in enumerate(v_plan):
                if n >= 4:
                    pe.wait_ge(v_cp, n - 3)
                if t < CH:
                    xh, xl, c0 = m.x1h, m.x1l, L * b + P * t
                else:
                    xh, xl, c0 = ch, cl, M * b + P * (t - CH)
                for i, (kt, wt, xt) in enumerate((kt, wt, xt) for kt in range(2)
                                                 for wt, xt in ((wh, xl), (wl, xh), (wh, xh))):
                    mm = nc.tensor.matmul(m.ps[0:rows, 4 + n % 4, 0:D], xt[:, kt, c0:c0 + rows],
                                          wt[:, kt, 2 * D:3 * D], start=(i == 0), stop=(i == 5))
                mm.then_inc(v_mm, 1)


def score_plan():
    steps = []
    for c in range(2):
        for kt in range(4 * (c + 1)):
            steps.append((c, kt, P, max(0, P * kt - 512 * c)))
        steps += [(c, CH, P, 0), (c, CH + 1, M - P, 0)]
    return steps


def max_plan():
    units = []
    for h in range(HG):
        for i in range(CH):
            xk = P * (i + 1)
            cut = [(0, min(xk, 512), xk <= 512)] + ([(512, xk - 512, True)] if xk > 512 else [])
            chunks = [[(0, k0, kn, dg)] for k0, kn, dg in cut]
            if chunks[-1][0][2] + M <= 512:
                chunks[-1].append((chunks[-1][0][2], L, M, False))
            else:
                chunks.append([(0, L, M, False)])
            units += [(h, i, c, pc) for c, pc in enumerate(chunks)]
    return units


TERMS = ((0, 0), (0, 1), (1, 0), (0, 2), (2, 0), (1, 1))
TR = 16 * len(TERMS)
MR = TR + 3


def phase_attention(nc, m, a):
    S = 3
    RP = 8
    AHEAD = 2
    ROT = 6
    UPS = 4
    with ExitStack() as st:
        sb, sem = tensors(nc, st)
        Q = [sb(f"q_rows_{s}", [MR, HG, L], BF16) for s in range(S)]
        K = [sb(f"k_rows_{s}", [MR, HG, KP], BF16) for s in range(S)]
        V = [sb(f"v_rows_{s}", [P, KT, HG * 32]) for s in range(S)]
        PR = sb("probabilities", [P, RP, 2, 512])
        OT = sb("out_transposed", [P, 2, 512])
        O = sb("out_heads", [P, 2, 4, HG, DH])
        rc = sb("denominator_inverse", [P, 4, HG])
        mxp = sb("max_partial", [P, HG * CH, 3])
        negm = sb("minus_max", [P, HG * CH])
        rst = sb("minus_max_rest", [P, HG * CH])
        M3 = sb("minus_max_parts", [P, 3, HG * CH], BF16)
        MT = sb("minus_max_rows", [3 * HG * CH, P], BF16)

        ini = sem("constants_ready")
        ld = [sem(f"step_loaded_{s}") for s in range(S)]
        mr = [sem(f"max_rows_loaded_{s}") for s in range(S)]
        nat = sem("max_scores_done")
        red = sem("max_bank_read")
        mx = sem("max_chain")
        t_mm = sem("small_transpose_done")
        mt_rd = sem("max_rows_ready")
        mw = sem("max_rows_written")
        s_mm = sem("score_pair_done")
        e_dn = sem("exp_pair_done")
        k_dn = sem("pair_masked")
        p_dn = sem("pv_step_done")
        o_cp = sem("pv_bank_read")
        r_dn = sem("inverse_ready")
        o_rd = sem("out_ready")
        turn = sem("waits_carried")
        o_wr = [sem(f"out_written_{c}") for c in range(2)]

        steps = score_plan()
        units = max_plan()
        NU, NSP = len(units), len(steps)
        NSC = 2 * NSP
        assert NU == UPS * NSP
        MAXED = NSP - ROT
        LOADS = 16 * 14
        diag = [si for si, (c, kt, rows, off) in enumerate(steps) if kt < CH and kt >= 4 * c]

        def units_at(si, more, more2):
            ahead, u = (1, UPS * (si + ROT)) if si < MAXED else (2, UPS * (si - MAXED))
            return [(ahead, u + k) for k in range(UPS)] if (more if ahead == 1 else more2) else []

        blk = st.enter_context(nc.Block())

        def loop(eng, body):
            body(0, 0, 0, True, True, True)
            with eng.Fori(0, (IT - 4) // S) as i:
                for j in range(S):
                    body(i * S + (j + 1), (j + 1) % S, i + (j + 1) // S, False, True, True)
            for n in range(IT - 3, IT):
                body(n, n % S, n // S, False, n < IT - 1, n < IT - 2)

        @blk.sync
        def _(sp):
            def load(n, s):
                for t, (pq, pk) in enumerate(TERMS):
                    sp.dma_start(Q[s][DH * t:DH * t + DH, :, :],
                                 m.q_dram[n, :, pq, :].rearrange("(h r) l -> r h l", r=DH)).then_inc(ld[s], 16)
                    sp.dma_start(K[s][DH * t:DH * t + DH, :, 0:KEYS],
                                 m.k_dram[n, :, pk, 0:KEYS].rearrange("(h r) l -> r h l", r=DH)).then_inc(ld[s], 16)
                sp.dma_start(V[s][:, 0:KT - 1, :],
                             m.v_dram[n, 0:P * (KT - 1), :].rearrange("(t p) c -> p t c", p=P)).then_inc(ld[s], 16)
                sp.dma_start(V[s][0:M - P, KT - 1, :],
                             m.v_dram[n, P * (KT - 1):P * (KT - 1) + M - P, :]).then_inc(ld[s], 16)

            def max_rows(n, s):
                sp.wait_ge(mt_rd, n + 1)
                sp.dma_start(m.max_dram[:, :], MT[:, :]).then_inc(mw, 16)
                sp.wait_ge(mw, n * 16 + 16)
                sp.dma_start(Q[s][TR:MR, :, :].rearrange("o h l -> o (h l)"),
                             m.max_dram.rearrange("(o k) p -> o (k p)", o=3)).then_inc(mr[s], 16)

            def store(n, c):
                sp.wait_ge(o_rd, 2 * n + (c + 2))
                sp.dma_start(m.o_dram[n, c, :, :, :],
                             O[:, c, :, :, :].rearrange("p q h d -> p q (h d)")).then_inc(o_wr[c], 16)

            def body(n, s, use, first, more, more2):
                if more2:
                    sp.wait_ge(p_dn, n * NSP + 4)
                    load(n + 2, (s + 2) % S)
                if not first:
                    store(n - 1, 1)
                store(n, 0)
                if more:
                    max_rows(n + 1, (s + 1) % S)

            for c in range(2):
                sp.sem_inc(o_wr[c], 16)
            load(0, 0)
            load(1, 1)
            max_rows(0, 0)
            loop(sp, body)
            store(IT - 1, 1)
            for c in range(2):
                sp.wait_ge(o_wr[c], 16 * IT + 16)

        @blk.gpsimd
        def _(gp):
            gp.memset(mxp[:, :, :], LOWEST).then_inc(ini, 1)

            def body(n, s, use, first, more, more2):
                for d, si in enumerate(diag):
                    c, kt, rows, off = steps[si]
                    for pr in range(2):
                        u = 2 * si + pr
                        gp.wait_ge(e_dn, n * NSC + u + 3)
                        gp.sem_inc(turn, 1)
                        blk_ = PR[:, u % RP, :, off:off + P]
                        gp.affine_select(out=blk_, in_=blk_, compare_op=ALU.is_ge, fill=0.0, base=0,
                                         pattern=[[0, 2], [1, P]], channel_multiplier=-1).then_inc(k_dn, 1)
            loop(gp, body)

        @blk.scalar
        def _(act):
            act.sem_inc(e_dn, 2)
            act.sem_inc(o_cp, 1)

            def out_copy(n, c):
                act.wait_ge(p_dn, n * NSP + ((6 if c == 0 else NSP) + 4))
                act.wait_ge(t_mm, n * 3 + (c + 1))
                act.activation(OT[:, c, :], m.ps[:, 6, :], ACT.Copy).then_inc(o_cp, 1)

            def body(n, s, use, first, more, more2):
                for si, (c, kt, rows, off) in enumerate(steps):
                    for pr in range(2):
                        u = 2 * si + pr
                        act.wait_ge(s_mm, n * NSC + (u + 1))
                        act.wait_ge(p_dn, n * NSP + (si + 1))
                        b0 = 2 + 2 * (u % 2)
                        act.activation(PR[0:rows, u % RP, :, off:512], m.ps[0:rows, b0:b0 + 2, off:512],
                                       ACT.Exp).then_inc(e_dn, 1)
                        if pr == 0 and si == 5 + AHEAD:
                            out_copy(n, 0)
                        if pr == 0 and si == AHEAD - 1 and not first:
                            out_copy(n - 1, 1)
            loop(act, body)
            out_copy(IT - 1, 1)

        @blk.vector
        def _(v):
            for s in range(S):
                v.memset(K[s][TR:MR, :, :], 1.0).then_inc(ini, 1)
            v.sem_inc(o_rd, 1)
            v.wait_ge(ini, 1 + S)

            def unit(n, u):
                h, i, c, pieces = units[u]
                v.wait_ge(nat, n * NU + u + 1)
                width = pieces[-1][0] + pieces[-1][2]
                j = CH * h + i
                v.tensor_reduce(mxp[:, j, c:c + 1], m.ps[:, u % 2, 0:width], AX_X, ALU.max).then_inc(red, 1)

            def maximum(n):
                v.wait_ge(red, (n + 1) * NU)
                v.tensor_reduce(negm[:, :], mxp[:, :, :], AX_X, ALU.max, negate=True).then_inc(mx, 1)
                v.wait_ge(mx, n * 5 + 1)
                v.tensor_copy(M3[:, 0, :], negm[:, :]).then_inc(mx, 1)
                v.wait_ge(mx, n * 5 + 2)
                v.tensor_tensor(rst[:, :], negm[:, :], M3[:, 0, :], ALU.subtract).then_inc(mx, 1)
                v.wait_ge(mx, n * 5 + 3)
                v.tensor_copy(M3[:, 1, :], rst[:, :]).then_inc(mx, 1)
                v.wait_ge(mx, n * 5 + 4)
                v.tensor_tensor(M3[:, 2, :], rst[:, :], M3[:, 1, :], ALU.subtract).then_inc(mx, 1)

            def max_rows(n, s, use, first=False):
                v.wait_ge(t_mm, 1 if first else n * 3)
                if not first:
                    ps_, pu = (s - 1) % S, use if s else use - 1
                    v.wait_ge(mr[ps_], (pu + 1) * 16)
                v.tensor_copy(MT[:, :], m.ps[0:3 * HG * CH, 7, 0:P // 2].bitcast(BF16)).then_inc(mt_rd, 1)

            def normalise(n, c, more=True):
                v.wait_ge(t_mm, n * 3 + (2 if c == 0 else 4 if more else 3))
                q = m.ps[:, 7, :].rearrange("p (q h e) -> p q h e", q=4, h=HG)
                v.wait_ge(o_rd, 2 * n + c + 1)
                v.reciprocal(rc[:, :, :], q[:, :, :, DH]).then_inc(r_dn, 1)
                v.wait_ge(r_dn, 2 * n + c + 1)
                v.wait_ge(o_wr[c], n * 16 + 16)
                v.tensor_tensor(O[:, c, :, :, :], q[:, :, :, 0:DH],
                                rc[:, :, :].unsqueeze(3).to_broadcast([P, 4, HG, DH]), ALU.mult).then_inc(o_rd, 1)

            for u in range(NU):
                unit(0, u)
            maximum(0)
            max_rows(0, 0, 0, first=True)
            for u in range(UPS * ROT):
                unit(1, u)

            def body(n, s, use, first, more, more2):
                for si in range(NSP):
                    for ahead, u in units_at(si, more, more2):
                        unit(n + ahead, u)
                    if si == 2 and not first:
                        normalise(n - 1, 1)
                    if si == 8:
                        normalise(n, 0)
                    if si == MAXED - 1 and more:
                        maximum(n + 1)
                    if si == MAXED and more:
                        max_rows(n + 1, (s + 1) % S, use + (s + 1) // S)
            loop(v, body)
            normalise(IT - 1, 1, more=False)

        @blk.tensor
        def _(pe):
            pe.sem_inc(p_dn, 4)

            def unit(n, u, s, first=False):
                h, i, c, pieces = units[u]
                if not first or u >= 2:
                    pe.wait_ge(red, n * NU + u - 1)
                bank = u % 2
                for col, k0, kn, masked in pieces:
                    mm = nc.tensor.matmul(m.ps[:, bank, col:col + kn], Q[s][0:TR, h, P * i:P * i + P],
                                          K[s][0:TR, h, k0:k0 + kn], start=True, stop=not masked)
                    if masked:
                        mm = nc.tensor.matmul(m.ps[:, bank, col + kn - P:col + kn], m.ident_bf[:, :],
                                              m.mask_bf[:, :], start=False, stop=True)
                mm.then_inc(nat, 1)

            def max_rows(n, first=False):
                pe.wait_ge(mx, n * 5 + 5)
                if not first:
                    pe.wait_ge(o_rd, 2 * n)
                nc.tensor.transpose(m.ps[0:3 * HG * CH, 7, 0:P // 2].bitcast(BF16),
                                    M3[:, :, :].rearrange("p a b -> p (a b)"), m.ident_bf[:, :]).then_inc(t_mm, 1)

            def out_rows(n, c, last=False):
                pe.wait_ge(o_cp, 2 * n + (c + 2))
                if c == 0:
                    pe.wait_ge(mt_rd, n + 1)
                    pe.wait_ge(o_rd, 2 * n + 1)
                elif last:
                    pe.wait_ge(o_rd, 2 * n + 2)
                else:
                    pe.wait_ge(mt_rd, n + 2)
                for q in range(4):
                    mm = nc.tensor.transpose(m.ps[:, 7, P * q:P * q + P], OT[:, c, P * q:P * q + P], m.ident[:, :])
                mm.then_inc(t_mm, 1)

            def scores(n, si, s, use, pr):
                c, kt, rows, off = steps[si]
                if si == 0 and pr == 0:
                    pe.wait_ge(mr[s], use * 16 + 16)
                u = 2 * si + pr
                pe.wait_ge(e_dn, n * NSC + (u + 1))
                b0 = 2 + 2 * (u % 2)
                for j in range(2):
                    mm = nc.tensor.matmul(m.ps[0:rows, b0 + j, off:512],
                                          K[s][:, 2 * pr + j, P * kt:P * kt + rows],
                                          Q[s][:, 2 * pr + j, 512 * c + off:512 * c + 512],
                                          start=True, stop=True)
                mm.then_inc(s_mm, 1)

            def pv(n, si, s):
                c, kt, rows, off = steps[si]
                pe.wait_ge(e_dn, n * NSC + 2 * si + 4)
                if si in diag:
                    pe.wait_ge(k_dn, n * 2 * len(diag) + 2 * diag.index(si) + 2)
                first = kt == 0
                last = kt == KT - 1
                if first:
                    pe.wait_ge(o_cp, 2 * n + c + 1)
                if rows < P:
                    pe.sem_inc(turn, 1)
                for h in range(HG):
                    mm = nc.tensor.matmul(m.ps[32 * h:32 * h + 32, 6, off:512], V[s][0:rows, kt, 32 * h:32 * h + 32],
                                          PR[0:rows, (2 * si + h // 2) % RP, h % 2, off:512],
                                          start=first, stop=last, tile_position=(0, 32 * h))
                mm.then_inc(p_dn, 1)

            pe.wait_ge(ini, 1 + S)
            pe.wait_ge(ld[0], LOADS)
            for u in range(NU):
                unit(0, u, 0, first=True)
            max_rows(0, first=True)
            pe.wait_ge(ld[1], LOADS)
            for u in range(UPS * ROT):
                unit(1, u, 1)
            for si in range(AHEAD):
                for pr in range(2):
                    scores(0, si, 0, 0, pr)

            def body(n, s, use, first, more, more2):
                def scores_ahead(si, pr):
                    if si + AHEAD < NSP:
                        scores(n, si + AHEAD, s, use, pr)
                    elif more:
                        scores(n + 1, si + AHEAD - NSP, (s + 1) % S, use + (s + 1) // S, pr)

                for si in range(NSP):
                    todo = units_at(si, more, more2)
                    if si == MAXED and more2:
                        pe.wait_ge(ld[(s + 2) % S], (use + (s + 2) // S) * LOADS + LOADS)
                    scores_ahead(si, 0)
                    for ahead, u in todo[:UPS // 2]:
                        unit(n + ahead, u, (s + ahead) % S)
                    scores_ahead(si, 1)
                    pv(n, si, s)
                    for ahead, u in todo[UPS // 2:]:
                        unit(n + ahead, u, (s + ahead) % S)
                    if si == 2 and not first:
                        out_rows(n - 1, 1)
                    if si == 8:
                        out_rows(n, 0)
                    if si == MAXED and more:
                        max_rows(n + 1)
            loop(pe, body)
            out_rows(IT - 1, 1, last=True)


def phase_output(nc, m, a):
    NB = NT // 4
    with ExitStack() as st:
        sb, sem = tensors(nc, st)
        w = sb("wout", [P, 2, D])
        wh = sb("wout_high", [P, 2, D], F32R)
        wl = sb("wout_low", [P, 2, D], F32R)
        o = sb("attention_out", [P, 2, 4, NG, HG * DH])
        oh = sb("attention_t_high", [P, 2, 2, 512], F32R)
        ol = sb("attention_t_low", [P, 2, 2, 512], F32R)
        xt = sb("x2_t", [P, 2, 2, 512])
        stats = sb("ln_stats_d", [P, NT, 6])
        mv = sb("ln_mean_var_d", [P, NT, 2])
        sd = sb("ln_sd_d", [P, NT])
        rs = sb("ln_rs_d", [P, NT])
        ld = sem("wout_loaded")
        wsp = sem("wout_split")
        o_ld = [sem(f"attention_out_loaded_{i}") for i in range(2)]
        xb = sem("x1_with_bias")
        tr = sem("attention_transposed")
        oh_r = sem("attention_high_ready")
        ol_r = sem("attention_low_ready")
        pj = sem("projected")
        z_r = sem("residual_sum_ready")
        bs = sem("ln_stats_ready_d")
        ba = sem("ln_variance_ready_d")
        sq = sem("ln_sd_ready_d")
        rr = sem("ln_rs_ready_d")
        x2r = sem("x2_ready")
        x_tr = sem("x2_transposed")
        x_cp = sem("x2_t_ready")
        x_wr = sem("x2_written")
        t_wr = [sem(f"x2_t_written_{i}") for i in range(2)]
        blk = st.enter_context(nc.Block())

        @blk.sync
        def _(sp):
            sp.dma_start(w[:, :, :], a["Wout"].rearrange("(k p) n -> p k n", p=P)).then_inc(ld, 16)

            def store(g):
                sp.wait_ge(x2r, 4 * g + 4)
                sp.dma_start(m.x2_dram[512 * g:512 * g + 512, :].rearrange("(t p) d -> p t d", p=P),
                             m.x1[:, 4 * g:4 * g + 4, :]).then_inc(x_wr, 16)
                sp.wait_ge(x_cp, 2 * g + 2)
                sp.dma_start(m.x2t_dram[:, 512 * g:512 * g + 512].rearrange("(k p) t -> p k t", p=P),
                             xt[:, g % 2, :, :]).then_inc(t_wr[g % 2], 16)
            for g in range(NB):
                b, c = g // 2, g % 2
                if g >= 2:
                    sp.wait_ge(tr, 2 * g - 2)
                for hg in range(NG):
                    sp.dma_start(o[:, g % 2, :, hg, :], m.o_dram[NG * b + hg, c, :, :, :]).then_inc(o_ld[g % 2], 16)
                if g >= 2:
                    store(g - 2)
            store(NB - 2)
            store(NB - 1)
            sp.wait_ge(x_wr, 16 * NB)
            for i in range(2):
                sp.wait_ge(t_wr[i], 16 * NB // 2)

        @blk.gpsimd
        def _(gp):
            for g in range(NB):
                v = m.x1[:, 4 * g:4 * g + 4, :]
                gp.tensor_tensor(v, v, m.bout[:, :].unsqueeze(1).to_broadcast([P, 4, D]), ALU.add).then_inc(xb, 1)

        @blk.scalar
        def _(act):
            def transposed_copy(g):
                for kt in range(2):
                    act.wait_ge(x_tr, 2 * g + kt + 1)
                    if g >= 2:
                        act.wait_ge(t_wr[g % 2], 16 * (g // 2))
                    act.activation(xt[:, g % 2, kt, :], m.ps[:, 6 + kt, :], ACT.Copy).then_inc(x_cp, 1)
            for g in range(NB):
                for kt in range(2):
                    act.wait_ge(tr, 2 * g + kt + 1)
                    if g >= 2:
                        act.wait_ge(pj, 2 * g - 2)
                    act.activation(oh[:, g % 2, kt, :], m.ps[:, kt, :], ACT.Copy).then_inc(oh_r, 1)
                if g >= 1:
                    transposed_copy(g - 1)
                act.wait_ge(ba, 4 * g + 4)
                act.activation(sd[:, 4 * g:4 * g + 4], mv[:, 4 * g:4 * g + 4, 1], ACT.Sqrt,
                               bias=m.eps[:, 0:1]).then_inc(sq, 1)
            transposed_copy(NB - 1)

        @blk.vector
        def _(v):
            v.wait_ge(ld, 16)
            v.tensor_copy(wh[:, :, :], w[:, :, :]).then_inc(wsp, 1)
            v.wait_ge(wsp, 1)
            v.tensor_tensor(wl[:, :, :], w[:, :, :], wh[:, :, :].bitcast(F32), ALU.subtract).then_inc(wsp, 1)
            for g in range(NB):
                for kt in range(2):
                    v.wait_ge(oh_r, 2 * g + kt + 1)
                    v.tensor_tensor(ol[:, g % 2, kt, :], m.ps[:, kt, :], oh[:, g % 2, kt, :].bitcast(F32),
                                    ALU.subtract).then_inc(ol_r, 1)
                v.wait_ge(xb, g + 1)
                for j in range(2):
                    z = m.x1[:, 4 * g + 2 * j:4 * g + 2 * j + 2, :]
                    v.wait_ge(pj, 2 * g + j + 1)
                    v.tensor_tensor(z, m.ps[:, 2 + 2 * (g % 2) + j, :].rearrange("p (t d) -> p t d", t=2), z,
                                    ALU.add).then_inc(z_r, 1)
                for t in range(4 * g, 4 * g + 4):
                    v.wait_ge(z_r, t // 2 + 1)
                    v.bn_stats(stats[:, t, :], m.x1[:, t, :]).then_inc(bs, 1)
                for t in range(4 * g, 4 * g + 4):
                    v.wait_ge(bs, t + 1)
                    v.bn_aggr(mv[:, t, :], stats[:, t, :]).then_inc(ba, 1)
                v.wait_ge(sq, g + 1)
                v.reciprocal(rs[:, 4 * g:4 * g + 4], sd[:, 4 * g:4 * g + 4]).then_inc(rr, 1)
                v.wait_ge(rr, g + 1)
                for t in range(4 * g, 4 * g + 4):
                    v.tensor_scalar(m.x1[:, t, :], m.x1[:, t, :], mv[:, t, 0:1], rs[:, t:t + 1], ALU.subtract,
                                    ALU.mult).then_inc(x2r, 1)

        @blk.tensor
        def _(pe):
            def in_transposes(g):
                pe.wait_ge(o_ld[g % 2], 64 * (g // 2 + 1))
                for kt in range(2):
                    if g >= 1:
                        pe.wait_ge(ol_r, 2 * g - 1 + kt)
                    for q in range(4):
                        mm = nc.tensor.transpose(
                            m.ps[:, kt, P * q:P * q + P],
                            o[:, g % 2, q, 2 * kt:2 * kt + 2, :].rearrange("p g d -> p (g d)"), m.ident[:, :])
                    mm.then_inc(tr, 1)

            def out_transposes(g):
                for kt in range(2):
                    if g >= 1:
                        pe.wait_ge(x_cp, 2 * g - 1 + kt)
                    pe.wait_ge(x2r, 4 * g + 4)
                    for q in range(4):
                        mm = nc.tensor.transpose(m.ps[:, 6 + kt, P * q:P * q + P],
                                                 m.x1[:, 4 * g + q, P * kt:P * kt + P], m.ident[:, :])
                    mm.then_inc(x_tr, 1)

            pe.wait_ge(wsp, 2)
            in_transposes(0)
            for g in range(NB):
                if g + 1 < NB:
                    in_transposes(g + 1)
                pe.wait_ge(ol_r, 2 * g + 2)
                for j in range(2):
                    if g >= 2:
                        pe.wait_ge(z_r, 2 * g - 3 + j)
                    for q in range(2 * j, 2 * j + 2):
                        for i, (kt, x, y) in enumerate((kt, x, y) for kt in range(2)
                                                       for x, y in ((ol, wh), (oh, wl), (oh, wh))):
                            mm = nc.tensor.matmul(m.ps[:, 2 + 2 * (g % 2) + j, D * (q % 2):D * (q % 2) + D],
                                                  x[:, g % 2, kt, P * q:P * q + P], y[:, kt, :],
                                                  start=(i == 0), stop=(i == 5))
                    mm.then_inc(pj, 1)
                if g >= 1:
                    out_transposes(g - 1)
            out_transposes(NB - 1)


def weight_stream(nc, m, st, tag, jobs, done):
    RING = 2
    sb, sem = tensors(nc, st)
    width = jobs[0][0].shape[1]
    stage = sb(f"weight_stage_{tag}", [P, RING, width])
    low_max = sb(f"low_max_{tag}", [P, len(jobs)])
    low_any = sb(f"low_any_{tag}", [P, 1])
    ones = sb(f"ones_{tag}", [P, 1])
    needed = sb(f"low_needed_{tag}", [1, 1], mybir.dt.int32)
    s_ld = [sem(f"weight_rows_loaded_{tag}_{i}") for i in range(RING)]
    s_hi = sem(f"weight_high_ready_{tag}")
    s_fl = sem(f"low_max_chain_{tag}")
    s_sum = sem(f"low_sum_done_{tag}")
    s_nd = sem(f"low_needed_ready_{tag}")

    def sync(sp):
        for n, (rows, hi, lo) in enumerate(jobs):
            if n >= RING:
                sp.wait_ge(done, n - RING + 1)
            sp.dma_start(stage[:, n % RING, 0:rows.shape[1]], rows).then_inc(s_ld[n % RING], 16)

    def low_maximum(v, n):
        v.wait_ge(done, n + 1)
        v.tensor_reduce(low_max[:, n:n + 1], jobs[n][2].bitcast(F32), AX_X, ALU.max,
                        apply_absolute_value=True).then_inc(s_fl, 1)

    def vector(v, first, last):
        if first == 0:
            v.memset(ones[:, :], 1.0).then_inc(s_fl, 1)
        for n in range(first, last):
            rows, hi, lo = jobs[n]
            v.wait_ge(s_ld[n % RING], 16 * (n // RING + 1))
            v.tensor_copy(hi, stage[:, n % RING, 0:rows.shape[1]]).then_inc(s_hi, 1)
            if n:
                low_maximum(v, n - 1)
        if last == len(jobs):
            low_maximum(v, last - 1)
            v.wait_ge(s_fl, len(jobs) + 1)
            v.tensor_reduce(low_any[:, :], low_max[:, :], AX_X, ALU.max).then_inc(s_fl, 1)
            v.wait_ge(s_fl, len(jobs) + 2)
            v.tensor_scalar(low_any[:, :], low_any[:, :], 0.0, None, ALU.is_gt).then_inc(s_fl, 1)

    def vector_needed(v):
        v.wait_ge(s_sum, 1)
        v.tensor_copy(needed[:, :], m.ps[0:1, 7, 0:1]).then_inc(s_nd, 1)

    def gpsimd(gp, first, last):
        for n in range(first, last):
            rows, hi, lo = jobs[n]
            gp.wait_ge(s_hi, n + 1)
            gp.tensor_tensor(lo, stage[:, n % RING, 0:rows.shape[1]], hi.bitcast(F32), ALU.subtract).then_inc(done, 1)

    def low_needed(pe):
        pe.wait_ge(s_fl, len(jobs) + 3)
        nc.tensor.matmul(m.ps[0:1, 7, 0:1], low_any[:, :], ones[:, :], start=True, stop=True).then_inc(s_sum, 1)
        pe.wait_ge(s_nd, 1)
        return pe.value_load(needed[0:1, 0:1], min_val=0, max_val=P)
    return sync, vector, vector_needed, gpsimd, low_needed


def passes(kts, high, low, with_low):
    return [(kt, wi, xx) for kt in kts for wi, xx in ((0, low),) + (((1, high),) if with_low else ()) + ((0, high),)]


def phase_ffn_first(nc, m, a):
    NB = 8
    with ExitStack() as st:
        sb, sem = tensors(nc, st)
        w1 = [sb(f"w1_{p}", [P, 2, F], F32R) for p in ("high", "low")]
        w2 = [sb(f"w2_{p}", [P, 2, F], F32R) for p in ("high", "low")]
        h1 = [sb(f"h1_{p}", [P, 8, F], F32R) for p in ("high", "low")]
        s1 = sb("w1_scale", [P, 8])
        s2 = sb("w2_scale", [P, 8])
        s3 = sb("h1_scale", [P, 8])
        x = sb("x2_block", [P, 2, 512])
        xh = sb("x2_high", [P, 2, 512], F32R)
        xl = sb("x2_low", [P, 2, 512], F32R)
        g = sb("silu_out", [P, 2, 512])
        h = sb("gated", [P, 2, 512])
        hh = sb("gated_high", [P, 2, 8, 512], F32R)
        hl = sb("gated_low", [P, 2, 8, 512], F32R)
        y = sb("gelu_out", [P, 4, 512])
        sc = sem("scales_loaded")
        w_dn = sem("weight_rows_split")
        x_ld = sem("x2_block_loaded")
        x_hi = sem("x2_high_ready")
        x_lo = sem("x2_low_ready")
        u_mm = sem("up_pair_done")
        g_r = sem("silu_ready")
        h_r = sem("gated_ready")
        hh_r = sem("gated_high_ready")
        hl_r = sem("gated_low_ready")
        y_mm = sem("hidden_tile_done")
        y_r = sem("gelu_ready")
        y_wr = [sem(f"gelu_written_{i}") for i in range(4)]
        jobs = []
        for name, w in (("w1_T", w1), ("w2_T", w2), ("h1_T", h1)):
            for k in range(a[name].shape[0] // P):
                jobs.append((a[name][P * k:P * k + P, :], w[0][:, k, :], w[1][:, k, :]))
        w_sync, w_vec, w_flag, w_pool, low_needed = weight_stream(nc, m, st, "a", jobs, w_dn)
        hd = m.h_dram.rearrange("(k p) (b t) -> b k p t", p=P, t=512)
        blk = st.enter_context(nc.Block())

        def block_loop(eng, up, down, after_first=None):
            up(0, 0)
            if after_first:
                after_first(eng)
            with eng.Fori(0, NB // 2 - 1) as i:
                for p in range(2):
                    up(i * 2 + (p + 1), (p + 1) % 2)
                    down(i * 2 + p, p)
            up(NB - 1, 1)
            down(NB - 2, 0)
            down(NB - 1, 1)

        @blk.sync
        def _(sp):
            for t, n in ((s1, "w1_s"), (s2, "w2_s"), (s3, "h1_s")):
                sp.dma_start(t[:, :], a[n]).then_inc(sc, 16)
            sp.dma_start(x[:, :, :], m.x2t_dram[:, 0:512].rearrange("(k p) t -> p k t", p=P)).then_inc(x_ld, 16)
            w_sync(sp)
            x2t = m.x2t_dram.rearrange("(k p) (b t) -> b p k t", p=P, t=512)
            with sp.Fori(1, NB) as t:
                sp.wait_ge(x_lo, t)
                sp.dma_start(x[:, :, :], x2t[t, :, :, :]).then_inc(x_ld, 16)

        @blk.gpsimd
        def _(gp):
            gp.sem_inc(hl_r, 2)
            w_pool(gp, 0, 4)

            def up(t, p):
                for mt in range(8):
                    gp.wait_ge(hh_r, t * 8 + (mt + 1))
                    gp.tensor_tensor(hl[:, p, mt, :], h[:, mt % 2, :], hh[:, p, mt, :].bitcast(F32),
                                     ALU.subtract).then_inc(hl_r, 1)
                    if isinstance(t, int) and t == 0:
                        w_pool(gp, 4 + mt, 5 + mt)
            block_loop(gp, up, lambda t, p: None)

        @blk.scalar
        def _(act):
            act.sem_inc(y_r, 4)
            for s in range(4):
                act.sem_inc(y_wr[s], 16)
            act.wait_ge(sc, 48)

            def up(t, p):
                act.wait_ge(x_ld, t * 16 + 16)
                act.wait_ge(u_mm, t * 8)
                act.activation(xh[:, :, :], x[:, :, :], ACT.Copy).then_inc(x_hi, 1)

                def high(mt):
                    act.wait_ge(h_r, t * 8 + (mt + 3))
                    act.activation(hh[:, p, mt, :], h[:, mt % 2, :], ACT.Copy).then_inc(hh_r, 1)
                for mt in range(8):
                    act.wait_ge(u_mm, t * 8 + (mt + 1))
                    act.wait_ge(h_r, t * 8 + (mt + 1))
                    act.activation(g[:, mt % 2, :], m.ps[:, 2 * (mt % 2), :], ACT.Silu,
                                   scale=s1[:, mt:mt + 1]).then_inc(g_r, 1)
                    if mt:
                        high(mt - 1)
                high(7)

            def down(t, p):
                for mt in range(8):
                    s = mt % 4
                    act.wait_ge(y_mm, t * 8 + (mt + 1))
                    act.wait_ge(y_wr[s], t * 32 + 16 * (mt // 4 + 1))
                    act.activation(y[:, s, :], m.ps[:, 4 + s, :], ACT.Gelu, scale=s3[:, mt:mt + 1]).then_inc(y_r, 1)
                    act.wait_ge(y_r, t * 8 + (mt + 5))
                    act.dma_start(hd[t, mt, :, :], y[:, s, :]).then_inc(y_wr[s], 16)
            block_loop(act, up, down)
            for s in range(4):
                act.wait_ge(y_wr[s], NB * 32 + 16)

        @blk.vector
        def _(v):
            v.sem_inc(h_r, 2)
            w_vec(v, 0, 4)
            v.wait_ge(sc, 48)

            def up(t, p):
                v.wait_ge(x_hi, t + 1)
                v.tensor_tensor(xl[:, :, :], x[:, :, :], xh[:, :, :].bitcast(F32), ALU.subtract).then_inc(x_lo, 1)
                for mt in range(8):
                    v.wait_ge(g_r, t * 8 + (mt + 1))
                    v.wait_ge(hl_r, t * 8 + (mt + 1))
                    v.scalar_tensor_tensor(h[:, mt % 2, :], m.ps[:, 2 * (mt % 2) + 1, :], s2[:, mt:mt + 1],
                                           g[:, mt % 2, :], ALU.mult, ALU.mult).then_inc(h_r, 1)
                    if isinstance(t, int) and t == 0:
                        w_vec(v, 4 + mt, 5 + mt)
            block_loop(v, up, lambda t, p: None, w_flag)

        @blk.tensor
        def _(pe):
            def up(t, p, with_low):
                pe.wait_ge(x_lo, t + 1)
                for mt in range(8):
                    pe.wait_ge(h_r, t * 8 + (mt + 1))
                    todo = passes(range(2), xh, xl, with_low)
                    for j, w in enumerate((w1, w2)):
                        for i, (kt, wi, xx) in enumerate(todo):
                            mm = nc.tensor.matmul(m.ps[:, 2 * (mt % 2) + j, :], w[wi][:, kt, P * mt:P * mt + P],
                                                  xx[:, kt, :], start=(i == 0), stop=(i == len(todo) - 1))
                    mm.then_inc(u_mm, 1)

            def down(t, p, with_low):
                pe.wait_ge(hl_r, t * 8 + 10)
                todo = passes(range(8), hh, hl, with_low)
                for mt in range(8):
                    pe.wait_ge(y_r, t * 8 + (mt + 1))
                    for i, (kt, wi, xx) in enumerate(todo):
                        mm = nc.tensor.matmul(m.ps[:, 4 + mt % 4, :], h1[wi][:, kt, P * mt:P * mt + P],
                                              xx[:, p, kt, :], start=(i == 0), stop=(i == len(todo) - 1))
                    mm.then_inc(y_mm, 1)

            def later(with_low):
                with pe.Fori(0, NB // 2 - 1) as i:
                    for p in range(2):
                        up(i * 2 + (p + 1), (p + 1) % 2, with_low)
                        down(i * 2 + p, p, with_low)
                up(NB - 1, 1, with_low)
                down(NB - 2, 0, with_low)
                down(NB - 1, 1, with_low)

            pe.wait_ge(w_dn, 4)
            up(0, 0, True)
            needed = low_needed(pe)
            with pe.If(needed > 0):
                later(True)
            with pe.Else():
                later(False)


def phase_ffn_second(nc, m, a, out):
    NB = 8
    with ExitStack() as st:
        sb, sem = tensors(nc, st)
        h2 = [sb(f"h2_{p}", [P, 8, F], F32R) for p in ("high", "low")]
        w3 = [sb(f"w3_{p}", [P, 8, D], F32R) for p in ("high", "low")]
        s4 = sb("h2_scale", [P, 8])
        s5 = sb("w3_scale", [P, D])
        hs = sb("hidden_rows", [P, 4, 512])
        hh = sb("hidden_high", [P, 2, 8, 512], F32R)
        hl = sb("hidden_low", [P, 2, 8, 512], F32R)
        g = sb("gelu2_out", [P, 2, 512])
        gh = sb("gelu2_high", [P, 8, 512], F32R)
        gl = sb("gelu2_low", [P, 8, 512], F32R)
        z = sb("sum", [P, 4, D])
        x2 = sb("x2_tiles", [P, 4, D])
        stats = sb("ln_stats_e", [P, 4, 6])
        mv = sb("ln_mean_var_e", [P, 4, 2])
        sd = sb("ln_sd_e", [P, 4])
        rs = sb("ln_rs_e", [P, 4])
        sc = sem("scales_loaded_e")
        w_dn = sem("weight_rows_split_e")
        r_ld = [sem(f"hidden_row_loaded_{i}") for i in range(4)]
        hh_r = sem("hidden_high_ready")
        hl_r = sem("hidden_low_ready")
        y_mm = sem("hidden2_tile_done")
        g_r = sem("gelu2_ready")
        gh_r = sem("gelu2_high_ready")
        gl_r = sem("gelu2_low_ready")
        o_mm = sem("w3_block_done")
        x_ld = sem("x2_tiles_loaded")
        z_m = sem("scaled_ready")
        z_a = sem("sum_ready")
        bs = sem("ln_stats_ready_e")
        ba = sem("ln_variance_ready_e")
        sq = sem("ln_sd_ready_e")
        rr = sem("ln_rs_ready_e")
        o_r = sem("out_tiles_ready")
        turn = sem("waits_carried_e")
        o_wr = sem("out_written")
        jobs = []
        for name, w in (("h2_T", h2), ("w3_T", w3)):
            for k in range(8):
                jobs.append((a[name][P * k:P * k + P, :], w[0][:, k, :], w[1][:, k, :]))
        w_sync, w_vec, w_flag, w_pool, low_needed = weight_stream(nc, m, st, "b", jobs, w_dn)
        hd = m.h_dram.rearrange("(k p) (b t) -> b k p t", p=P, t=512)
        x2d = m.x2_dram.rearrange("(b t p) d -> b p t d", p=P, t=4)
        od = out.rearrange("(b t p) d -> b p t d", p=P, t=4)
        blk = st.enter_context(nc.Block())

        def block_loop(eng, body):
            with eng.Fori(0, NB // 2 - 1) as i:
                for p in range(2):
                    body(i * 2 + p, p, True)
            body(NB - 2, 0, True)
            body(NB - 1, 1, False)

        @blk.sync
        def _(sp):
            sp.sem_inc(o_wr, 16)
            sp.dma_start(s4[:, :], a["h2_s"]).then_inc(sc, 16)
            sp.dma_start(s5[:, :], a["w3_s"].partition_broadcast(P)).then_inc(sc, 16)

            def rows(t):
                for k in range(8):
                    sp.wait_ge(hl_r, t * 8 + (k + 1))
                    sp.dma_start(hs[:, k % 4, :], hd[t, k, :, :]).then_inc(r_ld[k % 4], 16)
            rows(0)
            w_sync(sp)

            def body(t, p, more):
                sp.wait_ge(z_a, t + 1)
                sp.dma_start(x2[:, :, :], x2d[t, :, :, :]).then_inc(x_ld, 16)
                if more:
                    rows(t + 1)
                sp.wait_ge(o_r, t * 4 + 4)
                sp.dma_start(od[t, :, :, :], z[:, :, :]).then_inc(o_wr, 16)
            block_loop(sp, body)
            sp.wait_ge(o_wr, 16 * NB + 16)

        @blk.gpsimd
        def _(gp):
            gp.sem_inc(gl_r, 2)
            gp.sem_inc(z_a, 1)
            w_pool(gp, 0, len(jobs))

            def body(t, p, more):
                for mt in range(8):
                    gp.wait_ge(gh_r, t * 8 + (mt + 1))
                    gp.tensor_tensor(gl[:, mt, :], g[:, mt % 2, :], gh[:, mt, :].bitcast(F32),
                                     ALU.subtract).then_inc(gl_r, 1)
                gp.wait_ge(x_ld, t * 16 + 16)
                gp.wait_ge(z_m, t * 4 + 8)
                gp.tensor_tensor(z[:, :, :], z[:, :, :], x2[:, :, :], ALU.add).then_inc(z_a, 1)
            block_loop(gp, body)

        @blk.scalar
        def _(act):
            act.sem_inc(g_r, 4)

            def high(t, p, k):
                act.wait_ge(r_ld[k % 4], t * 32 + 16 * (k // 4 + 1))
                act.activation(hh[:, p, k, :], hs[:, k % 4, :], ACT.Copy).then_inc(hh_r, 1)
            for k in range(8):
                high(0, 0, k)
            act.wait_ge(sc, 32)

            def body(t, p, more):
                for mt in range(8):
                    act.wait_ge(y_mm, t * 8 + (mt + 1))
                    act.wait_ge(gl_r, t * 8 + (mt + 1))
                    act.activation(g[:, mt % 2, :], m.ps[:, mt % 4, :], ACT.Gelu, scale=s4[:, mt:mt + 1]).then_inc(g_r, 1)
                    if more:
                        high(t + 1, 1 - p, mt)
                act.wait_ge(ba, t * 4 + 4)
                act.activation(sd[:, :], mv[:, :, 1], ACT.Sqrt, bias=m.eps[:, 0:1]).then_inc(sq, 1)
            block_loop(act, body)

        @blk.vector
        def _(v):
            v.sem_inc(hl_r, 4)
            v.sem_inc(z_m, 4)

            def low(t, p, k):
                v.wait_ge(hh_r, t * 8 + (k + 1))
                v.tensor_tensor(hl[:, p, k, :], hs[:, k % 4, :], hh[:, p, k, :].bitcast(F32),
                                ALU.subtract).then_inc(hl_r, 1)
            for k in range(8):
                low(0, 0, k)
            w_vec(v, 0, len(jobs))
            w_flag(v)
            v.wait_ge(sc, 32)

            def body(t, p, more):
                for mt in range(8):
                    v.wait_ge(g_r, t * 8 + (mt + 5))
                    v.tensor_copy(gh[:, mt, :], g[:, mt % 2, :]).then_inc(gh_r, 1)
                    if more:
                        low(t + 1, 1 - p, mt)
                v.wait_ge(o_mm, t + 1)
                v.wait_ge(o_wr, t * 16 + 16)
                for q in range(4):
                    v.tensor_tensor(z[:, q, :], m.ps[:, 4 + q, 0:D], s5[:, :], ALU.mult).then_inc(z_m, 1)
                v.wait_ge(z_a, t + 2)
                for q in range(4):
                    v.bn_stats(stats[:, q, :], z[:, q, :]).then_inc(bs, 1)
                v.wait_ge(bs, t * 4 + 4)
                v.sem_inc(turn, 1)
                for q in range(4):
                    v.bn_aggr(mv[:, q, :], stats[:, q, :]).then_inc(ba, 1)
                v.wait_ge(sq, t + 1)
                v.reciprocal(rs[:, :], sd[:, :]).then_inc(rr, 1)
                v.wait_ge(rr, t + 1)
                for q in range(4):
                    v.tensor_scalar(z[:, q, :], z[:, q, :], mv[:, q, 0:1], rs[:, q:q + 1], ALU.subtract,
                                    ALU.mult).then_inc(o_r, 1)
            block_loop(v, body)

        @blk.tensor
        def _(pe):
            def blocks(with_low):
                def body(t, p, more):
                    pe.wait_ge(hl_r, t * 8 + 12)
                    todo = passes(range(8), hh, hl, with_low)
                    for mt in range(8):
                        pe.wait_ge(g_r, t * 8 + (mt + 1))
                        for i, (kt, wi, xx) in enumerate(todo):
                            mm = nc.tensor.matmul(m.ps[:, mt % 4, :], h2[wi][:, kt, P * mt:P * mt + P],
                                                  xx[:, p, kt, :], start=(i == 0), stop=(i == len(todo) - 1))
                        mm.then_inc(y_mm, 1)
                    pe.wait_ge(z_m, t * 4 + 4)
                    for kt in range(8):
                        pe.wait_ge(gl_r, t * 8 + (kt + 3))
                        todo = passes([kt], gh, gl, with_low)
                        for q in range(4):
                            for i, (_, wi, xx) in enumerate(todo):
                                mm = nc.tensor.matmul(m.ps[:, 4 + q, 0:D], xx[:, kt, P * q:P * q + P],
                                                      w3[wi][:, kt, :], start=(kt == 0 and i == 0),
                                                      stop=(kt == 7 and i == len(todo) - 1))
                    mm.then_inc(o_mm, 1)
                block_loop(pe, body)

            needed = low_needed(pe)
            with pe.If(needed > 0):
                blocks(True)
            with pe.Else():
                blocks(False)


def build(nc, a, out):
    m = Mem()
    with ExitStack() as st:
        def sb(name, shape, dtype=F32):
            return st.enter_context(nc.sbuf_tensor(name, shape, dtype))
        m.ps = st.enter_context(nc.psum_tensor("psum", [P, 8, 512], F32))
        m.ident = sb("ident", [P, P])
        m.ident_bf = sb("ident_bf", [P, P], BF16)
        m.mask_bf = sb("causal_mask", [P, P], BF16)
        m.eps = sb("eps", [P, 1])
        m.kpad_dram = nc.dram_tensor("kpad_scratch", [D, 256], F32).ap()
        m.q_dram = nc.dram_tensor("q_scratch", [IT, HG * DH, 3, L], BF16).ap()
        m.k_dram = nc.dram_tensor("k_scratch", [IT, HG * DH, 3, KP], BF16).ap()
        m.v_dram = nc.dram_tensor("v_scratch", [IT, KT * P, HG * 32], F32).ap()
        m.o_dram = nc.dram_tensor("o_scratch", [IT, 2, P, 4, HG * DH], F32).ap()
        m.max_dram = nc.dram_tensor("max_scratch", [3 * HG * CH, P], BF16).ap()
        m.x2t_dram = nc.dram_tensor("x2t_scratch", [D, B * L], F32).ap()
        m.x2_dram = nc.dram_tensor("x2_scratch", [B * L, D], F32).ap()
        m.h_dram = nc.dram_tensor("h_scratch", [F, B * L], F32).ap()
        with ExitStack() as st1:
            m.bout = st1.enter_context(nc.sbuf_tensor("bout", [P, D], F32))
            m.x1 = st1.enter_context(nc.sbuf_tensor("x1", [P, NT, D], F32))
            phase_convolution(nc, m, a)
            with ExitStack() as st2:
                m.x1h = st2.enter_context(nc.sbuf_tensor("x1t_high", [P, 2, B * L], F32R))
                m.x1l = st2.enter_context(nc.sbuf_tensor("x1t_low", [P, 2, B * L], F32R))
                phase_transpose(nc, m)
                phase_projections(nc, m, a)
            phase_attention(nc, m, a)
            phase_output(nc, m, a)
        phase_ffn_first(nc, m, a)
        phase_ffn_second(nc, m, a, out)


def kernel(**inputs):
    import concourse.bacc as _bacc
    from concourse.bass_utils import run_bass_kernel_spmd as _run

    g = {k: np.asarray(v) for k, v in inputs.items()}
    x = g["x"].reshape(B * L, D)
    laid = {
        "x": x,
        "x_rev": x.reshape(NT, P, D)[:, ::-1].reshape(B * L, D),
        "ctx_T": g["ctx_1024"].reshape(B * M, D).T,
        "A_log": g["L0_attn_A_log"],
        "C_T": g["L0_attn_C"].T,
        "delta": g["L0_attn_delta"],
        "freq_align": g["L0_attn_freq_align"],
        "fa_cols": g["L0_attn_freq_align"].reshape(2, P).T,
        "d_cols": g["L0_attn_D"].reshape(2, P).T,
        "reward": g["L0_attn_reward"],
        "gamma": g["L0_attn_gamma"],
        "beta": g["L0_attn_beta"],
        "Wq": g["L0_xattn_Wq"],
        "Wkv": g["L0_xattn_Wkv"],
        "Wout": g["L0_xattn_Wout"],
        "bout": g["L0_xattn_bout"],
    }
    for n in ("w1", "w2", "h1", "h2", "w3"):
        laid[n + "_T"] = g[f"L0_ffn_{n}_w"].T
    for n in ("w1", "w2", "h1", "h2"):
        laid[n + "_s"] = g[f"L0_ffn_{n}_s"].reshape(8, P).T
    laid["w3_s"] = g["L0_ffn_w3_s"]

    nc = _bacc.Bacc("TRN2", target_bir_lowering=False, num_devices=1)
    arrays, aps = {}, {}
    for name, v in laid.items():
        v = np.ascontiguousarray(v)
        arrays[f"in_{name}"] = v
        aps[name] = nc.dram_tensor(f"in_{name}", v.shape, mybir.dt.from_np(v.dtype), kind="ExternalInput").ap()
    out = nc.dram_tensor("out", (B * L, D), F32, kind="ExternalOutput").ap()
    build(nc, aps, out)
    r = _run(nc, [arrays], core_ids=[0])
    return r.results[0]["out"].reshape(B, L, D)
```

```python
import numpy as np
from contextlib import ExitStack

import concourse.bass as bass
from concourse import mybir

ALU = mybir.AluOpType
ACT = mybir.ActivationFunctionType
AX_X = mybir.AxisListType.X
F32 = mybir.dt.float32
F32R = mybir.dt.float32r
BF16 = mybir.dt.bfloat16

P = 128
B, L, D = 4, 1024, 256
NT = B * L // P
CH = L // P
NS = 64
M = 154
H, DH = 16, 16
HG = 4
NG = H // HG
IT = B * NG
KEYS = L + M
KP = 1184
KT = 10
F = 1024
EPS = 1e-5
NEG = -1.0e30
LOWEST = -3.0e38


ARENA = 24 * F


class Mem:
    pass


def arena(nc, m, name, first, shape, dtype=F32):
    return nc.alloc_sbuf_tensor_at(name, [P] + shape, dtype, offset=m.arena_base + 4 * first)


def arena_split(nc, m, name, first, first_low, shape):
    return (arena(nc, m, name + "_high", first, shape, F32R), arena(nc, m, name + "_low", first_low, shape, F32R),
            arena(nc, m, name + "_raw", first_low, shape))


def own_split(nc, sb, name, shape):
    high = sb(name + "_high", [P] + shape, F32R)
    offset = aligned(nc.sbuf_base)
    low = sb(name + "_low", [P] + shape, F32R)
    return high, low, nc.alloc_sbuf_tensor_at(name + "_raw", [P] + shape, F32, offset=offset)


def aligned(address):
    return -(-address // 32) * 32


def tensors(nc, stack):
    def sb(name, shape, dtype=F32):
        return stack.enter_context(nc.sbuf_tensor(name, shape, dtype))

    def sem(name):
        return stack.enter_context(nc.semaphore(name))
    return sb, sem


def phase_convolution(nc, m, a):
    GR = 8
    NGR = D // GR
    RING = 4
    with ExitStack() as st:
        sb, sem = tensors(nc, st)
        U = arena(nc, m, "x_reversed", 0, [NT, D])
        Y = arena(nc, m, "conv_out", NT * D, [NT, D])
        TZ = arena(nc, m, "toeplitz", 2 * NT * D, [RING, GR // 2, 3 * P])
        HS = sb("states", [NS, 2, B, D])
        CHs = sb("states_times_c", [NS, CH - 1, B, D])
        kpad = sb("k_padded", [P, 2, 256])
        alog_col = sb("alog_col", [NS, 1])
        alog_row = sb("alog_row", [P, NS])
        delta0 = sb("delta0", [P, 1])
        ct = sb("c_transposed", [NS, D])
        fa_row = sb("freq_align_row", [NS, D])
        fa_col = sb("freq_align_col", [P, 2])
        d_col = sb("d_col", [P, 2])
        rew = sb("reward", [1, D])
        gam = sb("gamma", [P, D])
        bet = sb("beta", [P, D])
        e_col = sb("exp_alog_col", [NS, 1])
        z_col = sb("z_col", [NS, 1])
        e_row = sb("exp_alog_row", [P, NS])
        z_row = sb("z_row", [P, NS])
        l_row = sb("l_row", [NS, P + 1])
        p1_col = sb("p_plus_1", [P, 1])
        pw = sb("powers", [NS, P + 1])
        prev = sb("powers_to_chunk_end", [P, NS])
        cta = sb("c_times_fa", [NS, D])
        dfa = sb("d_times_fa", [P, 2])
        by_tile = sb("conv_by_tile", [P, 2, GR // 4, P])
        stats = sb("ln_stats", [P, NT, 4, 6])
        stats2 = sb("ln_stats_2", [P, NT, 6])
        mv = sb("ln_mean_var", [P, 2, NT, 2])
        sd = sb("ln_sd", [P, 2, NT])
        rs = sb("ln_rs", [P, 2, NT])
        shift = sb("ln_minus_mean_rs", [P, 2, NT])

        par = sem("params_loaded")
        u_ld = sem("x_reversed_loaded")
        x_ld = [sem(f"x_loaded_{h}") for h in range(2)]
        io = sem("iota_ready")
        a_dn = sem("act_done")
        v_dn = sem("dve_done")
        k_mm = sem("k_matmul_done")
        k_rd = sem("k_padded_ready")
        k_wr = sem("k_written")
        t_ld = [sem(f"toeplitz_loaded_{i}") for i in range(RING)]
        t_us = sem("toeplitz_group_done")
        g_mm = sem("chunk_sum_matmul_done")
        g_rd = sem("state_updated")
        c_rd = sem("states_times_c_ready")
        y_mm = sem("carry_matmul_done")
        y_cp = sem("bank_copied")
        t_ev = sem("toeplitz_bank_read")
        st_rd = [sem(f"ln_stats_ready_{r}") for r in range(2)]
        ln_v = [sem(f"ln_variance_ready_{r}") for r in range(2)]
        ln_s = [sem(f"ln_sd_ready_{r}") for r in range(2)]
        rs_rd = [sem(f"ln_scale_and_shift_{r}") for r in range(2)]
        n_rd = sem("normalised_ready")
        xb_rd = sem("x_with_beta_ready")
        g_rd2 = sem("times_gamma_ready")
        n_gb = sem("residual_sum_ready")
        pool = sem("pool_step")
        x1_rd = sem("x1_ready")
        tr = sem("transposes_done")
        tr_h = sem("high_part_ready")
        tr_l = sem("low_part_ready")
        blk = st.enter_context(nc.Block())
        Yv = Y[:, :, :].rearrange("p (b c) d -> p b c d", b=B)
        Uv = U[:, :, :].rearrange("p (b c) d -> p b c d", b=B)
        PARAMS = 11
        FIRST_LN = ((0, 8), (8, NT))

        @blk.sync
        def _(sp):
            sp.dma_start(alog_col[:, :], a["A_log"].rearrange("(n a) -> n a", a=1)).then_inc(par, 16)
            sp.dma_start(alog_row[:, :], a["A_log"].partition_broadcast(P)).then_inc(par, 16)
            sp.dma_start(delta0[:, :], a["delta"][0:1].partition_broadcast(P)).then_inc(par, 16)
            sp.dma_start(ct[:, :], a["C_T"]).then_inc(par, 16)
            sp.dma_start(fa_row[:, :], a["freq_align"].partition_broadcast(NS)).then_inc(par, 16)
            sp.dma_start(fa_col[:, :], a["fa_cols"]).then_inc(par, 16)
            sp.dma_start(d_col[:, :], a["d_cols"]).then_inc(par, 16)
            sp.dma_start(rew[:, :], a["reward"].partition_broadcast(1)).then_inc(par, 16)
            sp.dma_start(gam[:, :], a["gamma"].partition_broadcast(P)).then_inc(par, 16)
            sp.dma_start(bet[:, :], a["beta"].partition_broadcast(P)).then_inc(par, 16)
            sp.dma_start(m.bout[:, :], a["bout"].partition_broadcast(P)).then_inc(par, 16)
            sp.wait_ge(k_rd, 1)
            sp.dma_start(m.kpad_dram.rearrange("(m p) l -> p m l", p=P), kpad[:, :, :]).then_inc(k_wr, 16)
            sp.wait_ge(k_wr, 16)
            for g in range(NGR):
                if g == RING:
                    for h in range(2):
                        sp.dma_start(m.x1[:, 16 * h:16 * h + 16, :],
                                     a["x"][2048 * h:2048 * h + 2048, :].rearrange("(t p) d -> p t d", p=P)).then_inc(x_ld[h], 16)
                if g >= RING:
                    sp.wait_ge(t_us, g - RING + 1)
                src = bass.AP(m.kpad_dram.tensor, g * GR * 256, [[1, P], [512, GR // 2], [1, 3 * P]])
                sp.dma_start(TZ[:, g % RING, :, :], src).then_inc(t_ld[g % RING], 16)

        @blk.gpsimd
        def _(gp):
            gp.iota(l_row[:, :], [[1, P + 1]], base=0, channel_multiplier=0,
                    allow_small_or_imprecise_dtypes=True).then_inc(io, 1)
            gp.iota(p1_col[:, :], [[0, 1]], base=1, channel_multiplier=1,
                    allow_small_or_imprecise_dtypes=True).then_inc(io, 1)
            gp.memset(kpad[:, :, :], 0.0).then_inc(io, 1)
            gp.memset(Yv[:, :, 0, :], 0.0).then_inc(io, 1)
            gp.memset(m.ident[:, :], 0.0).then_inc(pool, 1)
            gp.memset(m.ident_bf[:, :], 0.0).then_inc(pool, 1)
            gp.memset(m.mask_bf[:, :], 0.0).then_inc(pool, 1)
            gp.memset(m.eps[:, :], EPS).then_inc(pool, 1)
            gp.wait_ge(pool, 4)
            gp.affine_select(out=m.ident[:, :], in_=m.ident[:, :], compare_op=ALU.not_equal, fill=1.0,
                             base=0, pattern=[[-1, P]], channel_multiplier=1).then_inc(pool, 1)
            gp.affine_select(out=m.ident_bf[:, :], in_=m.ident_bf[:, :], compare_op=ALU.not_equal, fill=1.0,
                             base=0, pattern=[[-1, P]], channel_multiplier=1).then_inc(pool, 1)
            gp.affine_select(out=m.mask_bf[:, :], in_=m.mask_bf[:, :], compare_op=ALU.is_ge, fill=NEG,
                             base=0, pattern=[[-1, P]], channel_multiplier=1).then_inc(pool, 1)
            gp.wait_ge(par, 16 * PARAMS)
            gp.wait_ge(pool, 7)
            for q in range(4):
                tl = slice(8 * q, 8 * q + 8)
                gp.wait_ge(x_ld[q // 2], 16)
                gp.tensor_tensor(m.x1[:, tl, :], m.x1[:, tl, :], bet[:, :].unsqueeze(1).to_broadcast([P, 8, D]),
                                 ALU.add).then_inc(xb_rd, 1)
            for q in range(4):
                tl = slice(8 * q, 8 * q + 8)
                gp.wait_ge(n_rd, 8 * (q + 1))
                gp.tensor_tensor(Y[:, tl, :], Y[:, tl, :], gam[:, :].unsqueeze(1).to_broadcast([P, 8, D]),
                                 ALU.mult).then_inc(g_rd2, 1)

        @blk.scalar
        def _(act):
            act.dma_start(U[:, :, :], a["x_rev"].rearrange("(t p) d -> p t d", p=P)).then_inc(u_ld, 16)
            act.wait_ge(par, 16 * PARAMS)
            act.activation(e_col[:, :], alog_col[:, :], ACT.Exp).then_inc(a_dn, 1)
            act.activation(e_row[:, :], alog_row[:, :], ACT.Exp).then_inc(a_dn, 1)
            act.wait_ge(io, 2)
            act.wait_ge(v_dn, 2)
            act.activation(pw[:, :], l_row[:, :], ACT.Exp, scale=z_col[:, 0:1]).then_inc(a_dn, 1)
            act.activation(prev[:, :], z_row[:, :], ACT.Exp, scale=p1_col[:, 0:1]).then_inc(a_dn, 1)
            for i in range(2 * (CH - 1)):
                c, half = i // 2, i % 2
                act.wait_ge(y_mm, i + 1)
                act.activation(Yv[:, 2 * half:2 * half + 2, c + 1, :],
                               m.ps[:, 2 + i % 2, :].rearrange("p (b d) -> p b d", b=2), ACT.Copy).then_inc(y_cp, 1)
            for g in range(NGR):
                act.wait_ge(t_us, g + 1)
                if g >= 2:
                    act.wait_ge(tr, g - 1)
                act.activation(by_tile[:, g % 2, :, :].rearrange("p q l -> p (q l)"),
                               m.ps[:, g % 4, 0:GR // 4 * P], ACT.Copy).then_inc(y_cp, 1)
            act.wait_ge(pool, 4)

            def deviation(r, sl, n):
                act.wait_ge(ln_v[r], n)
                act.activation(sd[:, r, sl], mv[:, r, sl, 1], ACT.Sqrt, bias=m.eps[:, 0:1]).then_inc(ln_s[r], 1)

            def normalise(r, q):
                act.wait_ge(rs_rd[r], 2 * q + 2 if r else 4 if q else 2)
                for t in range(8 * q, 8 * q + 8):
                    act.activation(Y[:, t, :] if r == 0 else m.x1[:, t, :], Y[:, t, :], ACT.Identity,
                                   scale=rs[:, r, t:t + 1], bias=shift[:, r, t:t + 1]).then_inc(n_rd if r == 0 else x1_rd, 1)

            def high(i):
                kt, tg = i % 2, i // 2
                act.wait_ge(tr, NGR + i + 1)
                act.activation(m.x1h[:, kt, 512 * tg:512 * tg + 512], m.ps[:, i % 4, :], ACT.Copy).then_inc(tr_h, 1)
            for n, (t0, t1) in enumerate(FIRST_LN):
                deviation(0, slice(t0, t1), t1)
                if n == 0:
                    normalise(0, 0)
            for q in range(5):
                if q + 1 < 4:
                    normalise(0, q + 1)
                if q < 4:
                    deviation(1, slice(8 * q, 8 * q + 8), 8 * q + 8)
                if q:
                    for i in range(4 * q - 4, 4 * q):
                        high(i)
                if q < 4:
                    normalise(1, q)

        @blk.vector
        def _(v):
            v.wait_ge(par, 16 * PARAMS)
            v.wait_ge(a_dn, 2)
            v.tensor_scalar(z_col[:, :], e_col[:, :], delta0[0:NS, 0:1], -1.0, ALU.mult, ALU.mult).then_inc(v_dn, 1)
            v.tensor_scalar(z_row[:, :], e_row[:, :], delta0[:, 0:1], -1.0, ALU.mult, ALU.mult).then_inc(v_dn, 1)
            v.tensor_tensor(cta[:, :], ct[:, :], fa_row[:, :], ALU.mult).then_inc(v_dn, 1)
            v.tensor_tensor(dfa[:, :], d_col[:, :], fa_col[:, :], ALU.mult).then_inc(v_dn, 1)
            v.wait_ge(k_mm, 1)
            v.wait_ge(io, 3)
            v.tensor_copy(kpad[:, :, P - 1:2 * P - 1],
                          m.ps[:, 0, 0:256].rearrange("p (m l) -> p m l", m=2)).then_inc(v_dn, 1)
            v.wait_ge(v_dn, 5)
            v.tensor_tensor(kpad[:, :, P - 1], kpad[:, :, P - 1], dfa[:, :], ALU.add).then_inc(k_rd, 1)
            for i in range(2 * (CH - 1)):
                c, half = i // 2, i % 2
                bs = slice(2 * half, 2 * half + 2)
                v.wait_ge(g_mm, i + 1)
                g = m.ps[0:NS, i % 2, :].rearrange("p (b d) -> p b d", b=2)
                if c == 0:
                    v.tensor_copy(HS[:, c % 2, bs, :], g).then_inc(g_rd, 1)
                else:
                    v.wait_ge(g_rd, i - 1)
                    v.scalar_tensor_tensor(HS[:, c % 2, bs, :].rearrange("p b d -> p (b d)"),
                                           HS[:, (c - 1) % 2, bs, :].rearrange("p b d -> p (b d)"), pw[:, P:P + 1],
                                           m.ps[0:NS, i % 2, :], ALU.mult, ALU.add).then_inc(g_rd, 1)
                v.wait_ge(g_rd, i + 1)
                v.tensor_tensor(CHs[:, c, bs, :], HS[:, c % 2, bs, :],
                                cta[:, :].unsqueeze(1).to_broadcast([NS, 2, D]), ALU.mult).then_inc(c_rd, 1)
            v.wait_ge(y_cp, 2 * (CH - 1))
            v.wait_ge(io, 4)
            for g in range(NGR):
                v.wait_ge(tr, g + 1)
                yd = Y[:, :, GR * g:GR * g + GR].rearrange("p t d -> p d t")
                v.tensor_tensor(yd, m.ps[:, 4 + g % 4, 0:GR * NT].rearrange("p (d t) -> p d t", d=GR), yd,
                                ALU.add).then_inc(t_ev, 1)
                if (g + 1) % (64 // GR) == 0:
                    c = g * GR // 64
                    cs = slice(64 * c, 64 * c + 64)
                    v.wait_ge(t_ev, g + 1)
                    v.tensor_tensor(Yv[0:1, :, 0, cs], Yv[0:1, :, 0, cs],
                                    rew[0:1, cs].unsqueeze(1).to_broadcast([1, B, 64]), ALU.add).then_inc(v_dn, 1)
                    v.wait_ge(v_dn, 6 + c)
                    for t in range(NT if c < 3 else 0):
                        v.bn_stats(stats[:, t, c, :], Y[:, t, cs]).then_inc(st_rd[0], 1)
            v.wait_ge(v_dn, 9)

            def scale_and_shift(r, sl, n):
                v.wait_ge(ln_s[r], n + 1)
                v.reciprocal(rs[:, r, sl], sd[:, r, sl]).then_inc(rs_rd[r], 1)
                v.wait_ge(rs_rd[r], 2 * n + 1)
                v.scalar_tensor_tensor(shift[:, r, sl], mv[:, r, sl, 0], -1.0, rs[:, r, sl], ALU.mult,
                                       ALU.mult).then_inc(rs_rd[r], 1)

            def low(i):
                kt, tg = i % 2, i // 2
                v.wait_ge(tr_h, i + 1)
                v.tensor_tensor(m.x1l[:, kt, 512 * tg:512 * tg + 512], m.ps[:, i % 4, :],
                                m.x1h[:, kt, 512 * tg:512 * tg + 512].bitcast(F32), ALU.subtract).then_inc(tr_l, 1)
            for n, (t0, t1) in enumerate(FIRST_LN):
                for t in range(t0, t1):
                    v.bn_stats(stats[:, t, 3, :], Y[:, t, 192:D]).then_inc(st_rd[0], 1)
                for t in range(t0, t1):
                    v.wait_ge(st_rd[0], 3 * NT + t + 1)
                    v.bn_aggr(mv[:, 0, t, :], stats[:, t, :, :].rearrange("p c s -> p (c s)")).then_inc(ln_v[0], 1)
                scale_and_shift(0, slice(t0, t1), n)
            for q in range(5):
                sl = slice(8 * q, 8 * q + 8)
                if q < 4:
                    v.wait_ge(g_rd2, q + 1)
                    v.wait_ge(xb_rd, q + 1)
                    v.tensor_tensor(Y[:, sl, :], Y[:, sl, :], m.x1[:, sl, :], ALU.add).then_inc(n_gb, 1)
                    v.wait_ge(n_gb, q + 1)
                    for t in range(8 * q, 8 * q + 8):
                        v.bn_stats(stats2[:, t, :], Y[:, t, :]).then_inc(st_rd[1], 1)
                    for t in range(8 * q, 8 * q + 8):
                        v.wait_ge(st_rd[1], t + 1)
                        v.bn_aggr(mv[:, 1, t, :], stats2[:, t, :]).then_inc(ln_v[1], 1)
                if q:
                    for i in range(4 * q - 4, 4 * q):
                        low(i)
                if q < 4:
                    scale_and_shift(1, sl, q)

        @blk.tensor
        def _(pe):
            pe.wait_ge(a_dn, 4)
            pe.wait_ge(v_dn, 3)
            for mt in range(2):
                mm = nc.tensor.matmul(m.ps[:, 0, P * mt:P * mt + P], cta[:, P * mt:P * mt + P], pw[:, 0:P],
                                      start=True, stop=True)
            mm.then_inc(k_mm, 1)
            pe.wait_ge(u_ld, 16)
            pe.wait_ge(k_rd, 1)

            def carry(i):
                c, half = i // 2, i % 2
                pe.wait_ge(c_rd, i + 1)
                if i >= 2:
                    pe.wait_ge(y_cp, i - 1)
                nc.tensor.matmul(m.ps[:, 2 + i % 2, :], pw[:, 0:P],
                                 CHs[:, c, 2 * half:2 * half + 2, :].rearrange("p b d -> p (b d)"),
                                 start=True, stop=True).then_inc(y_mm, 1)
            for i in range(2 * (CH - 1)):
                c, half = i // 2, i % 2
                if i >= 2:
                    pe.wait_ge(g_rd, i - 1)
                nc.tensor.matmul(m.ps[0:NS, i % 2, :], prev[:, :], Uv[:, 2 * half:2 * half + 2, c, :],
                                 start=True, stop=True).then_inc(g_mm, 1)
                if i >= 2:
                    carry(i - 2)
            carry(2 * CH - 4)
            carry(2 * CH - 3)

            def by_position(g):
                pe.wait_ge(y_cp, CARRIES + g + 1)
                if g >= 4:
                    pe.wait_ge(t_ev, g - 3)
                for q in range(GR // 4):
                    mm = nc.tensor.transpose(m.ps[:, 4 + g % 4, P * q:P * q + P], by_tile[:, g % 2, q, :], m.ident[:, :])
                mm.then_inc(tr, 1)
            CARRIES = 2 * (CH - 1)
            pe.wait_ge(g_rd, CARRIES)
            pe.wait_ge(pool, 7)
            for g in range(NGR):
                pe.wait_ge(t_ld[g % RING], 16 * (g // RING + 1))
                pe.wait_ge(y_cp, CARRIES + max(0, g - 3))
                for j in range(GR):
                    p0, q = 32 * (j % 4), j // 4
                    mm = nc.tensor.matmul(m.ps[p0:p0 + NT, g % 4, P * q:P * q + P], U[:, :, GR * g + j],
                                          TZ[:, g % RING, j // 2, 2 * P * (j % 2):2 * P * (j % 2) + P],
                                          start=True, stop=True, tile_position=(0, p0))
                mm.then_inc(t_us, 1)
                if g:
                    by_position(g - 1)
            by_position(NGR - 1)
            for i in range(16):
                kt, tg = i % 2, i // 2
                pe.wait_ge(x1_rd, 4 * tg + 4)
                if i >= 4:
                    pe.wait_ge(tr_l, i - 3)
                for j in range(4):
                    mm = nc.tensor.transpose(m.ps[:, i % 4, P * j:P * j + P],
                                             m.x1[:, 4 * tg + j, P * kt:P * kt + P], m.ident[:, :])
                mm.then_inc(tr, 1)


def split_plan():
    plan = [("c", mt, 2 * M * hb, 2 * M) for mt in range(2) for hb in range(2)]
    plan += [("q", mt, 512 * tb, 512) for mt in range(2) for tb in range(8)]
    plan += [("k", mt, 512 * tb, 512) for mt in range(2) for tb in range(8)]
    return plan


def phase_projections(nc, m, a):
    SLOTS = 6
    with ExitStack() as st:
        sb, sem = tensors(nc, st)
        w = sb("qkv_weights", [P, 2, 3 * D])
        wh = sb("qkv_high", [P, 2, 3 * D], F32R)
        wl = sb("qkv_low", [P, 2, 3 * D], F32R)
        c = sb("context_t", [P, 2, B * M])
        ch = sb("context_high", [P, 2, B * M], F32R)
        cl = sb("context_low", [P, 2, B * M], F32R)
        parts = sb("parts", [P, SLOTS, 3, 512], BF16)
        rest = sb("rest", [P, 4, 512])
        vt = sb("v_tiles", [P, 4, H, 32])
        ld = sem("weights_loaded")
        wsp = sem("weights_split")
        ones = sem("ones_ready")
        qk_mm = sem("qk_matmul_done")
        p1 = sem("part1_ready")
        r1 = sem("rest_ready")
        p2 = sem("part2_ready")
        p3 = sem("part3_ready")
        wr = [sem(f"parts_written_{i}") for i in range(SLOTS)]
        v_mm = sem("v_matmul_done")
        v_cp = sem("v_copied")
        v_wr = [sem(f"v_written_{i}") for i in range(4)]
        plan = split_plan()
        v_plan = [(b, t, P) for b in range(B) for t in range(CH)] + \
                 [(b, t, n) for b in range(B) for t, n in ((CH, P), (CH + 1, M - P))]
        done = [0] * SLOTS
        before = []
        for n, (kind, mt, c0, cols) in enumerate(plan):
            before.append(done[n % SLOTS])
            done[n % SLOTS] += 16 * (4 if kind == "c" else 2)
        blk = st.enter_context(nc.Block())

        def alternate(qk_tile, v_tile):
            for n in range(max(len(plan), len(v_plan))):
                if n < len(plan):
                    qk_tile(n)
                if n < len(v_plan):
                    v_tile(n)

        @blk.sync
        def _(sp):
            sp.dma_start(w[:, :, 0:D], a["Wq"].rearrange("(k p) n -> p k n", p=P)).then_inc(ld, 16)
            sp.dma_start(w[:, :, D:3 * D], a["Wkv"].rearrange("(k p) n -> p k n", p=P)).then_inc(ld, 16)
            sp.dma_start(c[:, :, :], a["ctx_T"].rearrange("(k p) n -> p k n", p=P)).then_inc(ld, 16)
            for n, (kind, mt, c0, cols) in enumerate(plan):
                s = n % SLOTS
                sp.wait_ge(p3, n + 1)
                for hg in range(2):
                    rows = parts[64 * hg:64 * hg + 64, s, :, :]
                    dram = m.q_dram if kind == "q" else m.k_dram
                    if kind == "c":
                        for j in range(2):
                            b = c0 // M + j
                            sp.dma_start(dram[NG * b + 2 * mt + hg, :, :, L:KEYS],
                                         rows[:, :, M * j:M * j + M]).then_inc(wr[s], 16)
                    else:
                        b, l0 = c0 // L, c0 % L
                        sp.dma_start(dram[NG * b + 2 * mt + hg, :, :, l0:l0 + 512], rows).then_inc(wr[s], 16)
            for s in range(SLOTS):
                sp.wait_ge(wr[s], done[s])

        @blk.gpsimd
        def _(gp):
            gp.memset(vt[:, :, :, DH:32], 1.0).then_inc(ones, 1)
            for n, (kind, mt, c0, cols) in enumerate(plan):
                s = n % SLOTS
                gp.wait_ge(p2, n + 1)
                if before[n]:
                    gp.wait_ge(wr[s], before[n])
                gp.tensor_tensor(parts[:, s, 2, 0:cols], rest[:, n % 4, 0:cols], parts[:, s, 1, 0:cols],
                                 ALU.subtract).then_inc(p3, 1)

        @blk.scalar
        def _(act):
            def first_part(n):
                kind, mt, c0, cols = plan[n]
                s = n % SLOTS
                act.wait_ge(qk_mm, n + 1)
                if before[n]:
                    act.wait_ge(wr[s], before[n])
                act.activation(parts[:, s, 0, 0:cols], m.ps[:, n % 4, 0:cols], ACT.Copy,
                               scale=DH ** -0.5 if kind == "q" else 1.0).then_inc(p1, 1)
                if n:
                    second_part(n - 1)
                if n + 1 == len(plan):
                    second_part(n)

            def second_part(n):
                kind, mt, c0, cols = plan[n]
                act.wait_ge(r1, n + 1)
                act.activation(parts[:, n % SLOTS, 1, 0:cols], rest[:, n % 4, 0:cols], ACT.Copy).then_inc(p2, 1)

            def v_tile(n):
                b, t, rows = v_plan[n]
                s = n % 4
                act.wait_ge(v_mm, n + 1)
                if n >= 4:
                    act.wait_ge(v_wr[s], 16 * (n // 4))
                act.activation(vt[0:rows, s, :, 0:DH],
                               m.ps[0:rows, 4 + s, 0:D].rearrange("p (h d) -> p h d", h=H),
                               ACT.Copy).then_inc(v_cp, 1)
                act.wait_ge(v_cp, n + 1)
                act.dma_start(m.v_dram[NG * b:NG * b + NG, P * t:P * t + rows, :].rearrange("g p c -> p g c"),
                              vt[0:rows, s, :, :].rearrange("p (g h) c -> p g (h c)", g=NG)).then_inc(v_wr[s], 16)
            act.wait_ge(ones, 1)
            alternate(first_part, v_tile)
            for s in range(4):
                act.wait_ge(v_wr[s], 16 * (len(v_plan) // 4))

        @blk.vector
        def _(v):
            v.wait_ge(ld, 48)
            v.tensor_copy(wh[:, :, :], w[:, :, :]).then_inc(wsp, 1)
            v.tensor_copy(ch[:, :, :], c[:, :, :]).then_inc(wsp, 1)
            v.wait_ge(wsp, 2)
            v.tensor_tensor(wl[:, :, :], w[:, :, :], wh[:, :, :].bitcast(F32), ALU.subtract).then_inc(wsp, 1)
            v.tensor_tensor(cl[:, :, :], c[:, :, :], ch[:, :, :].bitcast(F32), ALU.subtract).then_inc(wsp, 1)
            for n, (kind, mt, c0, cols) in enumerate(plan):
                s = n % SLOTS
                v.wait_ge(p1, n + 1)
                if n >= 4:
                    v.wait_ge(p3, n - 3)
                v.scalar_tensor_tensor(rest[:, n % 4, 0:cols], m.ps[:, n % 4, 0:cols], DH ** -0.5 if kind == "q" else 1.0,
                                       parts[:, s, 0, 0:cols], ALU.mult, ALU.subtract).then_inc(r1, 1)

        @blk.tensor
        def _(pe):
            pe.wait_ge(wsp, 4)
            def qk_tile(n):
                kind, mt, c0, cols = plan[n]
                if n >= 4:
                    pe.wait_ge(r1, n - 3)
                w0 = (0 if kind == "q" else D) + P * mt
                xh, xl = (ch, cl) if kind == "c" else (m.x1h, m.x1l)
                for i, (kt, wt, xt) in enumerate((kt, wt, xt) for kt in range(2)
                                                 for wt, xt in ((wh, xl), (wl, xh), (wh, xh))):
                    mm = nc.tensor.matmul(m.ps[:, n % 4, 0:cols], wt[:, kt, w0:w0 + P], xt[:, kt, c0:c0 + cols],
                                          start=(i == 0), stop=(i == 5))
                mm.then_inc(qk_mm, 1)

            def v_tile(n):
                b, t, rows = v_plan[n]
                if n >= 4:
                    pe.wait_ge(v_cp, n - 3)
                if t < CH:
                    xh, xl, c0 = m.x1h, m.x1l, L * b + P * t
                else:
                    xh, xl, c0 = ch, cl, M * b + P * (t - CH)
                for i, (kt, wt, xt) in enumerate((kt, wt, xt) for kt in range(2)
                                                 for wt, xt in ((wh, xl), (wl, xh), (wh, xh))):
                    mm = nc.tensor.matmul(m.ps[0:rows, 4 + n % 4, 0:D], xt[:, kt, c0:c0 + rows],
                                          wt[:, kt, 2 * D:3 * D], start=(i == 0), stop=(i == 5))
                mm.then_inc(v_mm, 1)
            alternate(qk_tile, v_tile)


def passes(kts, high, low, with_low):
    return [(kt, wi, xx) for kt in kts for wi, xx in ((0, low),) + (((1, high),) if with_low else ()) + ((0, high),)]


def split_high(eng, high, raw):
    return eng.tensor_copy(high, raw)


def split_low(eng, high, low, raw):
    return eng.tensor_tensor(low, raw, high.bitcast(F32), ALU.subtract)


def low_maximum(v, column, low):
    return v.tensor_reduce(column, low.bitcast(F32), AX_X, ALU.max, apply_absolute_value=True)


def low_question(nc, m, sb, sem, low_any, tag):
    needed = sb(f"low_needed_{tag}", [1, 1], mybir.dt.int32)
    s_sum = sem(f"low_sum_done_{tag}")
    s_nd = sem(f"low_needed_ready_{tag}")

    def vector(v):
        v.wait_ge(s_sum, 1)
        v.tensor_copy(needed[:, :], m.ps[0:1, 7, 0:1]).then_inc(s_nd, 1)

    def tensor(pe):
        nc.tensor.matmul(m.ps[0:1, 7, 0:1], low_any, m.ones[:, :], start=True, stop=True).then_inc(s_sum, 1)
        pe.wait_ge(s_nd, 1)
        return pe.value_load(needed[0:1, 0:1], min_val=0, max_val=P)
    return vector, tensor


def score_plan():
    steps = []
    for c in range(2):
        for kt in range(4 * (c + 1)):
            steps.append((c, kt, P, max(0, P * kt - 512 * c)))
        steps += [(c, CH, P, 0), (c, CH + 1, M - P, 0)]
    return steps


def max_plan():
    units = []
    for h in range(HG):
        for i in range(CH):
            xk = P * (i + 1)
            cut = [(0, min(xk, 512), xk <= 512)] + ([(512, xk - 512, True)] if xk > 512 else [])
            chunks = [[(0, k0, kn, dg)] for k0, kn, dg in cut]
            if chunks[-1][0][2] + M <= 512:
                chunks[-1].append((chunks[-1][0][2], L, M, False))
            else:
                chunks.append([(0, L, M, False)])
            units += [(h, i, c, pc) for c, pc in enumerate(chunks)]
    return units


TERMS = ((0, 0), (0, 1), (1, 0), (0, 2), (2, 0), (1, 1))
TR = 16 * len(TERMS)
MR = TR + 3


def phase_attention(nc, m, a):
    S = 3
    RP = 8
    AHEAD = 2
    ROT = 5
    UPS = 4
    with ExitStack() as st:
        sb, sem = tensors(nc, st)
        Q = [sb(f"q_rows_{s}", [MR, HG, L], BF16) for s in range(S)]
        K = [sb(f"k_rows_{s}", [MR, HG, KP], BF16) for s in range(S)]
        V = [sb(f"v_rows_{s}", [P, KT - 1, HG * 32]) for s in range(S)]
        VT = [sb(f"v_tail_{s}", [P, HG * 32]) for s in range(S)]
        PR = arena(nc, m, "probabilities", 8 * F, [RP, 2, 512])
        OT = sb("out_transposed", [P, 2, 512])
        O = sb("out_heads", [P, 2, 4, HG, DH])
        rc = sb("denominator_inverse", [P, 4, HG])
        mxp = sb("max_partial", [P, HG * CH, 3])
        negm = sb("minus_max", [P, HG * CH])
        rst = sb("minus_max_rest", [P, HG * CH])
        M3 = sb("minus_max_parts", [P, 3, HG * CH], BF16)
        MT = sb("minus_max_rows", [3 * HG * CH, P], BF16)

        ini = sem("constants_ready")
        INI = 1 + 3 * S
        w_ld = sem("w1_w2_loaded")
        h_ld = sem("h1_loaded")
        w_hi = sem("w1_w2_high_ready")
        w_lo = sem("w1_w2_low_ready")
        ld = [sem(f"step_loaded_{s}") for s in range(S)]
        mr = [sem(f"max_rows_loaded_{s}") for s in range(S)]
        nat = sem("max_scores_done")
        red = sem("max_bank_read")
        mx = sem("max_chain")
        t_mm = sem("small_transpose_done")
        mt_rd = sem("max_rows_ready")
        mw = sem("max_rows_written")
        s_mm = sem("score_pair_done")
        e_dn = sem("exp_pair_done")
        k_dn = sem("pair_masked")
        p_dn = sem("pv_step_done")
        o_cp = sem("pv_bank_read")
        r_dn = sem("inverse_ready")
        o_rd = sem("out_ready")
        turn = sem("waits_carried")
        o_wr = [sem(f"out_written_{c}") for c in range(2)]

        steps = score_plan()
        units = max_plan()
        NU, NSP = len(units), len(steps)
        NSC = 2 * NSP
        assert NU == UPS * NSP
        MAXED = NSP - ROT
        LOADS = 16 * (2 * len(TERMS) + 1 + HG)
        TAIL = KEYS - P * (KT - 1)
        diag = [si for si, (c, kt, rows, off) in enumerate(steps) if kt < CH and kt >= 4 * c]

        def units_at(si, more, more2):
            ahead, u = (1, UPS * (si + ROT)) if si < MAXED else (2, UPS * (si - MAXED))
            return [(ahead, u + k) for k in range(UPS)] if (more if ahead == 1 else more2) else []

        blk = st.enter_context(nc.Block())

        def loop(eng, body):
            body(0, 0, 0, True, True, True)
            with eng.Fori(0, (IT - 4) // S) as i:
                for j in range(S):
                    body(i * S + (j + 1), (j + 1) % S, i + (j + 1) // S, False, True, True)
            for n in range(IT - 3, IT):
                body(n, n % S, n // S, False, n < IT - 1, n < IT - 2)

        @blk.sync
        def _(sp):
            def load(n, s):
                for t, (pq, pk) in enumerate(TERMS):
                    sp.dma_start(Q[s][DH * t:DH * t + DH, :, :],
                                 m.q_dram[n, :, pq, :].rearrange("(h r) l -> r h l", r=DH)).then_inc(ld[s], 16)
                    sp.dma_start(K[s][DH * t:DH * t + DH, :, 0:KEYS],
                                 m.k_dram[n, :, pk, 0:KEYS].rearrange("(h r) l -> r h l", r=DH)).then_inc(ld[s], 16)
                sp.dma_start(V[s][:, 0:KT - 1, :],
                             m.v_dram[n, 0:P * (KT - 1), :].rearrange("(t p) c -> p t c", p=P)).then_inc(ld[s], 16)
                for h in range(HG):
                    sp.dma_start(VT[s][32 * h:32 * h + TAIL, 32 * h:32 * h + 32],
                                 m.v_dram[n, P * (KT - 1):P * (KT - 1) + TAIL, 32 * h:32 * h + 32]).then_inc(ld[s], 16)

            def max_rows(n, s):
                sp.wait_ge(mt_rd, n + 1)
                sp.dma_start(m.max_dram[:, :], MT[:, :]).then_inc(mw, 16)
                sp.wait_ge(mw, n * 16 + 16)
                sp.dma_start(Q[s][TR:MR, :, :].rearrange("o h l -> o (h l)"),
                             m.max_dram.rearrange("(o k) p -> o (k p)", o=3)).then_inc(mr[s], 16)

            def store(n, c):
                sp.wait_ge(o_rd, 2 * n + (c + 2))
                sp.dma_start(m.o_dram[n, c, :, :, :],
                             O[:, c, :, :, :].rearrange("p q h d -> p q (h d)")).then_inc(o_wr[c], 16)

            def body(n, s, use, first, more, more2):
                if more2:
                    sp.wait_ge(p_dn, n * NSP + 4)
                    load(n + 2, (s + 2) % S)
                if not first:
                    store(n - 1, 1)
                store(n, 0)
                if more:
                    max_rows(n + 1, (s + 1) % S)

            for c in range(2):
                sp.sem_inc(o_wr[c], 16)
            sp.wait_ge(ini, S)
            load(0, 0)
            load(1, 1)
            for w, name in ((m.w1, "w1_T"), (m.w2, "w2_T")):
                sp.dma_start(w[2][:, :, :], a[name].rearrange("(k p) n -> p k n", p=P)).then_inc(w_ld, 16)
            sp.dma_start(m.h1[2][:, :, :], a["h1_T"].rearrange("(k p) n -> p k n", p=P)).then_inc(h_ld, 16)
            max_rows(0, 0)
            loop(sp, body)
            store(IT - 1, 1)
            for c in range(2):
                sp.wait_ge(o_wr[c], 16 * IT + 16)

        @blk.gpsimd
        def _(gp):
            for s in range(S):
                gp.memset(VT[s][:, :], 0.0).then_inc(ini, 1)
            gp.memset(mxp[:, :, :], LOWEST).then_inc(ini, 1)
            done = S + 1
            for s in range(S):
                gp.wait_ge(ini, done)
                gp.memset(K[s][TR:MR, :, 0:KEYS], 1.0).then_inc(ini, 1)
                gp.wait_ge(ini, done + 1)
                gp.memset(K[s][0:MR, :, KEYS:KP], 0.0).then_inc(ini, 1)
                done += 2
            gp.wait_ge(ini, INI)
            gp.wait_ge(w_ld, 32)
            for n, w in enumerate((m.w1, m.w2)):
                split_high(gp, w[0][:, :, :], w[2][:, :, :]).then_inc(w_hi, 1)
                gp.wait_ge(w_hi, n + 1)
                split_low(gp, w[0][:, :, :], w[1][:, :, :], w[2][:, :, :]).then_inc(w_lo, 1)

            def body(n, s, use, first, more, more2):
                for d, si in enumerate(diag):
                    c, kt, rows, off = steps[si]
                    for pr in range(2):
                        u = 2 * si + pr
                        gp.wait_ge(e_dn, n * NSC + u + 3)
                        gp.sem_inc(turn, 1)
                        blk_ = PR[:, u % RP, :, off:off + P]
                        gp.affine_select(out=blk_, in_=blk_, compare_op=ALU.is_ge, fill=0.0, base=0,
                                         pattern=[[0, 2], [1, P]], channel_multiplier=-1).then_inc(k_dn, 1)
            loop(gp, body)
            gp.wait_ge(h_ld, 16)

        @blk.scalar
        def _(act):
            act.sem_inc(e_dn, 2)
            act.sem_inc(o_cp, 1)

            def out_copy(n, c):
                act.wait_ge(p_dn, n * NSP + ((6 if c == 0 else NSP) + 4))
                act.wait_ge(t_mm, n * 3 + (c + 1))
                act.activation(OT[:, c, :], m.ps[:, 6, :], ACT.Copy).then_inc(o_cp, 1)

            def body(n, s, use, first, more, more2):
                for si, (c, kt, rows, off) in enumerate(steps):
                    for pr in range(2):
                        u = 2 * si + pr
                        b0 = 2 + 2 * (u % 2)
                        if rows < P:
                            if pr == 0:
                                act.wait_ge(s_mm, n * NSC + (u + 1))
                                act.wait_ge(p_dn, n * NSP + (si + 1))
                                act.activation(PR[:, u % RP, 0, :], m.ps[:, b0, :], ACT.Exp).then_inc(e_dn, 2)
                        else:
                            act.wait_ge(s_mm, n * NSC + (u + 1))
                            act.wait_ge(p_dn, n * NSP + (si + 1))
                            act.activation(PR[:, u % RP, :, off:512], m.ps[:, b0:b0 + 2, off:512],
                                           ACT.Exp).then_inc(e_dn, 1)
                        if pr == 0 and si == 5 + AHEAD:
                            out_copy(n, 0)
                        if pr == 0 and si == AHEAD - 1 and not first:
                            out_copy(n - 1, 1)
            loop(act, body)
            out_copy(IT - 1, 1)

        @blk.vector
        def _(v):
            v.sem_inc(o_rd, 1)
            v.wait_ge(ini, S + 1)

            def unit(n, u):
                h, i, c, pieces = units[u]
                v.wait_ge(nat, n * NU + u + 1)
                width = pieces[-1][0] + pieces[-1][2]
                j = CH * h + i
                v.tensor_reduce(mxp[:, j, c:c + 1], m.ps[:, u % 2, 0:width], AX_X, ALU.max).then_inc(red, 1)

            def maximum(n):
                v.wait_ge(red, (n + 1) * NU)
                v.tensor_reduce(negm[:, :], mxp[:, :, :], AX_X, ALU.max, negate=True).then_inc(mx, 1)
                v.wait_ge(mx, n * 5 + 1)
                v.tensor_copy(M3[:, 0, :], negm[:, :]).then_inc(mx, 1)
                v.wait_ge(mx, n * 5 + 2)
                v.tensor_tensor(rst[:, :], negm[:, :], M3[:, 0, :], ALU.subtract).then_inc(mx, 1)
                v.wait_ge(mx, n * 5 + 3)
                v.tensor_copy(M3[:, 1, :], rst[:, :]).then_inc(mx, 1)
                v.wait_ge(mx, n * 5 + 4)
                v.tensor_tensor(M3[:, 2, :], rst[:, :], M3[:, 1, :], ALU.subtract).then_inc(mx, 1)

            def max_rows(n, s, use, first=False):
                v.wait_ge(t_mm, 1 if first else n * 3)
                if not first:
                    ps_, pu = (s - 1) % S, use if s else use - 1
                    v.wait_ge(mr[ps_], (pu + 1) * 16)
                v.tensor_copy(MT[:, :], m.ps[0:3 * HG * CH, 7, 0:P // 2].bitcast(BF16)).then_inc(mt_rd, 1)

            def normalise(n, c, more=True):
                v.wait_ge(t_mm, n * 3 + (2 if c == 0 else 4 if more else 3))
                q = m.ps[:, 7, :].rearrange("p (q h e) -> p q h e", q=4, h=HG)
                v.wait_ge(o_rd, 2 * n + c + 1)
                v.reciprocal(rc[:, :, :], q[:, :, :, DH]).then_inc(r_dn, 1)
                v.wait_ge(r_dn, 2 * n + c + 1)
                v.wait_ge(o_wr[c], n * 16 + 16)
                v.tensor_tensor(O[:, c, :, :, :], q[:, :, :, 0:DH],
                                rc[:, :, :].unsqueeze(3).to_broadcast([P, 4, HG, DH]), ALU.mult).then_inc(o_rd, 1)

            for u in range(NU):
                unit(0, u)
            maximum(0)
            max_rows(0, 0, 0, first=True)
            for u in range(UPS * ROT):
                unit(1, u)

            def body(n, s, use, first, more, more2):
                for si in range(NSP):
                    for ahead, u in units_at(si, more, more2):
                        unit(n + ahead, u)
                    if si == 3 and not first:
                        normalise(n - 1, 1)
                    if si == 9:
                        normalise(n, 0)
                    if si == MAXED - 1 and more:
                        maximum(n + 1)
                    if si == MAXED and more:
                        max_rows(n + 1, (s + 1) % S, use + (s + 1) // S)
            loop(v, body)
            normalise(IT - 1, 1, more=False)

        @blk.tensor
        def _(pe):
            pe.sem_inc(p_dn, 4)

            def unit(n, u, s, first=False):
                h, i, c, pieces = units[u]
                if not first or u >= 2:
                    pe.wait_ge(red, n * NU + u - 1)
                bank = u % 2
                for col, k0, kn, masked in pieces:
                    mm = nc.tensor.matmul(m.ps[:, bank, col:col + kn], Q[s][0:TR, h, P * i:P * i + P],
                                          K[s][0:TR, h, k0:k0 + kn], start=True, stop=not masked)
                    if masked:
                        mm = nc.tensor.matmul(m.ps[:, bank, col + kn - P:col + kn], m.ident_bf[:, :],
                                              m.mask_bf[:, :], start=False, stop=True)
                mm.then_inc(nat, 1)

            def max_rows(n, first=False):
                pe.wait_ge(mx, n * 5 + 5)
                if not first:
                    pe.wait_ge(o_rd, 2 * n)
                nc.tensor.transpose(m.ps[0:3 * HG * CH, 7, 0:P // 2].bitcast(BF16),
                                    M3[:, :, :].rearrange("p a b -> p (a b)"), m.ident_bf[:, :]).then_inc(t_mm, 1)

            def out_rows(n, c, last=False):
                pe.wait_ge(o_cp, 2 * n + (c + 2))
                if c == 0:
                    pe.wait_ge(mt_rd, n + 1)
                    pe.wait_ge(o_rd, 2 * n + 1)
                elif last:
                    pe.wait_ge(o_rd, 2 * n + 2)
                else:
                    pe.wait_ge(mt_rd, n + 2)
                for q in range(4):
                    mm = nc.tensor.transpose(m.ps[:, 7, P * q:P * q + P], OT[:, c, P * q:P * q + P], m.ident[:, :])
                mm.then_inc(t_mm, 1)

            def scores(n, si, s, use, pr):
                c, kt, rows, off = steps[si]
                if si == 0 and pr == 0:
                    pe.wait_ge(mr[s], use * 16 + 16)
                u = 2 * si + pr
                b0 = 2 + 2 * (u % 2)
                if rows < P and pr == 1:
                    return
                pe.wait_ge(e_dn, n * NSC + (u + 1))
                if rows < P:
                    pe.sem_inc(turn, 1)
                    for h in range(HG):
                        mm = nc.tensor.matmul(m.ps[32 * h:32 * h + 32, b0, :], K[s][:, h, P * kt:P * kt + 32],
                                              Q[s][:, h, 512 * c:512 * c + 512], start=True, stop=True,
                                              tile_position=(0, 32 * h))
                    mm.then_inc(s_mm, 2)
                    return
                for j in range(2):
                    mm = nc.tensor.matmul(m.ps[0:rows, b0 + j, off:512],
                                          K[s][:, 2 * pr + j, P * kt:P * kt + rows],
                                          Q[s][:, 2 * pr + j, 512 * c + off:512 * c + 512],
                                          start=True, stop=True)
                mm.then_inc(s_mm, 1)

            def pv(n, si, s):
                c, kt, rows, off = steps[si]
                pe.wait_ge(e_dn, n * NSC + 2 * si + 4)
                if si in diag:
                    pe.wait_ge(k_dn, n * 2 * len(diag) + 2 * diag.index(si) + 2)
                first = kt == 0
                last = kt == KT - 1
                if first:
                    pe.wait_ge(o_cp, 2 * n + c + 1)
                if last:
                    nc.tensor.matmul(m.ps[:, 6, :], VT[s][:, :], PR[:, (2 * si) % RP, 0, :],
                                     start=False, stop=True).then_inc(p_dn, 1)
                    return
                for h in range(HG):
                    mm = nc.tensor.matmul(m.ps[32 * h:32 * h + 32, 6, off:512], V[s][:, kt, 32 * h:32 * h + 32],
                                          PR[:, (2 * si + h // 2) % RP, h % 2, off:512],
                                          start=first, stop=False, tile_position=(0, 32 * h))
                mm.then_inc(p_dn, 1)

            pe.wait_ge(ld[0], LOADS)
            for u in range(NU):
                unit(0, u, 0, first=True)
            max_rows(0, first=True)
            pe.wait_ge(ld[1], LOADS)
            for u in range(UPS * ROT):
                unit(1, u, 1)
            pe.wait_ge(ini, INI)
            for si in range(AHEAD):
                for pr in range(2):
                    scores(0, si, 0, 0, pr)

            def body(n, s, use, first, more, more2):
                def scores_ahead(si, pr):
                    if si + AHEAD < NSP:
                        scores(n, si + AHEAD, s, use, pr)
                    elif more:
                        scores(n + 1, si + AHEAD - NSP, (s + 1) % S, use + (s + 1) // S, pr)

                for si in range(NSP):
                    todo = units_at(si, more, more2)
                    if si == MAXED and more2:
                        pe.wait_ge(ld[(s + 2) % S], (use + (s + 2) // S) * LOADS + LOADS)
                    def unit_at(k):
                        for ahead, u in todo[k:k + 1]:
                            unit(n + ahead, u, (s + ahead) % S)
                    scores_ahead(si, 0)
                    unit_at(0)
                    unit_at(1)
                    pv(n, si, s)
                    unit_at(2)
                    scores_ahead(si, 1)
                    unit_at(3)
                    if si == 2 and not first:
                        out_rows(n - 1, 1)
                    if si == 8:
                        out_rows(n, 0)
                    if si == MAXED and more:
                        max_rows(n + 1)
            loop(pe, body)
            out_rows(IT - 1, 1, last=True)


def phase_output(nc, m, a):
    NB = NT // 4
    with ExitStack() as st:
        sb, sem = tensors(nc, st)
        w = sb("wout", [P, 2, D])
        wh = sb("wout_high", [P, 2, D], F32R)
        wl = sb("wout_low", [P, 2, D], F32R)
        o = sb("attention_out", [P, NB, 4, NG, HG * DH])
        oh = sb("attention_t_high", [P, 2, 2, 512], F32R)
        ol = sb("attention_t_low", [P, 2, 2, 512], F32R)
        xt = sb("x2_t", [P, 2, 2, 512])
        stats = sb("ln_stats_d", [P, NT, 6])
        mv = sb("ln_mean_var_d", [P, NT, 2])
        sd = sb("ln_sd_d", [P, NT])
        rs = sb("ln_rs_d", [P, NT])
        low_max = sb("low_max_first", [P, 12])
        ld = sem("wout_loaded")
        wsp = sem("wout_split")
        o_ld = [sem(f"attention_out_loaded_{b}") for b in range(B)]
        xb = sem("x1_with_bias")
        tr = sem("attention_transposed")
        oh_r = sem("attention_high_ready")
        ol_r = sem("attention_low_ready")
        pj = sem("projected")
        z_r = sem("residual_sum_ready")
        bs = sem("ln_stats_ready_d")
        ba = sem("ln_variance_ready_d")
        sq = sem("ln_sd_ready_d")
        rr = sem("ln_rs_ready_d")
        x2r = sem("x2_ready")
        x_tr = sem("x2_transposed")
        x_cp = sem("x2_t_ready")
        x_wr = sem("x2_written")
        t_wr = [sem(f"x2_t_written_{i}") for i in range(2)]
        h_hi = sem("h1_high_ready")
        h_lo = sem("h1_low_ready")
        lm = sem("low_max_ready")
        blk = st.enter_context(nc.Block())
        low_parts = [m.w1[1][:, k, :] for k in range(2)] + [m.w2[1][:, k, :] for k in range(2)] + \
                    [m.h1[1][:, k, :] for k in range(8)]

        @blk.sync
        def _(sp):
            sp.dma_start(w[:, :, :], a["Wout"].rearrange("(k p) n -> p k n", p=P)).then_inc(ld, 16)
            for g in range(NB):
                b, c = g // 2, g % 2
                for hg in range(NG):
                    sp.dma_start(o[:, g, :, hg, :], m.o_dram[NG * b + hg, c, :, :, :]).then_inc(o_ld[b], 16)
            for g in range(NB):
                sp.wait_ge(x2r, 4 * g + 4)
                sp.dma_start(m.x2_dram[512 * g:512 * g + 512, :].rearrange("(t p) d -> p t d", p=P),
                             m.x1[:, 4 * g:4 * g + 4, :]).then_inc(x_wr, 16)
                sp.wait_ge(x_cp, 2 * g + 2)
                sp.dma_start(m.x2t_dram[:, 512 * g:512 * g + 512].rearrange("(k p) t -> p k t", p=P),
                             xt[:, g % 2, :, :]).then_inc(t_wr[g % 2], 16)
            sp.wait_ge(x_wr, 16 * NB)
            for i in range(2):
                sp.wait_ge(t_wr[i], 16 * NB // 2)

        @blk.gpsimd
        def _(gp):
            for g in range(NB):
                v = m.x1[:, 4 * g:4 * g + 4, :]
                gp.tensor_tensor(v, v, m.bout[:, :].unsqueeze(1).to_broadcast([P, 4, D]), ALU.add).then_inc(xb, 1)
                split_high(gp, m.h1[0][:, g, :], m.h1[2][:, g, :]).then_inc(h_hi, 1)
                gp.wait_ge(h_hi, g + 1)
                split_low(gp, m.h1[0][:, g, :], m.h1[1][:, g, :], m.h1[2][:, g, :]).then_inc(h_lo, 1)

        @blk.scalar
        def _(act):
            def high(g):
                for kt in range(2):
                    act.wait_ge(tr, 2 * g + kt + 1)
                    if g >= 2:
                        act.wait_ge(pj, 2 * g - 2)
                    act.activation(oh[:, g % 2, kt, :], m.ps[:, kt, :], ACT.Copy).then_inc(oh_r, 1)

            def transposed_copy(g):
                for kt in range(2):
                    act.wait_ge(x_tr, 2 * g + kt + 1)
                    if g >= 2:
                        act.wait_ge(t_wr[g % 2], 16 * (g // 2))
                    act.activation(xt[:, g % 2, kt, :], m.ps[:, 6 + kt, :], ACT.Copy).then_inc(x_cp, 1)
            high(0)
            for g in range(NB):
                if g + 1 < NB:
                    high(g + 1)
                if g >= 1:
                    transposed_copy(g - 1)
                act.wait_ge(ba, 4 * g + 4)
                act.activation(sd[:, 4 * g:4 * g + 4], mv[:, 4 * g:4 * g + 4, 1], ACT.Sqrt,
                               bias=m.eps[:, 0:1]).then_inc(sq, 1)
            transposed_copy(NB - 1)

        @blk.vector
        def _(v):
            def low(g):
                for kt in range(2):
                    v.wait_ge(oh_r, 2 * g + kt + 1)
                    v.tensor_tensor(ol[:, g % 2, kt, :], m.ps[:, kt, :], oh[:, g % 2, kt, :].bitcast(F32),
                                    ALU.subtract).then_inc(ol_r, 1)

            def normalise(g):
                v.wait_ge(sq, g + 1)
                v.reciprocal(rs[:, 4 * g:4 * g + 4], sd[:, 4 * g:4 * g + 4]).then_inc(rr, 1)
                v.wait_ge(rr, g + 1)
                for t in range(4 * g, 4 * g + 4):
                    v.tensor_scalar(m.x1[:, t, :], m.x1[:, t, :], mv[:, t, 0:1], rs[:, t:t + 1], ALU.subtract,
                                    ALU.mult).then_inc(x2r, 1)

            def maximum(n):
                low_maximum(v, low_max[:, n:n + 1], low_parts[n]).then_inc(lm, 1)

            v.wait_ge(ld, 16)
            v.tensor_copy(wh[:, :, :], w[:, :, :]).then_inc(wsp, 1)
            v.wait_ge(wsp, 1)
            v.tensor_tensor(wl[:, :, :], w[:, :, :], wh[:, :, :].bitcast(F32), ALU.subtract).then_inc(wsp, 1)
            v.memset(m.ones[:, :], 1.0).then_inc(wsp, 1)
            for n in range(4):
                maximum(n)
            low(0)
            for g in range(NB):
                if g + 1 < NB:
                    low(g + 1)
                if g >= 1:
                    normalise(g - 1)
                v.wait_ge(xb, g + 1)
                for j in range(2):
                    z = m.x1[:, 4 * g + 2 * j:4 * g + 2 * j + 2, :]
                    v.wait_ge(pj, 2 * g + j + 1)
                    v.tensor_tensor(z, m.ps[:, 2 + 2 * (g % 2) + j, :].rearrange("p (t d) -> p t d", t=2), z,
                                    ALU.add).then_inc(z_r, 1)
                for t in range(4 * g, 4 * g + 4):
                    v.wait_ge(z_r, t // 2 + 1)
                    v.bn_stats(stats[:, t, :], m.x1[:, t, :]).then_inc(bs, 1)
                for t in range(4 * g, 4 * g + 4):
                    v.wait_ge(bs, t + 1)
                    v.bn_aggr(mv[:, t, :], stats[:, t, :]).then_inc(ba, 1)
                if g >= 1:
                    v.wait_ge(h_lo, g)
                    maximum(3 + g)
            normalise(NB - 1)
            v.wait_ge(h_lo, 8)
            maximum(11)
            v.wait_ge(lm, 12)
            v.tensor_reduce(m.low_any[:, 0:1], low_max[:, :], AX_X, ALU.max).then_inc(lm, 1)
            v.wait_ge(lm, 13)
            v.tensor_scalar(m.low_any[:, 0:1], m.low_any[:, 0:1], 0.0, None, ALU.is_gt).then_inc(lm, 1)

        @blk.tensor
        def _(pe):
            def in_transposes(g):
                pe.wait_ge(o_ld[g // 2], 128)
                for kt in range(2):
                    if g >= 1:
                        pe.wait_ge(ol_r, 2 * g - 1 + kt)
                    for q in range(4):
                        mm = nc.tensor.transpose(
                            m.ps[:, kt, P * q:P * q + P],
                            o[:, g, q, 2 * kt:2 * kt + 2, :].rearrange("p g d -> p (g d)"), m.ident[:, :])
                    mm.then_inc(tr, 1)

            def out_transposes(g):
                for kt in range(2):
                    if g >= 1:
                        pe.wait_ge(x_cp, 2 * g - 1 + kt)
                    pe.wait_ge(x2r, 4 * g + 4)
                    for q in range(4):
                        mm = nc.tensor.transpose(m.ps[:, 6 + kt, P * q:P * q + P],
                                                 m.x1[:, 4 * g + q, P * kt:P * kt + P], m.ident[:, :])
                    mm.then_inc(x_tr, 1)

            in_transposes(0)
            in_transposes(1)
            pe.wait_ge(wsp, 2)
            for g in range(NB):
                pe.wait_ge(ol_r, 2 * g + 2)
                for j in range(2):
                    if g >= 2:
                        pe.wait_ge(z_r, 2 * g - 3 + j)
                    for q in range(2 * j, 2 * j + 2):
                        for i, (kt, x, y) in enumerate((kt, x, y) for kt in range(2)
                                                       for x, y in ((ol, wh), (oh, wl), (oh, wh))):
                            mm = nc.tensor.matmul(m.ps[:, 2 + 2 * (g % 2) + j, D * (q % 2):D * (q % 2) + D],
                                                  x[:, g % 2, kt, P * q:P * q + P], y[:, kt, :],
                                                  start=(i == 0), stop=(i == 5))
                    mm.then_inc(pj, 1)
                if g >= 1:
                    out_transposes(g - 1)
                if g + 2 < NB:
                    in_transposes(g + 2)
            out_transposes(NB - 1)


def phase_ffn_first(nc, m, a):
    NB = 8
    with ExitStack() as st:
        sb, sem = tensors(nc, st)
        w1, w2, h1 = m.w1, m.w2, m.h1
        hh, hl, hr = m.rows
        s1 = sb("w1_scale", [P, 8])
        s2 = sb("w2_scale", [P, 8])
        s3 = sb("h1_scale", [P, 8])
        xh, xl, xr = own_split(nc, sb, "x2_block", [2, 512])
        y = sb("gelu_out", [P, 2, 512])
        low_max = sb("low_max_second", [P, 24])
        sc = sem("scales_loaded")
        x_ld = sem("x2_block_loaded")
        x_hi = sem("x2_high_ready")
        x_lo = sem("x2_low_ready")
        u_mm = sem("up_pair_done")
        g_r = sem("silu_ready")
        h_r = sem("gated_ready")
        hh_r = sem("gated_high_ready")
        hl_r = sem("gated_low_ready")
        y_mm = sem("hidden_tile_done")
        y_r = sem("gelu_ready")
        y_wr = [sem(f"gelu_written_{i}") for i in range(2)]
        h2_ld = [sem(f"h2_loaded_{j}") for j in range(3)]
        r_ld = [sem(f"rows_loaded_{j}") for j in range(2)]
        n_hi = sem("second_half_high_ready")
        n_lo = sem("second_half_low_ready")
        lm = sem("low_max_ready_e")
        ask_v, ask_pe = low_question(nc, m, sb, sem, m.low_any[:, 0:1], "a")
        hd = m.h_dram.rearrange("(k p) (b t) -> b k p t", p=P, t=512)
        hd8 = m.h_dram.rearrange("(k p) (b t) -> b p k t", p=P, t=512)
        nxt = [(h2_ld[0], 48, m.h2[0][k], m.h2[1][k], m.h2[2][k]) for k in range(2)]
        nxt += [(h2_ld[0], 48, m.w3[0][:, :, :], m.w3[1][:, :, :], m.w3[2][:, :, :])]
        nxt += [(h2_ld[1], 64, m.h2[0][k], m.h2[1][k], m.h2[2][k]) for k in range(2, 6)]
        nxt += [(r_ld[k // 4], 16, hh[:, 0, k, :], hl[:, 0, k, :], hr[:, 0, k, :]) for k in range(8)]
        nxt += [(h2_ld[2], 32, m.h2[0][k], m.h2[1][k], m.h2[2][k]) for k in range(6, 8)]
        MAXIMA = (list(range(7)), [15, 16])
        blk = st.enter_context(nc.Block())

        def block_loop(eng, up, down, split_x=None, after_first=None):
            if split_x:
                split_x(0)
            up(0, 0)
            if split_x:
                split_x(1)
            if after_first:
                after_first(eng)
            with eng.Fori(0, NB // 2 - 1) as i:
                for p in range(2):
                    up(i * 2 + (p + 1), (p + 1) % 2)
                    down(i * 2 + p, p, i * 2 + (p + 2))
            up(NB - 1, 1)
            down(NB - 2, 0, None)
            down(NB - 1, 1, None)

        @blk.sync
        def _(sp):
            x2t = m.x2t_dram.rearrange("(k p) (b t) -> b p k t", p=P, t=512)
            sp.dma_start(xr[:, :, :], x2t[0, :, :, :]).then_inc(x_ld, 16)
            for t, n in ((s1, "w1_s"), (s2, "w2_s"), (s3, "h1_s")):
                sp.dma_start(t[:, :], a[n]).then_inc(sc, 16)
            h2t = a["h2_T"].rearrange("(k p) n -> p k n", p=P)

            def h2_rows(k, part):
                sp.dma_start(m.h2[2][k], h2t[:, k, :].rearrange("p (a b) -> p a b", a=2)).then_inc(h2_ld[part], 16)
            h2_rows(0, 0)
            h2_rows(1, 0)
            sp.dma_start(m.w3[2][:, :, :], a["w3_T"].rearrange("(k p) n -> p k n", p=P)).then_inc(h2_ld[0], 16)
            with sp.Fori(1, NB) as t:
                sp.wait_ge(u_mm, t * 8)
                sp.dma_start(xr[:, :, :], x2t[t, :, :, :]).then_inc(x_ld, 16)
            sp.wait_ge(u_mm, NB * 8)
            for k in range(2, 6):
                h2_rows(k, 1)
            sp.wait_ge(y_mm, (NB - 1) * 8)
            for s in range(2):
                sp.wait_ge(y_wr[s], 16 + 64)
            for j in range(2):
                sp.dma_start(hr[:, 0, 4 * j:4 * j + 4, :], hd8[0, :, 4 * j:4 * j + 4, :]).then_inc(r_ld[j], 16)
            sp.wait_ge(y_mm, NB * 8 - 4)
            for k in range(6, 8):
                h2_rows(k, 2)

        @blk.gpsimd
        def _(gp):
            def up(t, p):
                for mt in range(8):
                    gp.wait_ge(hh_r, t * 8 + (mt + 1))
                    split_low(gp, hh[:, p, mt, :], hl[:, p, mt, :], hr[:, p, mt, :]).then_inc(hl_r, 1)
            block_loop(gp, up, lambda t, p, later: None)
            for n, (loaded, count, high, low, raw) in enumerate(nxt):
                gp.wait_ge(n_hi, n + 1)
                split_low(gp, high, low, raw).then_inc(n_lo, 1)

        @blk.scalar
        def _(act):
            act.sem_inc(y_r, 2)
            for s in range(2):
                act.sem_inc(y_wr[s], 16)

            def split_x(t):
                act.wait_ge(x_ld, t * 16 + 16)
                act.activation(xh[:, :, :], xr[:, :, :], ACT.Copy).then_inc(x_hi, 1)

            def up(t, p):
                if isinstance(t, int) and t == 0:
                    act.wait_ge(sc, 48)

                def high(mt):
                    act.wait_ge(h_r, t * 8 + (mt + 4))
                    act.activation(hh[:, p, mt, :], hr[:, p, mt, :], ACT.Copy).then_inc(hh_r, 1)
                for mt in range(8):
                    act.wait_ge(u_mm, t * 8 + (mt + 1))
                    act.activation(hr[:, p, mt, :], m.ps[:, 2 * (mt % 3), :], ACT.Silu,
                                   scale=s1[:, mt:mt + 1]).then_inc(g_r, 1)
                    if mt:
                        high(mt - 1)
                high(7)

            def down(t, p, later):
                for mt in range(8):
                    s = mt % 2
                    if mt == 4 and later is not None:
                        split_x(later)
                    act.wait_ge(y_mm, t * 8 + (mt + 1))
                    act.wait_ge(y_wr[s], t * 64 + 16 * (mt // 2 + 1))
                    act.activation(y[:, s, :], m.ps[:, 6 + mt % 2, :], ACT.Gelu, scale=s3[:, mt:mt + 1]).then_inc(y_r, 1)
                    act.wait_ge(y_r, t * 8 + (mt + 3))
                    act.dma_start(hd[t, mt, :, :], y[:, s, :]).then_inc(y_wr[s], 16)
            block_loop(act, up, down, split_x)
            for s in range(2):
                act.wait_ge(y_wr[s], NB * 64 + 16)

        @blk.vector
        def _(v):
            v.sem_inc(h_r, 3)

            def split_x(t):
                v.wait_ge(x_hi, t + 1)
                split_low(v, xh[:, :, :], xl[:, :, :], xr[:, :, :]).then_inc(x_lo, 1)

            def down(t, p, later):
                if later is not None:
                    split_x(later)

            def up(t, p):
                if isinstance(t, int) and t == 0:
                    v.wait_ge(sc, 48)
                for mt in range(8):
                    v.wait_ge(g_r, t * 8 + (mt + 1))
                    g = hr[:, p, mt, :]
                    v.scalar_tensor_tensor(g, m.ps[:, 2 * (mt % 3) + 1, :], s2[:, mt:mt + 1],
                                           g, ALU.mult, ALU.mult).then_inc(h_r, 1)
            block_loop(v, up, down, split_x, ask_v)
            column = 0
            for n, (loaded, count, high, low, raw) in enumerate(nxt):
                v.wait_ge(loaded, count)
                split_high(v, high, raw).then_inc(n_hi, 1)
                for j in MAXIMA[0] if n == 6 else MAXIMA[1] if n + 1 == len(nxt) else []:
                    part = nxt[j][3]
                    v.wait_ge(n_lo, j + 1)
                    low_maximum(v, low_max[:, column:column + part.shape[1]], part).then_inc(lm, 1)
                    column += part.shape[1]
            v.wait_ge(lm, 9)
            v.tensor_reduce(m.low_any[:, 1:2], low_max[:, 0:column], AX_X, ALU.max).then_inc(lm, 1)
            v.wait_ge(lm, 10)
            v.tensor_scalar(m.low_any[:, 1:2], m.low_any[:, 1:2], 0.0, None, ALU.is_gt).then_inc(lm, 1)

        @blk.tensor
        def _(pe):
            def up(t, p, with_low):
                pe.wait_ge(x_lo, t + 1)
                for mt in range(8):
                    pe.wait_ge(h_r, t * 8 + max(mt + 1, 3))
                    todo = passes(range(2), xh, xl, with_low)
                    for j, w in enumerate((w1, w2)):
                        for i, (kt, wi, xx) in enumerate(todo):
                            mm = nc.tensor.matmul(m.ps[:, 2 * (mt % 3) + j, :], w[wi][:, kt, P * mt:P * mt + P],
                                                  xx[:, kt, :], start=(i == 0), stop=(i == len(todo) - 1))
                    mm.then_inc(u_mm, 1)

            def down(t, p, with_low):
                pe.wait_ge(hl_r, t * 8 + 8)
                todo = passes(range(8), hh, hl, with_low)
                for mt in range(8):
                    pe.wait_ge(y_r, t * 8 + (mt + 1))
                    for i, (kt, wi, xx) in enumerate(todo):
                        mm = nc.tensor.matmul(m.ps[:, 6 + mt % 2, :], h1[wi][:, kt, P * mt:P * mt + P],
                                              xx[:, p, kt, :], start=(i == 0), stop=(i == len(todo) - 1))
                    mm.then_inc(y_mm, 1)

            def later(with_low):
                with pe.Fori(0, NB // 2 - 1) as i:
                    for p in range(2):
                        up(i * 2 + (p + 1), (p + 1) % 2, with_low)
                        down(i * 2 + p, p, with_low)
                up(NB - 1, 1, with_low)
                down(NB - 2, 0, with_low)
                down(NB - 1, 1, with_low)

            up(0, 0, True)
            needed = ask_pe(pe)
            with pe.If(needed > 0):
                later(True)
            with pe.Else():
                later(False)


def phase_ffn_second(nc, m, a, out):
    NB = 8
    with ExitStack() as st:
        sb, sem = tensors(nc, st)
        h2, w3 = m.h2, m.w3
        hh, hl, hr = m.rows
        s4 = sb("h2_scale", [P, 8])
        s5 = sb("w3_scale", [P, D])
        gh, gl, gr = arena_split(nc, m, "gelu2", 12 * F, 20 * F, [8, 512])
        z = sb("sum", [P, 4, D])
        x2 = sb("x2_tiles", [P, 4, D])
        stats = sb("ln_stats_e", [P, 4, 6])
        mv = sb("ln_mean_var_e", [P, 4, 2])
        sd = sb("ln_sd_e", [P, 4])
        rs = sb("ln_rs_e", [P, 4])
        sc = sem("scales_loaded_e")
        r_ld = [sem(f"hidden_rows_loaded_{j}") for j in range(4)]
        hh_r = sem("hidden_high_ready")
        hl_r = sem("hidden_low_ready")
        y_mm = sem("hidden2_tile_done")
        g_r = sem("gelu2_ready")
        gh_r = sem("gelu2_high_ready")
        gl_r = sem("gelu2_low_ready")
        o_mm = sem("w3_block_done")
        x_ld = sem("x2_tiles_loaded")
        z_m = sem("scaled_ready")
        z_a = sem("sum_ready")
        bs = sem("ln_stats_ready_e")
        ba = sem("ln_variance_ready_e")
        sq = sem("ln_sd_ready_e")
        rr = sem("ln_rs_ready_e")
        o_r = sem("out_tiles_ready")
        turn = sem("waits_carried_e")
        o_wr = sem("out_written")
        ask_v, ask_pe = low_question(nc, m, sb, sem, m.low_any[:, 1:2], "b")
        hd = m.h_dram.rearrange("(k p) (b t) -> b p k t", p=P, t=512)
        x2d = m.x2_dram.rearrange("(b t p) d -> b p t d", p=P, t=4)
        od = out.rearrange("(b t p) d -> b p t d", p=P, t=4)
        blk = st.enter_context(nc.Block())

        def block_loop(eng, body):
            body(0, None, 0, False, True)
            with eng.Fori(0, NB // 2 - 1) as i:
                for p in range(2):
                    body(i * 2 + (p + 1), i * 2 + p, (p + 1) % 2, True, True)
            body(NB - 1, NB - 2, 1, True, False)

        @blk.sync
        def _(sp):
            sp.sem_inc(o_wr, 16)
            sp.dma_start(s4[:, :], a["h2_s"]).then_inc(sc, 16)
            sp.dma_start(s5[:, :], a["w3_s"].partition_broadcast(P)).then_inc(sc, 16)

            def residual(t):
                sp.wait_ge(z_a, t + 1)
                sp.dma_start(x2[:, :, :], x2d[t, :, :, :]).then_inc(x_ld, 16)

            def store(t):
                sp.wait_ge(o_r, t * 4 + 4)
                sp.dma_start(od[t, :, :, :], z[:, :, :]).then_inc(o_wr, 16)

            def body(t, before, p, has_before, more):
                if more:
                    sp.wait_ge(y_mm, t * 8 + 1)
                    for j in range(4):
                        sp.dma_start(hr[:, 1 - p, 2 * j:2 * j + 2, :], hd[t + 1, :, 2 * j:2 * j + 2, :]).then_inc(r_ld[j], 16)
                residual(t)
                if has_before:
                    store(before)
            block_loop(sp, body)
            store(NB - 1)
            sp.wait_ge(o_wr, 16 * NB + 16)

        @blk.gpsimd
        def _(gp):
            gp.sem_inc(z_a, 1)

            def add(t):
                gp.wait_ge(x_ld, t * 16 + 16)
                gp.wait_ge(z_m, t * 4 + 8)
                gp.tensor_tensor(z[:, :, :], z[:, :, :], x2[:, :, :], ALU.add).then_inc(z_a, 1)

            def body(t, before, p, has_before, more):
                for mt in range(8):
                    gp.wait_ge(gh_r, t * 8 + (mt + 1))
                    split_low(gp, gh[:, mt, :], gl[:, mt, :], gr[:, mt, :]).then_inc(gl_r, 1)
                    if mt == 2 and has_before:
                        add(before)
            block_loop(gp, body)
            add(NB - 1)

        @blk.scalar
        def _(act):
            act.sem_inc(g_r, 4)
            act.wait_ge(sc, 32)

            def deviation(t):
                act.wait_ge(ba, t * 4 + 4)
                act.activation(sd[:, :], mv[:, :, 1], ACT.Sqrt, bias=m.eps[:, 0:1]).then_inc(sq, 1)

            def body(t, before, p, has_before, more):
                for mt in range(8):
                    act.wait_ge(y_mm, t * 8 + (mt + 1))
                    act.activation(gr[:, mt, :], m.ps[:, mt % 4, :], ACT.Gelu,
                                   scale=s4[:, mt:mt + 1]).then_inc(g_r, 1)
                    if mt == 5 and has_before:
                        deviation(before)
                    if more:
                        act.wait_ge(r_ld[mt // 2], t * 16 + 16)
                        act.activation(hh[:, 1 - p, mt, :], hr[:, 1 - p, mt, :], ACT.Copy).then_inc(hh_r, 1)
            block_loop(act, body)
            deviation(NB - 1)

        @blk.vector
        def _(v):
            v.sem_inc(hl_r, 8)
            v.sem_inc(z_m, 4)
            ask_v(v)
            v.wait_ge(sc, 32)

            def scaled(t):
                v.wait_ge(o_mm, t + 1)
                v.wait_ge(o_wr, t * 16 + 16)
                for q in range(4):
                    v.tensor_tensor(z[:, q, :], m.ps[:, 4 + q, 0:D], s5[:, :], ALU.mult).then_inc(z_m, 1)

            def statistics(t):
                v.wait_ge(z_a, t + 2)
                for q in range(4):
                    v.bn_stats(stats[:, q, :], z[:, q, :]).then_inc(bs, 1)
                v.wait_ge(bs, t * 4 + 4)
                v.sem_inc(turn, 1)
                for q in range(4):
                    v.bn_aggr(mv[:, q, :], stats[:, q, :]).then_inc(ba, 1)

            def normalise(t):
                v.wait_ge(sq, t + 1)
                v.reciprocal(rs[:, :], sd[:, :]).then_inc(rr, 1)
                v.wait_ge(rr, t + 1)
                for q in range(4):
                    v.tensor_scalar(z[:, q, :], z[:, q, :], mv[:, q, 0:1], rs[:, q:q + 1], ALU.subtract,
                                    ALU.mult).then_inc(o_r, 1)

            def body(t, before, p, has_before, more):
                for mt in range(8):
                    v.wait_ge(g_r, t * 8 + (mt + 5))
                    split_high(v, gh[:, mt, :], gr[:, mt, :]).then_inc(gh_r, 1)
                    if more:
                        v.wait_ge(hh_r, t * 8 + (mt + 1))
                        split_low(v, hh[:, 1 - p, mt, :], hl[:, 1 - p, mt, :], hr[:, 1 - p, mt, :]).then_inc(hl_r, 1)
                    if has_before:
                        if mt == 1:
                            scaled(before)
                        if mt == 4:
                            statistics(before)
                        if mt == 6:
                            normalise(before)
            block_loop(v, body)
            for stage in (scaled, statistics, normalise):
                stage(NB - 1)

        @blk.tensor
        def _(pe):
            def blocks(with_low):
                def last_layer(t, kt):
                    pe.wait_ge(gl_r, t * 8 + (kt + 1))
                    if kt == 0:
                        pe.wait_ge(z_m, t * 4 + 4)
                    todo = passes([kt], gh, gl, with_low)
                    for q in range(4):
                        for i, (_, wi, xx) in enumerate(todo):
                            mm = nc.tensor.matmul(m.ps[:, 4 + q, 0:D], xx[:, kt, P * q:P * q + P],
                                                  w3[wi][:, kt, :], start=(kt == 0 and i == 0),
                                                  stop=(kt == 7 and i == len(todo) - 1))
                    if kt == 7:
                        mm.then_inc(o_mm, 1)

                def body(t, before, p, has_before, more):
                    pe.wait_ge(hl_r, t * 8 + 8)
                    todo = passes(range(8), hh, hl, with_low)
                    for mt in range(8):
                        pe.wait_ge(g_r, t * 8 + (mt + 1))
                        for i, (kt, wi, xx) in enumerate(todo):
                            mm = nc.tensor.matmul(m.ps[:, mt % 4, :], h2[wi][kt][:, mt // 4, P * (mt % 4):P * (mt % 4) + P],
                                                  xx[:, p, kt, :], start=(i == 0), stop=(i == len(todo) - 1))
                        mm.then_inc(y_mm, 1)
                        if mt >= 2:
                            last_layer(t, mt - 2)
                        elif has_before:
                            last_layer(before, 6 + mt)
                block_loop(pe, body)
                last_layer(NB - 1, 6)
                last_layer(NB - 1, 7)

            needed = ask_pe(pe)
            with pe.If(needed > 0):
                blocks(True)
            with pe.Else():
                blocks(False)


def build(nc, a, out):
    m = Mem()
    with ExitStack() as st:
        def sb(name, shape, dtype=F32):
            return st.enter_context(nc.sbuf_tensor(name, shape, dtype))
        m.ps = st.enter_context(nc.psum_tensor("psum", [P, 8, 512], F32))
        m.ident = sb("ident", [P, P])
        m.ident_bf = sb("ident_bf", [P, P], BF16)
        m.mask_bf = sb("causal_mask", [P, P], BF16)
        m.eps = sb("eps", [P, 1])
        m.arena_base = aligned(nc.sbuf_base)
        sb("arena", [P, ARENA])
        m.ones = sb("ones", [P, 1])
        m.low_any = sb("low_any", [P, 2])
        m.kpad_dram = nc.dram_tensor("kpad_scratch", [D, 256], F32).ap()
        m.q_dram = nc.dram_tensor("q_scratch", [IT, HG * DH, 3, L], BF16).ap()
        m.k_dram = nc.dram_tensor("k_scratch", [IT, HG * DH, 3, KP], BF16).ap()
        m.v_dram = nc.dram_tensor("v_scratch", [IT, KT * P, HG * 32], F32).ap()
        m.o_dram = nc.dram_tensor("o_scratch", [IT, 2, P, 4, HG * DH], F32).ap()
        m.max_dram = nc.dram_tensor("max_scratch", [3 * HG * CH, P], BF16).ap()
        m.x2t_dram = nc.dram_tensor("x2t_scratch", [D, B * L], F32).ap()
        m.x2_dram = nc.dram_tensor("x2_scratch", [B * L, D], F32).ap()
        m.h_dram = nc.dram_tensor("h_scratch", [F, B * L], F32).ap()
        with ExitStack() as st1:
            m.bout = st1.enter_context(nc.sbuf_tensor("bout", [P, D], F32))
            m.x1 = st1.enter_context(nc.sbuf_tensor("x1", [P, NT, D], F32))
            m.x1h = arena(nc, m, "x1t_high", 0, [2, B * L], F32R)
            m.x1l = arena(nc, m, "x1t_low", 4 * B * L, [2, B * L], F32R)
            phase_convolution(nc, m, a)
            phase_projections(nc, m, a)
            m.w1 = arena_split(nc, m, "w1", 0, 2 * F, [2, F])
            m.w2 = arena_split(nc, m, "w2", 4 * F, 6 * F, [2, F])
            m.h1 = arena_split(nc, m, "h1", 8 * F, 16 * F, [8, F])
            phase_attention(nc, m, a)
            phase_output(nc, m, a)
        m.rows = own_split(nc, sb, "rows", [2, 8, 512])
        m.w3 = own_split(nc, sb, "w3", [8, D])
        h2a = own_split(nc, sb, "h2_first_rows", [2, 2, 512])
        h2b = arena_split(nc, m, "h2_more_rows", 0, 4 * F, [4, 2, 512])
        m.h2 = [[h2a[i][:, k] for k in range(2)] + [h2b[i][:, k] for k in range(4)] +
                [m.h1[i][:, 2 * k:2 * k + 2, 0:512] for k in range(2)] for i in range(3)]
        phase_ffn_first(nc, m, a)
        phase_ffn_second(nc, m, a, out)


def kernel(**inputs):
    import concourse.bacc as _bacc
    from concourse.bass_utils import run_bass_kernel_spmd as _run

    g = {k: np.asarray(v) for k, v in inputs.items()}
    x = g["x"].reshape(B * L, D)
    laid = {
        "x": x,
        "x_rev": x.reshape(NT, P, D)[:, ::-1].reshape(B * L, D),
        "ctx_T": g["ctx_1024"].reshape(B * M, D).T,
        "A_log": g["L0_attn_A_log"],
        "C_T": g["L0_attn_C"].T,
        "delta": g["L0_attn_delta"],
        "freq_align": g["L0_attn_freq_align"],
        "fa_cols": g["L0_attn_freq_align"].reshape(2, P).T,
        "d_cols": g["L0_attn_D"].reshape(2, P).T,
        "reward": g["L0_attn_reward"],
        "gamma": g["L0_attn_gamma"],
        "beta": g["L0_attn_beta"],
        "Wq": g["L0_xattn_Wq"],
        "Wkv": g["L0_xattn_Wkv"],
        "Wout": g["L0_xattn_Wout"],
        "bout": g["L0_xattn_bout"],
    }
    for n in ("w1", "w2", "h1", "h2", "w3"):
        laid[n + "_T"] = g[f"L0_ffn_{n}_w"].T
    for n in ("w1", "w2", "h1", "h2"):
        laid[n + "_s"] = g[f"L0_ffn_{n}_s"].reshape(8, P).T
    laid["w3_s"] = g["L0_ffn_w3_s"]

    nc = _bacc.Bacc("TRN2", target_bir_lowering=False, num_devices=1)
    arrays, aps = {}, {}
    for name, v in laid.items():
        v = np.ascontiguousarray(v)
        arrays[f"in_{name}"] = v
        aps[name] = nc.dram_tensor(f"in_{name}", v.shape, mybir.dt.from_np(v.dtype), kind="ExternalInput").ap()
    out = nc.dram_tensor("out", (B * L, D), F32, kind="ExternalOutput").ap()
    build(nc, aps, out)
    r = _run(nc, [arrays], core_ids=[0])
    return r.results[0]["out"].reshape(B, L, D)
```
